# Optimizing a Trainium2 kernel written in Bass

```python
import numpy as np
import jax
import jax.numpy as jnp

def _softmax(x, axis=-1):
    return jax.nn.softmax(x, axis=axis)

def _gelu(x):
    return jax.nn.gelu(x, approximate=True)

def _silu(x):
    return jax.nn.silu(x)

def _sigmoid(x):
    return jax.nn.sigmoid(x)

def _layernorm(x, axis=-1, eps=1e-05):
    m = jnp.mean(x, axis=axis, keepdims=True)
    v = jnp.var(x, axis=axis, keepdims=True)
    return (x - m) / jnp.sqrt(v + eps)

def _scatter_add(tgt, idx, src, axis=0):
    return tgt.at[idx].add(src)

def _segment_sum(src, seg, n):
    return jax.ops.segment_sum(src, seg, n)
kernel_name = 'mk_macaron_d1_jaxref_r8_187b8b'

def setup_inputs(seed: int=0):
    np.random.seed(seed)
    _w = jnp.asarray

    def _L0_attn_setup():
        import jax, jax.numpy as jnp
        import numpy as np
        EMBED_DIM = 128
        NUM_HEADS = 16
        HEAD_DIM = EMBED_DIM // NUM_HEADS
        ROPE_BASE = 10000.0

        def _rope(t):
            hd = t.shape[-1]
            half = hd // 2
            S = t.shape[2]
            inv_freq = 1.0 / ROPE_BASE ** (jnp.arange(half, dtype=jnp.float32) / half)
            ang = jnp.arange(S, dtype=jnp.float32)[:, None] * inv_freq[None, :]
            cos, sin = (jnp.cos(ang), jnp.sin(ang))
            t1, t2 = (t[..., :half], t[..., half:])
            return jnp.concatenate([t1 * cos - t2 * sin, t1 * sin + t2 * cos], axis=-1)

        def _attention_mc(x, Wq, Wk, Wv, Wo):
            B, S, D = x.shape
            H, hd = (NUM_HEADS, HEAD_DIM)
            q = (x @ Wq.T).reshape(B, S, H, hd).transpose(0, 2, 1, 3)
            k = (x @ Wk.T).reshape(B, S, H, hd).transpose(0, 2, 1, 3)
            v = (x @ Wv.T).reshape(B, S, H, hd).transpose(0, 2, 1, 3)
            q = _rope(q)
            k = _rope(k)
            scale = 1.0 / jnp.sqrt(jnp.float32(hd))
            scores = jnp.einsum('bhqd,bhkd->bhqk', q, k) * scale
            causal = jnp.tril(jnp.ones((S, S), dtype=bool))
            scores = jnp.where(causal, scores, jnp.finfo(scores.dtype).min)
            attn = jax.nn.softmax(scores, axis=-1)
            out = jnp.einsum('bhqk,bhkd->bhqd', attn, v)
            out = out.transpose(0, 2, 1, 3).reshape(B, S, D)
            return out @ Wo.T
        key = jax.random.key(seed)
        ks = jax.random.split(key, 5)
        B, S, D = (2, 256, EMBED_DIM)
        bound = 1.0 / np.sqrt(D)
        x = jax.random.normal(ks[0], (B, S, D), dtype=jnp.float32)
        Wq = jax.random.uniform(ks[1], (D, D), dtype=jnp.float32, minval=-bound, maxval=bound)
        Wk = jax.random.uniform(ks[2], (D, D), dtype=jnp.float32, minval=-bound, maxval=bound)
        Wv = jax.random.uniform(ks[3], (D, D), dtype=jnp.float32, minval=-bound, maxval=bound)
        Wo = jax.random.uniform(ks[4], (D, D), dtype=jnp.float32, minval=-bound, maxval=bound)
        return {'x': x, 'Wq': Wq, 'Wk': Wk, 'Wv': Wv, 'Wo': Wo}
    _L0_attn_in = _L0_attn_setup()

    def _L0_ffn_setup():
        import jax, jax.numpy as jnp
        import numpy as np
        DIM = 128
        DEPTH = 2
        HEADS = 8
        DIM_HEAD = 64
        WINDOW = 64
        INNER = HEADS * DIM_HEAD
        HID = int(DIM * 4 * 2 / 3)
        B, N = (2, 1024)
        QK_SCALE = 8.0

        def shift_token(t):
            t1, t2 = jnp.split(t, 2, axis=-1)
            t2 = jnp.pad(t2, ((0, 0), (1, 0), (0, 0)))[:, :-1]
            return jnp.concatenate([t1, t2], axis=-1)

        def l2norm(t):
            return t / jnp.clip(jnp.linalg.norm(t, axis=-1, keepdims=True), 1e-12)

        def rotate_half(x):
            x1, x2 = jnp.split(x, 2, axis=-1)
            return jnp.concatenate([-x2, x1], axis=-1)

        def rotary_xpos(q, k):
            n = q.shape[-2]
            half_idx = jnp.arange(0, DIM_HEAD, 2, dtype=jnp.float32)
            inv_freq = 1.0 / 10000.0 ** (half_idx / DIM_HEAD)
            t = jnp.arange(n, dtype=jnp.float32)
            freqs = t[:, None] * inv_freq[None, :]
            freqs = jnp.concatenate([freqs, freqs], axis=-1)
            base = (half_idx + 0.4 * DIM_HEAD) / (1.4 * DIM_HEAD)
            power = (t - n // 2) / float(WINDOW // 2)
            scale = base[None, :] ** power[:, None]
            scale = jnp.concatenate([scale, scale], axis=-1)
            cos, sin = (jnp.cos(freqs), jnp.sin(freqs))
            q = q * cos * scale + rotate_half(q) * sin * scale
            k = k * cos / scale + rotate_half(k) * sin / scale
            return (q, k)

        def local_attention(q, k, v):
            b, h, n, d = q.shape
            w = n // WINDOW
            bq = q.reshape(b, h, w, WINDOW, d) * QK_SCALE
            bk = k.reshape(b, h, w, WINDOW, d)
            bv = v.reshape(b, h, w, WINDOW, d)

            def look_around(t):
                p = jnp.pad(t, ((0, 0), (0, 0), (1, 0), (0, 0), (0, 0)))
                return jnp.concatenate([p[:, :, :w], p[:, :, 1:]], axis=3)
            bk, bv = (look_around(bk), look_around(bv))
            bt = jnp.arange(n).reshape(w, WINDOW)
            btp = jnp.pad(bt, ((1, 0), (0, 0)), constant_values=-1)
            btk = jnp.concatenate([btp[:w], btp[1:]], axis=1)
            sim = jnp.einsum('bhwid,bhwjd->bhwij', bq, bk)
            i = bt[:, :, None]
            j = btk[:, None, :]
            mask = (i < j) | (i > j + WINDOW) | (j == -1)
            sim = jnp.where(mask, -jnp.finfo(sim.dtype).max, sim)
            attn = jax.nn.softmax(sim, axis=-1)
            out = jnp.einsum('bhwij,bhwjd->bhwid', attn, bv)
            return out.reshape(b, h, n, d)

        def _layer(x, wqkv, qs, ksc, wo, lg, lb, w1, b1, w2, b2):
            b, n, _ = x.shape
            h = shift_token(x)
            qkv = h @ wqkv
            q, k, v = jnp.split(qkv, 3, axis=-1)
            to_heads = lambda t: t.reshape(b, n, HEADS, DIM_HEAD).transpose(0, 2, 1, 3)
            q, k, v = (to_heads(q), to_heads(k), to_heads(v))
            q = l2norm(q) * qs
            k = l2norm(k) * ksc
            q, k = rotary_xpos(q, k)
            o = local_attention(q, k, v)
            o = o.transpose(0, 2, 1, 3).reshape(b, n, INNER)
            x = x + o @ wo
            h = shift_token(x)
            mu = h.mean(-1, keepdims=True)
            var = h.var(-1, keepdims=True)
            h = (h - mu) / jnp.sqrt(var + 1e-05) * lg + lb
            h = h @ w1 + b1
            a, g = jnp.split(h, 2, axis=-1)
            h = a * jax.nn.gelu(g, approximate=False)
            x = x + h @ w2 + b2
            return x
        key = jax.random.key(seed)
        ks = jax.random.split(key, 6)
        return {'x': jax.random.normal(ks[0], (B, N, DIM), jnp.float32), 'wqkv': jax.random.normal(ks[1], (DEPTH, DIM, 3 * INNER), jnp.float32) * 0.02, 'q_scale': jnp.ones((DEPTH, DIM_HEAD), jnp.float32), 'k_scale': jnp.ones((DEPTH, DIM_HEAD), jnp.float32), 'wo': jax.random.normal(ks[2], (DEPTH, INNER, DIM), jnp.float32) * 0.02, 'ln_g': jnp.ones((DEPTH, DIM), jnp.float32), 'ln_b': jnp.zeros((DEPTH, DIM), jnp.float32), 'w1': jax.random.normal(ks[3], (DEPTH, DIM, 2 * HID), jnp.float32) * 0.02, 'b1': jnp.zeros((DEPTH, 2 * HID), jnp.float32), 'w2': jax.random.normal(ks[4], (DEPTH, HID, DIM), jnp.float32) * 0.02, 'b2': jnp.zeros((DEPTH, DIM), jnp.float32)}
    _L0_ffn_in = _L0_ffn_setup()
    _d = {'L0_attn_x': _L0_attn_in['x'], 'L0_attn_Wq': _L0_attn_in['Wq'], 'L0_attn_Wk': _L0_attn_in['Wk'], 'L0_attn_Wv': _L0_attn_in['Wv'], 'L0_attn_Wo': _L0_attn_in['Wo'], 'L0_ffn_wqkv': _L0_ffn_in['wqkv'], 'L0_ffn_q_scale': _L0_ffn_in['q_scale'], 'L0_ffn_k_scale': _L0_ffn_in['k_scale'], 'L0_ffn_wo': _L0_ffn_in['wo'], 'L0_ffn_ln_g': _L0_ffn_in['ln_g'], 'L0_ffn_ln_b': _L0_ffn_in['ln_b'], 'L0_ffn_w1': _L0_ffn_in['w1'], 'L0_ffn_b1': _L0_ffn_in['b1'], 'L0_ffn_w2': _L0_ffn_in['w2'], 'L0_ffn_b2': _L0_ffn_in['b2']}
    _x0 = _d['L0_attn_x']
    _d['L0_attn_x'] = jax.random.normal(jax.random.fold_in(jax.random.key(seed), 1), (4, 1024, 128), dtype=_x0.dtype)
    del _x0
    return _d

def reference(L0_attn_x, L0_attn_Wq, L0_attn_Wk, L0_attn_Wv, L0_attn_Wo, L0_ffn_wqkv, L0_ffn_q_scale, L0_ffn_k_scale, L0_ffn_wo, L0_ffn_ln_g, L0_ffn_ln_b, L0_ffn_w1, L0_ffn_b1, L0_ffn_w2, L0_ffn_b2):

    def _L0_attn_ref(x, Wq, Wk, Wv, Wo):
        import jax, jax.numpy as jnp
        import numpy as np
        EMBED_DIM = 128
        NUM_HEADS = 16
        HEAD_DIM = EMBED_DIM // NUM_HEADS
        ROPE_BASE = 10000.0

        def _rope(t):
            hd = t.shape[-1]
            half = hd // 2
            S = t.shape[2]
            inv_freq = 1.0 / ROPE_BASE ** (jnp.arange(half, dtype=jnp.float32) / half)
            ang = jnp.arange(S, dtype=jnp.float32)[:, None] * inv_freq[None, :]
            cos, sin = (jnp.cos(ang), jnp.sin(ang))
            t1, t2 = (t[..., :half], t[..., half:])
            return jnp.concatenate([t1 * cos - t2 * sin, t1 * sin + t2 * cos], axis=-1)

        def _attention_mc(x, Wq, Wk, Wv, Wo):
            B, S, D = x.shape
            H, hd = (NUM_HEADS, HEAD_DIM)
            q = (x @ Wq.T).reshape(B, S, H, hd).transpose(0, 2, 1, 3)
            k = (x @ Wk.T).reshape(B, S, H, hd).transpose(0, 2, 1, 3)
            v = (x @ Wv.T).reshape(B, S, H, hd).transpose(0, 2, 1, 3)
            q = _rope(q)
            k = _rope(k)
            scale = 1.0 / jnp.sqrt(jnp.float32(hd))
            scores = jnp.einsum('bhqd,bhkd->bhqk', q, k) * scale
            causal = jnp.tril(jnp.ones((S, S), dtype=bool))
            scores = jnp.where(causal, scores, jnp.finfo(scores.dtype).min)
            attn = jax.nn.softmax(scores, axis=-1)
            out = jnp.einsum('bhqk,bhkd->bhqd', attn, v)
            out = out.transpose(0, 2, 1, 3).reshape(B, S, D)
            return out @ Wo.T
        return _attention_mc(x, Wq, Wk, Wv, Wo)

    def _L0_ffn_ref(x, wqkv, q_scale, k_scale, wo, ln_g, ln_b, w1, b1, w2, b2):
        import jax, jax.numpy as jnp
        import numpy as np
        DIM = 128
        DEPTH = 2
        HEADS = 8
        DIM_HEAD = 64
        WINDOW = 64
        INNER = HEADS * DIM_HEAD
        HID = int(DIM * 4 * 2 / 3)
        B, N = (2, 1024)
        QK_SCALE = 8.0

        def shift_token(t):
            t1, t2 = jnp.split(t, 2, axis=-1)
            t2 = jnp.pad(t2, ((0, 0), (1, 0), (0, 0)))[:, :-1]
            return jnp.concatenate([t1, t2], axis=-1)

        def l2norm(t):
            return t / jnp.clip(jnp.linalg.norm(t, axis=-1, keepdims=True), 1e-12)

        def rotate_half(x):
            x1, x2 = jnp.split(x, 2, axis=-1)
            return jnp.concatenate([-x2, x1], axis=-1)

        def rotary_xpos(q, k):
            n = q.shape[-2]
            half_idx = jnp.arange(0, DIM_HEAD, 2, dtype=jnp.float32)
            inv_freq = 1.0 / 10000.0 ** (half_idx / DIM_HEAD)
            t = jnp.arange(n, dtype=jnp.float32)
            freqs = t[:, None] * inv_freq[None, :]
            freqs = jnp.concatenate([freqs, freqs], axis=-1)
            base = (half_idx + 0.4 * DIM_HEAD) / (1.4 * DIM_HEAD)
            power = (t - n // 2) / float(WINDOW // 2)
            scale = base[None, :] ** power[:, None]
            scale = jnp.concatenate([scale, scale], axis=-1)
            cos, sin = (jnp.cos(freqs), jnp.sin(freqs))
            q = q * cos * scale + rotate_half(q) * sin * scale
            k = k * cos / scale + rotate_half(k) * sin / scale
            return (q, k)

        def local_attention(q, k, v):
            b, h, n, d = q.shape
            w = n // WINDOW
            bq = q.reshape(b, h, w, WINDOW, d) * QK_SCALE
            bk = k.reshape(b, h, w, WINDOW, d)
            bv = v.reshape(b, h, w, WINDOW, d)

            def look_around(t):
                p = jnp.pad(t, ((0, 0), (0, 0), (1, 0), (0, 0), (0, 0)))
                return jnp.concatenate([p[:, :, :w], p[:, :, 1:]], axis=3)
            bk, bv = (look_around(bk), look_around(bv))
            bt = jnp.arange(n).reshape(w, WINDOW)
            btp = jnp.pad(bt, ((1, 0), (0, 0)), constant_values=-1)
            btk = jnp.concatenate([btp[:w], btp[1:]], axis=1)
            sim = jnp.einsum('bhwid,bhwjd->bhwij', bq, bk)
            i = bt[:, :, None]
            j = btk[:, None, :]
            mask = (i < j) | (i > j + WINDOW) | (j == -1)
            sim = jnp.where(mask, -jnp.finfo(sim.dtype).max, sim)
            attn = jax.nn.softmax(sim, axis=-1)
            out = jnp.einsum('bhwij,bhwjd->bhwid', attn, bv)
            return out.reshape(b, h, n, d)

        def _layer(x, wqkv, qs, ksc, wo, lg, lb, w1, b1, w2, b2):
            b, n, _ = x.shape
            h = shift_token(x)
            qkv = h @ wqkv
            q, k, v = jnp.split(qkv, 3, axis=-1)
            to_heads = lambda t: t.reshape(b, n, HEADS, DIM_HEAD).transpose(0, 2, 1, 3)
            q, k, v = (to_heads(q), to_heads(k), to_heads(v))
            q = l2norm(q) * qs
            k = l2norm(k) * ksc
            q, k = rotary_xpos(q, k)
            o = local_attention(q, k, v)
            o = o.transpose(0, 2, 1, 3).reshape(b, n, INNER)
            x = x + o @ wo
            h = shift_token(x)
            mu = h.mean(-1, keepdims=True)
            var = h.var(-1, keepdims=True)
            h = (h - mu) / jnp.sqrt(var + 1e-05) * lg + lb
            h = h @ w1 + b1
            a, g = jnp.split(h, 2, axis=-1)
            h = a * jax.nn.gelu(g, approximate=False)
            x = x + h @ w2 + b2
            return x
        for l in range(DEPTH):
            x = _layer(x, wqkv[l], q_scale[l], k_scale[l], wo[l], ln_g[l], ln_b[l], w1[l], b1[l], w2[l], b2[l])
        return x
    x = L0_attn_x
    x = x + 0.5 * _L0_ffn_ref(_layernorm(x, axis=-1), L0_ffn_wqkv, L0_ffn_q_scale, L0_ffn_k_scale, L0_ffn_wo, L0_ffn_ln_g, L0_ffn_ln_b, L0_ffn_w1, L0_ffn_b1, L0_ffn_w2, L0_ffn_b2)
    x = x + _L0_attn_ref(_layernorm(x, axis=-1), L0_attn_Wq, L0_attn_Wk, L0_attn_Wv, L0_attn_Wo)
    x = x + 0.5 * _L0_ffn_ref(_layernorm(x, axis=-1), L0_ffn_wqkv, L0_ffn_q_scale, L0_ffn_k_scale, L0_ffn_wo, L0_ffn_ln_g, L0_ffn_ln_b, L0_ffn_w1, L0_ffn_b1, L0_ffn_w2, L0_ffn_b2)
    return x

_drawn_inputs = setup_inputs


def setup_inputs(seed=0):
    import zlib

    import numpy as np

    out = dict(_drawn_inputs(seed))
    spreads = {'L0_ffn_q_scale': (1.0, 0.6),
     'L0_ffn_k_scale': (1.0, 0.6),
     'L0_ffn_ln_g': (1.0, 0.6),
     'L0_ffn_ln_b': (0.0, 0.8),
     'L0_ffn_b1': (0.0, 0.8),
     'L0_ffn_b2': (0.0, 0.1)}
    factors = {'L0_attn_Wq': 7.828,
     'L0_attn_Wk': 7.693,
     'L0_ffn_wqkv': 3.335,
     'L0_ffn_wo': 3.316,
     'L0_ffn_w1': 5.292,
     'L0_ffn_w2': 5.212}
    for name, (base, spread) in spreads.items():
        noise = np.random.default_rng([zlib.crc32(name.encode()), seed]).standard_normal(out[name].shape)
        drawn = base * np.exp(spread * noise) if base else spread * noise
        out[name] = jnp.asarray(drawn.astype(out[name].dtype))
    for name, factor in factors.items():
        out[name] = (out[name] * factor).astype(out[name].dtype)
    return out
```

```python
from contextlib import ExitStack

import numpy as np

import concourse.bass as bass
from concourse import mybir

F32 = mybir.dt.float32
BF16 = mybir.dt.bfloat16
ALU = mybir.AluOpType
ACT = mybir.ActivationFunctionType
AX = mybir.AxisListType.X

P = 128
B, S = 4, 1024
NT = S // P
TOK = B * S
FH, FD = 8, 64
INNER = FH * FD
PAIRS = FH // 2
WIN = 64
UNITS = 2 * PAIRS
DEPTH = 2
HID = 341
CH = 3
CHN = [min(P, HID - P * j) for j in range(CH)]
GH, GD = 16, 8
STACK = 96
LN_EPS = 1e-5
NORM_LIFT = 20
BLOCKS = 8
CW = TOK // BLOCKS
HEADS = B * GH
TURN = 4
CHUNKS = [(i, c) for i in range(NT) for c in range(1 + i // 4)]
VW = GD + 1


class Count:

    def __init__(self, sem, per, by=1, first=1):
        self.sem, self.per, self.by, self.first = sem, per, by, first

    def at(self, layer, n, c):
        return (layer * NT + n) * (self.per * self.by) + (self.first + c * self.by)


def need(eng, count, layer, n, c):
    v = count.at(layer, n, c)
    if not isinstance(v, int) or v > count.first:
        eng.wait_ge(count.sem, v)


def program(nc, x, wqkv, qkscale, wo, w1, w2, cols, rope_cos, rope_sin, bandmask, identb_d, identf_d,
            gw, g_cos, g_sin, causal, stack_tail, out):
    ctx = ExitStack()
    with ctx:
        def sb(name, shape, dt=F32):
            return ctx.enter_context(nc.sbuf_tensor(name, shape, dt))

        def sem(name):
            return ctx.enter_context(nc.semaphore(name))

        xT = sb("xT", [P, B, S])
        y_in = sb("y_in", [P, B, S + 1])
        y_att = sb("y_att", [P, B, S + 1])
        y_mid = sb("y_mid", [P, B, S + 1])
        identf = sb("identf", [P, P])
        identb = sb("identb", [P, P], BF16)
        ones = sb("ones", [P, P])
        mask = sb("mask", [P, 2 * NT, P], BF16)
        ropec = sb("ropec", [P, NT, 2, FD])
        ropes = sb("ropes", [P, NT, 2, FD])
        consts = sb("consts", [P, 2])
        wqkv_s = sb("wqkv_s", [P, 3 * INNER])
        wo_s = sb("wo_s", [P, PAIRS, P])
        w1_s = sb("w1_s", [P, 2 * HID])
        w2_s = sb("w2_s", [P, CH, P])
        cols_s = sb("cols_s", [P, 9])
        rope_n = sb("rope_n", [P, 2, 2, FD])
        scl = sb("scl", [P, 2, 2, FD])
        hs = sb("hs", [P, B, P])
        sqk = sb("sqk", [P, 2 * INNER])
        ss = sb("ss", [P, 2, 4, 2 * FH])
        nw = sb("nw", [P, 2, 2, 2 * FH])
        qkn = sb("qkn", [P, 2, 2 * INNER])
        t1 = sb("t1", [P, 2, 2 * INNER])
        t2 = sb("t2", [P, 2, 2 * INNER])
        qbd = sb("qbd", [P, 2, PAIRS, 2, P])
        kT = sb("kT", [P, B, PAIRS, WIN + P])
        vown = sb("vown", [P, B, INNER])
        vprev = sb("vprev", [P, B, INNER])
        nmax = sb("nmax", [P, 2, UNITS])
        psum_e = sb("psum_e", [P, 2, 2, UNITS])
        pr = sb("pr", [P, 2, UNITS, P])
        prT = sb("prT", [P, 2, UNITS, P])
        oT = sb("oT", [P, PAIRS, B, P])
        h1 = sb("h1", [P, CW])
        hc = sb("hc", [P, CW])
        hq = sb("hq", [P, CW])
        rstd = sb("rstd", [P, CW])
        hn = sb("hn", [P, CW])
        gel = sb("gel", [P, CH, CW])
        act_t = sb("act_t", [P, CH, CW])
        ps = [ctx.enter_context(nc.psum_tensor(f"ps{i}", [P, 2, 512], F32)) for i in range(2)]
        psr = ctx.enter_context(nc.psum_tensor("psr", [P, 4, 512], F32))
        psm = psr[:, 3, :]
        ps_qk, ps_s = ps

        gw_s = wqkv_s[:, 0:6 * P].rearrange("p (w n) -> p w n", w=6)
        gcos = gel[:].rearrange("p a b -> p (a b)")[:, 0:S]
        gsin = act_t[:].rearrange("p a b -> p (a b)")[:, 0:S]
        zs = [hs[:].rearrange("p b t -> p (b t)"), h1[:]]
        parts = [t[:].rearrange("p a u k -> p (a u k)").bitcast(BF16)[:, 0:6 * CW].rearrange("p (a j t) -> p a j t", a=2, j=3)
                 for t in (pr, prT)]
        kst, qst = [t[:].rearrange("p a u k -> p (a u k)").bitcast(BF16).rearrange("p (u t) -> p u t", u=TURN)
                    for t in (pr, prT)]
        v_all = y_att[:].rearrange("p b t -> p (b t)")[:, 4:4 + TOK]
        o_all = y_mid[:].rearrange("p b t -> p (b t)")[:, 4:4 + TOK]
        pT = [t1[:, 0, :], t1[:, 1, 0:896], t2[:, 0, 0:768], t2[:, 1, 0:640],
              qkn[:, 0, 0:512], qkn[:, 0, 512:896], qkn[:, 1, 0:256], qkn[:, 1, 256:384]]
        acc = psr[:, 2:4, :]
        acc_sb = sqk
        causal_s = sb("causal_s", [P, 2, P], BF16)
        vh = sb("vh", [P, 2, NT, VW])
        nm = sb("nm", [P, 2, 2, NT])
        nres = sb("nres", [P, 2, NT])
        nparts = sb("nparts", [P, 2, 3, NT], BF16)
        nT = sb("nT", [3 * NT, 2, P], BF16)
        osum = sb("osum", [P, 2, NT, VW])
        orec = sb("orec", [P, 2, NT])
        scratch = nc.dram_tensor("scratch", (2, HEADS, 3, GD, S), BF16, kind="Internal").ap()

        one = lambda name, per: Count(sem(name), per)
        hs_ready = one("hs_ready", 2)
        tab_scaled = one("tab_scaled", 2)
        qk_ps = one("qk_ps", 4)
        v_ps = one("v_ps", 4)
        sq_done = one("sq_done", 4)
        ss_red = one("ss_red", 4)
        ss_lift = one("ss_lift", 8)
        rn_log = one("rn_log", 4)
        rn_guess = one("rn_guess", 4)
        rn_step = one("rn_step", 12)
        qkn_done = one("qkn_done", 4)
        t1_done = one("t1_done", 4)
        t2_done = one("t2_done", 8)
        rot_done = one("rot_done", 4)
        ring_ps = one("ring_ps", 24)
        ring_free = one("ring_free", 24)
        k_carry = one("k_carry", 4)
        v_sb = one("v_sb", 4)
        s_ps = one("s_ps", 4)
        max_done = one("max_done", 4)
        exp_done = one("exp_done", 4)
        rsum_done = one("rsum_done", 4)
        p_norm = one("p_norm", 4)
        wo_ps = one("wo_ps", 1)
        y1_done = one("y1_done", 1)
        h1_done = one("h1_done", 2)
        mean_ps = one("mean_ps", 1)
        hc_done = one("hc_done", 1)
        hq_done = one("hq_done", 1)
        var_ps = one("var_ps", 1)
        lnv_done = one("lnv_done", 1)
        rstd_done = one("rstd_done", 1)
        hn_done = one("hn_done", 2)
        g_ps = one("g_ps", CH)
        gelu_done = one("gelu_done", CH)
        a_ps = one("a_ps", CH)
        glu_done = one("glu_done", CH)
        w2_ps = one("w2_ps", 1)
        yo_done = one("yo_done", 2)
        v_lo = [Count(sem(f"v_lo{b}"), 1, 16, 0) for b in range(B)]
        v_hi = [Count(sem(f"v_hi{b}"), 1, 16, 0) for b in range(B)]
        scl_in = sem("scl_in")
        wqkv_in = sem("wqkv_in")
        wmlp_in = sem("wmlp_in")
        const_in = sem("const_in")
        memsets = sem("memsets")
        x_in = [sem(f"x_in{i}") for i in range(2)]
        xt_ps = sem("xt_ps")
        xt_sb = sem("xt_sb")
        n_mean = sem("n_mean")
        n_cen = sem("n_cen")
        n_sq = sem("n_sq")
        n_var = sem("n_var")
        n_log = sem("n_log")
        n_rstd = sem("n_rstd")
        n_out = sem("n_out")
        o_stage = sem("o_stage")
        o_ps = sem("o_ps")
        o_sb = sem("o_sb")
        o_out = [sem(f"o_out{i}") for i in range(2)]
        N_MEMSET = 13
        gw_in = sem("gw_in")
        gz_done = sem("gz_done")
        gqk_ps = sem("gqk_ps")
        gv_ps = sem("gv_ps")
        gv_sb = sem("gv_sb")
        grot = sem("grot")
        gsum = sem("gsum")
        gp1 = sem("gp1")
        gr1 = sem("gr1")
        gp2 = sem("gp2")
        gp3 = sem("gp3")
        gparts_out = [sem(f"gparts_out{u}") for u in range(2)]
        st_in = [sem(f"st_in{u}") for u in range(TURN)]
        tail_in = sem("tail_in")
        p1_ps = one("p1_ps", len(CHUNKS))
        p1_max = one("p1_max", len(CHUNKS))
        nm_done = one("nm_done", 1)
        n1_done = one("n1_done", 1)
        r1_done = one("r1_done", 1)
        n2_done = one("n2_done", 1)
        n3_done = one("n3_done", 1)
        nT_ps = one("nT_ps", 1)
        nT_sb = one("nT_sb", 1)
        nT_in = [sem(f"nT_in{u}") for u in range(TURN)]
        p2_ps = one("p2_ps", NT)
        p2_exp = one("p2_exp", NT)
        vh_done = one("vh_done", 1)
        pv_ps = one("pv_ps", 2)
        acc_done = one("acc_done", 1)
        fin_ps = one("fin_ps", 1)
        osum_done = one("osum_done", 1)
        orec_done = one("orec_done", 1)
        o_done = one("o_done", 1)
        w_stage = sem("w_stage")
        w_tps = sem("w_tps")
        w_tsb = sem("w_tsb")
        w_ps = sem("w_ps")
        w_done = sem("w_done")
        zero_done = sem("zero_done")

        credits = {
            "vector": [hs_ready, tab_scaled, ss_red, ss_lift, rn_step, qkn_done, t1_done, rot_done, k_carry, max_done,
                       rsum_done, y1_done, h1_done, hc_done, hn_done, glu_done, yo_done, p1_max, nm_done, n1_done,
                       r1_done, n2_done, n3_done, nT_sb, vh_done, osum_done, orec_done, o_done],
            "scalar": [sq_done, rn_log, rn_guess, ring_free, v_sb, exp_done, hq_done, lnv_done, rstd_done,
                       gelu_done, p2_exp, acc_done],
            "tensor": [qk_ps, v_ps, ring_ps, s_ps, wo_ps, mean_ps, var_ps, g_ps, a_ps, w2_ps,
                       p1_ps, nT_ps, p2_ps, pv_ps, fin_ps],
            "gpsimd": [t2_done, p_norm],
        }

        def steps(eng, step, layer0):
            for l in range(DEPTH):
                lay = layer0 + l
                step((lay, 0), (lay - 1, NT - 1) if l else None)
                with eng.Fori(1, NT) as n:
                    step((lay, n), (lay, n - 1))
            step(None, (layer0 + 1, NT - 1))

        def head_steps(eng, step):
            for i in range(TURN):
                step(i, i)
            with eng.Fori(1, HEADS // TURN) as g:
                for u in range(TURN):
                    step(g * TURN + u, u)
            for u in range(3):
                step(HEADS + u, u)

        def live(i, back):
            return not isinstance(i, int) or back <= i < HEADS + back

        def ring1(i, u):
            jobs = [("max", i, c) for c in range(len(CHUNKS))] if live(i, 0) else []
            if live(i, 1):
                jobs.insert(2, ("nT", i - 1, 0))
            first = (u + 1) % 2 if not isinstance(i, int) or i else 0
            return [(*job, (first + n) % 2) for n, job in enumerate(jobs)]

        def ring1_free(eng, i, jobs, n):
            if n < 2:
                kind, head, c = "max", i - 1, len(CHUNKS) - 2 + n
                if isinstance(head, int) and head < 0:
                    return
            else:
                kind, head, c, _ = jobs[n - 2]
            need(eng, p1_max if kind == "max" else nT_sb, 0, head, c + 1)

        def ring2(i, u):
            jobs = [("fin", i - 3, 0)] if live(i, 3) else []
            if live(i, 2):
                jobs += [("exp", i - 2, kt) for kt in range(NT)]
            first = (u + 1) % 2 if not isinstance(i, int) or i > 2 else 0
            return [(*job, (first + n) % 2) for n, job in enumerate(jobs)]

        def ring2_free(eng, i, jobs, n):
            if n < 2:
                kind, head, c = "exp", i - 3, NT - 2 + n
                if isinstance(head, int) and head < 0:
                    return
            else:
                kind, head, c, _ = jobs[n - 2]
            need(eng, p2_exp if kind == "exp" else osum_done, 0, head, c + 1)

        M_JOBS = ["v0", "wo", "v1", "mean", "v2", "var", "v3", "g0", "g1", "g2", "a0", "a1", "a2", "w2"]

        def m_free(eng, job, att, mlp):
            of_v = lambda j: j in ("v0", "v1", "v2", "v3")
            names = [j for j in M_JOBS if (att if of_v(j) else mlp) is not None]
            i = names.index(job)
            if i == 0:
                need(eng, yo_done, *(mlp if mlp is not None else att), 0)
                need(eng, v_sb, *(att if att is not None else (mlp[0] + 1, 0)), 0)
                return
            j = names[i - 1]
            is_v = of_v(j)
            lay, n = att if is_v else mlp
            if is_v:
                need(eng, v_sb, lay, n, int(j[1]) + 1)
            elif j == "wo":
                need(eng, y1_done, lay, n, 1)
            elif j == "mean":
                need(eng, hc_done, lay, n, 1)
            elif j == "var":
                need(eng, lnv_done, lay, n, 1)
            elif j[0] == "g":
                need(eng, gelu_done, lay, n, int(j[1]) + 1)
            elif j[0] == "a":
                need(eng, glu_done, lay, n, int(j[1]) + 1)

        RING = []
        for s in range(B + 2):
            if 1 <= s <= B:
                RING += [("q", s - 1), ("k", s - 1)]
            if s >= 2:
                RING += [("pt0", s - 2), ("pt1", s - 2), ("pv0", s - 2), ("pv1", s - 2)]
        ring_at = {job: i for i, job in enumerate(RING)}

        block = ctx.enter_context(nc.Block())

        def turn_at(i, u, per, first):
            if isinstance(i, int):
                return (i // TURN) * per + first
            return (i - u) * (per // TURN) + first

        @block.sync
        def _(sp):
            sp.dma_start(identf[:], identf_d).then_inc(const_in, 16)
            sp.dma_start(identb[:], identb_d).then_inc(const_in, 16)
            sp.dma_start(mask[:], bandmask).then_inc(const_in, 16)
            sp.dma_start(ropec[:], rope_cos).then_inc(const_in, 16)
            sp.dma_start(ropes[:], rope_sin).then_inc(const_in, 16)
            sp.dma_start(causal_s[:], causal).then_inc(const_in, 16)
            with sp.Fori(0, NT // 2) as i:
                for u in range(2):
                    sp.wait_ge(xt_ps, 2 * i + u + 1)
                    sp.dma_start(prT[:, u, 0:B, :], x[:, bass.ds((2 * i + u) * P, P), :].rearrange("b p d -> p b d")).then_inc(x_in[u], 16)

            def load_attention(lay):
                l = lay % DEPTH
                if lay == DEPTH:
                    sp.wait_ge(w_ps, NT)
                need(sp, v_ps, lay, 0, 0)
                need(sp, qk_ps, lay, 0, 0)
                need(sp, t2_done, lay, 0, 0)
                sp.dma_start(wqkv_s[:], wqkv[l]).then_inc(wqkv_in, 16)
                sp.dma_start(scl[:], qkscale[l]).then_inc(scl_in, 16)

            def load_mlp(lay):
                l = lay % DEPTH
                need(sp, w2_ps, lay, 0, 0)
                need(sp, yo_done, lay, 0, 0)
                sp.dma_start(wo_s[:], wo[l].rearrange("(j p) n -> p j n", p=P)).then_inc(wmlp_in, 16)
                sp.dma_start(w1_s[:], w1[l]).then_inc(wmlp_in, 16)
                sp.dma_start(w2_s[:, 0:2, :], w2[l, 0:2 * P, :].rearrange("(j p) n -> p j n", p=P)).then_inc(wmlp_in, 16)
                sp.dma_start(w2_s[0:CHN[2], 2, :], w2[l, 2 * P:HID, :]).then_inc(wmlp_in, 16)
                sp.dma_start(cols_s[:], cols[l]).then_inc(wmlp_in, 16)

            def step(att, mlp):
                if att is not None:
                    lay, n = att
                    if isinstance(n, int) and n == 0:
                        load_attention(lay)
                    for b in range(B):
                        need(sp, ring_ps, lay, n, ring_at["pv1", b] - 24 + 1)
                        if isinstance(n, int) and n == 0 and lay == 0:
                            sp.wait_ge(memsets, N_MEMSET)
                        sp.dma_start(vprev[0:WIN, b, :], vown[WIN:P, b, :]).then_inc(v_lo[b].sem, 16)
                    for b in range(B):
                        need(sp, v_sb, lay, n, b + 1)
                        sp.dma_start(vprev[WIN:P, b, :], vown[0:WIN, b, :]).then_inc(v_hi[b].sem, 16)
                if mlp is not None and att is not None and isinstance(att[1], int):
                    load_mlp(att[0])
                elif att is not None and isinstance(att[1], int):
                    load_mlp(att[0])
            steps(sp, step, 0)

            need(sp, v_ps, DEPTH, 0, 0)
            need(sp, yo_done, DEPTH, 0, 0)
            sp.dma_start(gw_s, gw.rearrange("w p n -> p w n")).then_inc(gw_in, 16)
            sp.dma_start(gcos, g_cos).then_inc(gw_in, 16)
            sp.dma_start(gsin, g_sin).then_inc(gw_in, 16)
            with sp.Fori(0, B) as b:
                for u in range(2):
                    sp.wait_ge(gp1, 2 * b + u + 1)
                    sp.wait_ge(gp2, 2 * b + u + 1)
                    sp.wait_ge(gp3, 2 * b + u + 1)
                    for a in range(2):
                        for j in range(3):
                            sp.dma_start(scratch[a, bass.ds(b * GH, GH), j, :, u * CW:(u + 1) * CW],
                                         parts[u][:, a, j, :]).then_inc(gparts_out[u], 16)
            for u in range(2):
                sp.wait_ge(gparts_out[u], 96 * (B + 1))
            for u in range(TURN):
                sp.dma_start(kst[3 * 3 * GD:STACK, u, :], stack_tail[0]).then_inc(tail_in, 16)

            def load_stacks(i, u):
                need(sp, pv_ps, 0, i - TURN + 1, 0) if live(i, TURN) else None
                src = scratch[0, bass.ds(i, 1), :, :, :].rearrange("o j d t -> (o j d) t").unsqueeze(0)
                sp.dma_start(qst[0:9 * GD, u, :], src.broadcast_to([3, 3 * GD, S])).then_inc(st_in[u], 16)
                sp.dma_start(qst[9 * GD:STACK, u, :], stack_tail[1]).then_inc(st_in[u], 16)
                for j in range(3):
                    sp.dma_start(kst[3 * GD * j:3 * GD * (j + 1), u, :],
                                 scratch[1, bass.ds(i, 1), j, :, :].broadcast_to([3, GD, S])).then_inc(st_in[u], 16)

            def store_max(i, u):
                need(sp, nT_sb, 0, i, 1)
                sp.dma_start(qst[9 * GD:9 * GD + 3, u, :], nT[:, u % 2, :]).then_inc(nT_in[u], 16)

            def head_step(i, u):
                if live(i, 0):
                    load_stacks(i, u)
                if live(i, 2):
                    store_max(i - 2, (u - 2) % TURN)
            for i in range(TURN):
                head_step(i, i)
            with sp.Fori(1, HEADS // TURN) as g:
                for u in range(TURN):
                    head_step(g * TURN + u, u)
            for i in range(HEADS, HEADS + 2):
                head_step(i, i % TURN)

            steps(sp, step, DEPTH)
            with sp.Fori(0, NT // 2) as i:
                for u in range(2):
                    sp.wait_ge(o_sb, 2 * i + u + 3)
                    sp.dma_start(out[:, bass.ds((2 * i + u) * P, P), :].rearrange("b p d -> p b d"), pr[:, u, 0:B, :]).then_inc(o_out[u], 16)
            for u in range(2):
                sp.wait_ge(o_out[u], 16 * (NT // 2 + 1))

        @block.tensor
        def _(pe):
            for c in credits["tensor"]:
                pe.sem_inc(c.sem, 1)
            pe.wait_ge(const_in, 96)
            pe.wait_ge(memsets, N_MEMSET)
            with pe.Fori(0, NT // 2) as i:
                for u in range(2):
                    pe.wait_ge(x_in[u], 16 * i + 16)
                    pe.wait_ge(xt_sb, 2 * i + u + 1)
                    for b in range(B):
                        last = pe.transpose(ps_qk[:, u, b * P:(b + 1) * P], prT[:, u, b, :], identf[:])
                    last.then_inc(xt_ps, 1)

            def norm(k, src):
                base = 1 + k * BLOCKS
                with pe.Fori(0, BLOCKS // 2) as i:
                    for u in range(2):
                        pe.wait_ge(n_cen, base + 2 * i)
                        pe.matmul(ps_qk[:, u, :], ones[:], src[:, bass.ds((2 * i + u) * CW, CW)],
                                  start=True, stop=True).then_inc(n_mean, 1)
                    for u in range(2):
                        pe.wait_ge(n_sq, k * BLOCKS + 2 * i + u + 1)
                        pe.matmul(ps_s[:, u, :], ones[:], t1[:, u, 0:CW], start=True, stop=True).then_inc(n_var, 1)

            xf = xT[:, :, :].rearrange("p b t -> p (b t)")

            def step(att, mlp):
                for s in range(B + 2):
                    if att is not None and s < B:
                        lay, n = att
                        if s == 0:
                            if isinstance(n, int) and n == 0:
                                pe.wait_ge(wqkv_in, 16 * (lay + 1))
                            need(pe, hs_ready, lay, n, 2)
                        need(pe, qkn_done, lay, n, s)
                        for j in range(2):
                            last = pe.matmul(ps_qk[:, j, :], hs[:, s, :], wqkv_s[:, j * INNER:(j + 1) * INNER],
                                             start=True, stop=True)
                        last.then_inc(qk_ps.sem, 1)
                        m_free(pe, f"v{s}", att, mlp)
                        pe.matmul(psm[:], hs[:, s, :], wqkv_s[:, 2 * INNER:], start=True, stop=True).then_inc(v_ps.sem, 1)
                    if mlp is not None and s == 0:
                        lay, m = mlp
                        pe.wait_ge(wmlp_in, 80 * (lay + 1))
                        m_free(pe, "wo", att, mlp)
                        need(pe, ring_free, lay, m, 24)
                        for j in range(PAIRS):
                            last = pe.matmul(psm[:], wo_s[:, j, :], oT[:, j, :, :], start=(j == 0), stop=(j == PAIRS - 1))
                        last.then_inc(wo_ps.sem, 1)
                    if att is not None and 1 <= s <= B:
                        lay, n = att
                        b = s - 1
                        need(pe, rot_done, lay, n, b + 1)
                        for j, what in enumerate("qk"):
                            r = ring_at[what, b]
                            need(pe, ring_free, lay, n, r - 2)
                            for i in range(PAIRS):
                                last = pe.transpose(psr[:, r % 3, i * P:(i + 1) * P],
                                                    t1[:, b % 2, j * INNER + i * P:j * INNER + (i + 1) * P], identf[:])
                            last.then_inc(ring_ps.sem, 1)
                    if mlp is not None and s == 1:
                        lay, m = mlp
                        m_free(pe, "mean", att, mlp)
                        need(pe, h1_done, lay, m, 2)
                        pe.matmul(psm[:], ones[:], h1[:], start=True, stop=True).then_inc(mean_ps.sem, 1)
                    if mlp is not None and s == 2:
                        lay, m = mlp
                        m_free(pe, "var", att, mlp)
                        need(pe, hq_done, lay, m, 1)
                        pe.matmul(psm[:], ones[:], hq[:], start=True, stop=True).then_inc(var_ps.sem, 1)
                    if att is not None and 1 <= s <= B:
                        lay, n = att
                        b = s - 1
                        need(pe, exp_done, lay, n, b)
                        for j in range(PAIRS):
                            pe.matmul(ps_s[:, j // 2, (j % 2) * 2 * P:(j % 2 + 1) * 2 * P], identb[:],
                                      mask[:, bass.ds(2 * n, 2), :], start=(j % 2 == 0), stop=False, skip_group_check=True)
                        need(pe, ring_free, lay, n, ring_at["k", b] + 1)
                        for j in range(PAIRS):
                            for w in range(2):
                                last = pe.matmul(ps_s[:, j // 2, ((j % 2) * 2 + w) * P:((j % 2) * 2 + w + 1) * P],
                                                 qbd[:, b % 2, j, w, :], kT[:, b, j, w * WIN:w * WIN + P],
                                                 start=False, stop=(j % 2 == 1 and w == 1), skip_group_check=True)
                        last.then_inc(s_ps.sem, 1)
                    if mlp is not None and s == 4:
                        lay, m = mlp
                        for j in range(CH):
                            if j == 0:
                                need(pe, hn_done, lay, m, 2)
                            m_free(pe, f"g{j}", att, mlp)
                            pe.matmul(psm[0:CHN[j], :], w1_s[:, HID + j * P:HID + j * P + CHN[j]], hn[:],
                                      start=True, stop=True).then_inc(g_ps.sem, 1)
                    for h in range(2):
                        if att is not None and s >= 2:
                            lay, n = att
                            b = s - 2
                            r = ring_at[f"pt{h}", b]
                            if h == 0:
                                need(pe, p_norm, lay, n, b + 1)
                            need(pe, ring_free, lay, n, r - 2)
                            for i in range(4):
                                last = pe.transpose(psr[:, r % 3, i * P:(i + 1) * P], pr[:, b % 2, 4 * h + i, :], identf[:])
                            last.then_inc(ring_ps.sem, 1)
                        if mlp is not None and s in (4, 5) and not (s == 5 and h == 1):
                            lay, m = mlp
                            j = (s - 4) * 2 + h
                            m_free(pe, f"a{j}", att, mlp)
                            pe.matmul(psm[0:CHN[j], :], w1_s[:, j * P:j * P + CHN[j]], hn[:],
                                      start=True, stop=True).then_inc(a_ps.sem, 1)
                    if att is not None and s >= 2:
                        lay, n = att
                        b = s - 2
                        need(pe, v_lo[b], lay, n, 1)
                        need(pe, v_hi[b], lay, n, 1)
                        for h in range(2):
                            r = ring_at[f"pv{h}", b]
                            need(pe, ring_free, lay, n, max(r - 2, ring_at[f"pt{h}", b] + 1))
                            for i in range(4):
                                u = 4 * h + i
                                v = (vprev, vown)[u % 2]
                                last = pe.matmul(psr[:, r % 3, i * P:(i + 1) * P], v[:, b, (u // 2) * P:(u // 2 + 1) * P],
                                                 prT[:, b % 2, u, :], start=True, stop=True)
                            last.then_inc(ring_ps.sem, 1)
                if mlp is not None:
                    lay, m = mlp
                    m_free(pe, "w2", att, mlp)
                    for j in range(CH):
                        last = pe.matmul(psm[:], w2_s[0:CHN[j], j, :], act_t[0:CHN[j], j, :], start=(j == 0), stop=(j == CH - 1))
                    last.then_inc(w2_ps.sem, 1)

            pe.wait_ge(xt_sb, NT + 2)
            norm(0, xf)
            steps(pe, step, 0)
            need(pe, yo_done, DEPTH, 0, 0)
            norm(1, xf)

            pe.wait_ge(gw_in, 48)
            with pe.Fori(0, B) as b:
                for u in range(2):
                    pe.wait_ge(gz_done, 2 * b + u + 1)
                    pe.wait_ge(grot, 2 * (2 * b + u) + 1)
                    for j in range(2):
                        pe.matmul(ps_qk[:, j, :], gw_s[:, j, :], zs[u], start=True, stop=True)
                    for j in range(2):
                        last = pe.matmul(ps_s[:, j, :], gw_s[:, 2 + j, :], zs[u], start=True, stop=True)
                    last.then_inc(gqk_ps, 1)
                    pe.wait_ge(gv_sb, 2 * b + u + 1)
                    for i in range(4):
                        last = pe.matmul(psr[:, u, i * P:(i + 1) * P], zs[u][:, i * P:(i + 1) * P], gw_s[:, 4, :],
                                         start=True, stop=True)
                    last.then_inc(gv_ps, 1)

            pe.wait_ge(tail_in, 16 * TURN)
            pe.wait_ge(gv_sb, 2 * B + 2)
            pe.wait_ge(grot, 4 * B + 1)

            def max_job(i, u, c, bank):
                t, half = CHUNKS[c]
                lo, hi = half * 512, min((t + 1) * P, (half + 1) * 512)
                diag = hi == (t + 1) * P
                last = pe.matmul(psr[:, bank, 0:hi - lo], qst[0:STACK, u, t * P:(t + 1) * P], kst[0:STACK, u, lo:hi],
                                 start=True, stop=not diag)
                if diag:
                    last = pe.matmul(psr[:, bank, hi - lo - P:hi - lo], identb[:], causal_s[:, 0, :], start=False, stop=True)
                last.then_inc(p1_ps.sem, 1)

            def exp_job(i, u, kt, bank):
                if kt == 0:
                    pe.wait_ge(nT_in[u], turn_at(i, u, 16, 16))
                where = (ps_qk, ps_s)[bank]
                n = S - kt * P
                for lo in range(0, n, 512):
                    hi = min(n, lo + 512)
                    last = pe.matmul(where[:, lo // 512, 0:hi - lo], kst[0:STACK, u, kt * P:(kt + 1) * P],
                                     qst[0:STACK, u, kt * P + lo:kt * P + hi], start=True, stop=lo > 0)
                    if lo == 0:
                        last = pe.matmul(where[:, 0, 0:P], identb[:], causal_s[:, 1, :], start=False, stop=True)
                last.then_inc(p2_ps.sem, 1)

            def products(i, u, part):
                need(pe, p2_exp, 0, i, 4 * part + 4)
                if part == 0:
                    need(pe, vh_done, 0, i, 1)
                    pe.wait_ge(zero_done, 1)
                    need(pe, acc_done, 0, i, 0)
                for half in range(part, 2):
                    for kt in range(4 * part, 4 * part + 4):
                        lo = max(kt * P, half * 512)
                        c = kt % 4
                        last = pe.matmul(acc[32 * c:32 * c + VW, half, lo - half * 512:512], vh[:, u % 2, kt, :],
                                         pT[kt][:, lo - kt * P:(half + 1) * 512 - kt * P],
                                         start=(part == 0), stop=(part == 1 or half == 0), skip_group_check=True)
                last.then_inc(pv_ps.sem, 1)

            def head_step(i, u):
                jobs1, jobs2 = ring1(i, u), ring2(i, u)
                order = []
                for n in range(max(len(jobs1), len(jobs2) * 3 // 2 + 2)):
                    if n < len(jobs1):
                        order.append((1, n))
                    while len([o for o in order if o[0] == 2]) < min(len(jobs2), (n + 1) * 9 // 13 + (0 if n < len(jobs1) - 1 else len(jobs2))):
                        order.append((2, len([o for o in order if o[0] == 2])))
                if live(i, 0):
                    pe.wait_ge(st_in[u], turn_at(i, u, 80, 80))
                for ring, n in order:
                    if ring == 1:
                        kind, head, c, bank = jobs1[n]
                        ring1_free(pe, i, jobs1, n)
                        if kind == "max":
                            max_job(head, u, c, bank)
                        else:
                            need(pe, n3_done, 0, head, 1)
                            pe.transpose(psr[0:3 * NT, bank, 0:P // 2].bitcast(BF16),
                                         nparts[:, (u - 1) % 2, :, :].rearrange("p j t -> p (j t)"),
                                         identb[:]).then_inc(nT_ps.sem, 1)
                    else:
                        kind, head, c, bank = jobs2[n]
                        ring2_free(pe, i, jobs2, n)
                        if kind == "fin":
                            need(pe, acc_done, 0, head, 1)
                            where = (ps_qk, ps_s)[bank]
                            for t in range(NT):
                                last = pe.transpose(where[:, t // 4, (t % 4) * P:(t % 4 + 1) * P],
                                                    acc_sb[:, t * P:(t + 1) * P], identf[:])
                            last.then_inc(fin_ps.sem, 1)
                        else:
                            exp_job(head, (u - 2) % TURN, c, bank)
                            if c == 5:
                                products(head, (u - 2) % TURN, 0)
                if live(i, 2):
                    products(i - 2, (u - 2) % TURN, 1)
            head_steps(pe, head_step)

            with pe.Fori(0, NT // 2) as i:
                for u in range(2):
                    pe.wait_ge(w_stage, 2 * i + u + 1)
                    pe.wait_ge(w_tsb, 2 * i + u + 1)
                    for b in range(B):
                        last = pe.transpose(ps_qk[:, u, b * P:(b + 1) * P], t1[:, u, b * P:(b + 1) * P], identf[:])
                    last.then_inc(w_tps, 1)
                    pe.wait_ge(w_tsb, 2 * i + u + 3)
                    pe.wait_ge(w_done, 2 * i + u + 1)
                    pe.matmul(ps_s[:, u, :], gw_s[:, 5, :], t2[:, u, 0:CW], start=True, stop=True).then_inc(w_ps, 1)

            pe.wait_ge(w_done, NT + 2)
            norm(2, xf)
            steps(pe, step, DEPTH)
            with pe.Fori(0, NT // 2) as i:
                for u in range(2):
                    pe.wait_ge(o_stage, 2 * i + u + 1)
                    pe.wait_ge(o_sb, 2 * i + u + 1)
                    for b in range(B):
                        last = pe.transpose(ps_qk[:, u, b * P:(b + 1) * P], prT[:, u, b, :], identf[:])
                    last.then_inc(o_ps, 1)

        @block.vector
        def _(dve):
            for c in credits["vector"]:
                dve.sem_inc(c.sem, 1)
            dve.sem_inc(n_cen, 1)
            dve.sem_inc(n_out, 1)
            for buf in (qbd[:], kT[:], vown[:], vprev[:]):
                dve.memset(buf, 0.0).then_inc(memsets, 1)
            dve.memset(ones[:], 1.0 / P).then_inc(memsets, 1)
            dve.memset(consts[:, 0:1], LN_EPS).then_inc(memsets, 1)
            dve.memset(consts[:, 1:2], 0.5 * NORM_LIFT * float(np.log(2.0))).then_inc(memsets, 1)
            for y in (y_in, y_att, y_mid):
                dve.memset(y[:, :, 0:1], 0.0).then_inc(memsets, 1)
            dve.memset(w2_s[:, 2, :], 0.0).then_inc(memsets, 1)
            dve.memset(hs[:], 0.0).then_inc(memsets, 1)
            dve.memset(vh[:, :, :, GD:VW], 1.0).then_inc(memsets, 1)
            dve.wait_ge(memsets, N_MEMSET)
            dve.wait_ge(const_in, 96)

            def norm(k, src, dst, dst_off, dst_row):
                base = 1 + k * BLOCKS
                with dve.Fori(0, BLOCKS // 2) as i:
                    for u in range(2):
                        dve.wait_ge(n_mean, k * BLOCKS + 2 * i + u + 1)
                        dve.wait_ge(n_out, base + 2 * i)
                        dve.tensor_tensor(qkn[:, u, 0:CW], src[:, bass.ds((2 * i + u) * CW, CW)], ps_qk[:, u, :],
                                          ALU.subtract).then_inc(n_cen, 1)
                    for u in range(2):
                        dve.wait_ge(n_rstd, k * BLOCKS + 2 * i + u + 1)
                        dve.wait_ge(n_cen, base + 2 * i + u + 1)
                        dve.tensor_tensor(dst[:, bass.ds(i, 1), 1 + u * CW:1 + (u + 1) * CW].rearrange("p a t -> p (a t)"),
                                          qkn[:, u, 0:CW], t2[:, u, 0:CW], ALU.mult).then_inc(n_out, 1)

            def scale_tables(lay, n):
                dve.wait_ge(scl_in, 16 * (lay + 1))
                need(dve, t1_done, lay, n, 0)
                need(dve, t2_done, lay, n, 0)
                for i, tab in enumerate((ropec, ropes)):
                    dve.tensor_tensor(rope_n[:, i, :, :], tab[:, bass.ds(n, 1), :, :].rearrange("p o a d -> p (o a) d"),
                                      scl[:, i, :, :], ALU.mult).then_inc(tab_scaled.sem, 1)

            def stage(lay, n):
                y = (y_in, y_mid)[lay % DEPTH]
                dve.wait_ge(v_ps.sem, v_ps.at(lay, n, 0))
                need(dve, qk_ps, lay, n, 0)
                if isinstance(n, int):
                    if lay % DEPTH:
                        need(dve, yo_done, lay - 1, 0, 2)
                    else:
                        dve.wait_ge(n_out, 1 + BLOCKS * (2 * (lay // DEPTH) + 1))
                elif lay % DEPTH:
                    pass
                dve.tensor_copy(hs[0:64, :, :], y[0:64, :, bass.ds(n * P + 1, P)]).then_inc(hs_ready.sem, 1)
                dve.tensor_copy(hs[64:P, :, :], y[64:P, :, bass.ds(n * P, P)]).then_inc(hs_ready.sem, 1)

            def step(att, mlp):
                if att is not None:
                    lay, n = att
                    stage(lay, n)
                    scale_tables(lay, n)
                for s in range(B + 2):
                    if att is not None and s < B:
                        lay, n = att
                        u = s % 2
                        need(dve, s_ps, lay, n, s - 3)
                        need(dve, ring_free, lay, n, ring_at["k", s] + 1 - 24)
                        dve.tensor_copy(kT[:, s, :, 0:WIN], kT[:, s, :, P:P + WIN]).then_inc(k_carry.sem, 1)
                        need(dve, sq_done, lay, n, s + 1)
                        dve.tensor_reduce(nw[:, u, 1, :], sqk[:].rearrange("p (h d) -> p h d", d=FD), axis=AX,
                                          op=ALU.add).then_inc(ss_red.sem, 1)
                        need(dve, ss_red, lay, n, s + 1)
                        dve.tensor_scalar(ss[:, u, 0, :], nw[:, u, 1, :], 1e-24, None, ALU.max).then_inc(ss_lift.sem, 1)
                        dve.tensor_scalar(ss[:, u, 1, :], nw[:, u, 1, :], 1e-24, float(2.0 ** NORM_LIFT), ALU.max,
                                          ALU.mult).then_inc(ss_lift.sem, 1)
                    if mlp is not None and s == 1:
                        lay, m = mlp
                        y = (y_in, y_mid)[lay % DEPTH]
                        need(dve, wo_ps, lay, m, 1)
                        dve.tensor_tensor(y_att[:, :, bass.ds(m * P + 1, P)], psm[:].rearrange("p (b t) -> p b t", b=B),
                                          y[:, :, bass.ds(m * P + 1, P)], ALU.add).then_inc(y1_done.sem, 1)
                        need(dve, y1_done, lay, m, 1)
                        h1v = h1[:].rearrange("p (b t) -> p b t", b=B)
                        dve.tensor_scalar(h1v[0:64, :, :], y_att[0:64, :, bass.ds(m * P + 1, P)], 1.0, None, ALU.mult).then_inc(h1_done.sem, 1)
                        dve.tensor_copy(h1v[64:P, :, :], y_att[64:P, :, bass.ds(m * P, P)]).then_inc(h1_done.sem, 1)
                    if mlp is not None and s == 2:
                        lay, m = mlp
                        need(dve, mean_ps, lay, m, 1)
                        need(dve, h1_done, lay, m, 2)
                        dve.tensor_tensor(hc[:], h1[:], psm[:], ALU.subtract).then_inc(hc_done.sem, 1)
                    if att is not None and 1 <= s <= B:
                        lay, n = att
                        need(dve, s_ps, lay, n, s)
                        need(dve, exp_done, lay, n, s - 2)
                        dve.tensor_reduce(nmax[:, (s - 1) % 2, :], ps_s[:].rearrange("p a (u k) -> p (a u) k", k=P), axis=AX,
                                          op=ALU.max, negate=True).then_inc(max_done.sem, 1)
                    if att is not None and s < B:
                        lay, n = att
                        u = s % 2
                        need(dve, rn_guess, lay, n, s + 1)
                        dve.tensor_tensor(nw[:, u, 0, :], ss[:, u, 2, :], ss[:, u, 2, :], ALU.mult).then_inc(rn_step.sem, 1)
                        need(dve, rn_step, lay, n, 3 * s + 1)
                        dve.scalar_tensor_tensor(out=nw[:, u, 1, :], in0=nw[:, u, 0, :], scalar=-0.5, in1=ss[:, u, 0, :],
                                                 op0=ALU.mult, op1=ALU.mult).then_inc(rn_step.sem, 1)
                        need(dve, rn_step, lay, n, 3 * s + 2)
                        dve.scalar_tensor_tensor(out=ss[:, u, 3, :], in0=nw[:, u, 1, :], scalar=1.5, in1=ss[:, u, 2, :],
                                                 op0=ALU.add, op1=ALU.mult).then_inc(rn_step.sem, 1)
                        need(dve, rn_step, lay, n, 3 * s + 3)
                        need(dve, t2_done, lay, n, 2 * s - 2)
                        need(dve, t1_done, lay, n, s - 1)
                        dve.tensor_tensor(qkn[:, u, :].rearrange("p (h d) -> p h d", d=FD),
                                          ps_qk[:].rearrange("p a (h d) -> p (a h) d", d=FD),
                                          ss[:, u, 3, :].unsqueeze(2).broadcast_to([P, 2 * FH, FD]),
                                          ALU.mult).then_inc(qkn_done.sem, 1)
                        need(dve, qkn_done, lay, n, s + 1)
                        need(dve, tab_scaled, lay, n, 2)
                        need(dve, ring_ps, lay, n, ring_at["k", s - 2] + 1 if s >= 2 else ring_at["k", s + 2] + 1 - 24)
                        dve.tensor_tensor(t1[:, u, :].rearrange("p (a h d) -> p a h d", a=2, d=FD),
                                          qkn[:, u, :].rearrange("p (a h d) -> p a h d", a=2, d=FD),
                                          rope_n[:, 0, :, :].unsqueeze(2).broadcast_to([P, 2, FH, FD]),
                                          ALU.mult).then_inc(t1_done.sem, 1)
                    if att is not None and 1 <= s <= B:
                        lay, n = att
                        u = (s - 1) % 2
                        need(dve, exp_done, lay, n, s)
                        need(dve, p_norm, lay, n, s - 2)
                        dve.reciprocal(psum_e[:, u, 1, :], psum_e[:, u, 0, :]).then_inc(rsum_done.sem, 1)
                    if att is not None and s < B:
                        lay, n = att
                        u = s % 2
                        need(dve, t2_done, lay, n, 2 * s + 2)
                        need(dve, t1_done, lay, n, s + 1)
                        dve.tensor_tensor(t1[:, u, :], t1[:, u, :], t2[:, u, :], ALU.add).then_inc(rot_done.sem, 1)
                    if mlp is not None and s == 3:
                        lay, m = mlp
                        need(dve, rstd_done, lay, m, 1)
                        need(dve, hc_done, lay, m, 1)
                        dve.tensor_tensor(hc[:], hc[:], rstd[:], ALU.mult).then_inc(hn_done.sem, 1)
                        need(dve, hn_done, lay, m, 1)
                        dve.wait_ge(wmlp_in, 80 * (lay + 1))
                        dve.tensor_scalar(hn[:], hc[:], cols_s[:, 6:7], cols_s[:, 7:8], ALU.mult,
                                          ALU.add).then_inc(hn_done.sem, 1)
                    if mlp is not None and s >= 4:
                        lay, m = mlp
                        for j in ((0, 1) if s == 4 else (2,)):
                            need(dve, a_ps, lay, m, j + 1)
                            need(dve, gelu_done, lay, m, j + 1)
                            dve.scalar_tensor_tensor(out=act_t[0:CHN[j], j, :], in0=psm[0:CHN[j], :],
                                                     scalar=cols_s[0:CHN[j], j:j + 1], in1=gel[0:CHN[j], j, :],
                                                     op0=ALU.add, op1=ALU.mult).then_inc(glu_done.sem, 1)
                if mlp is not None:
                    lay, m = mlp
                    need(dve, w2_ps, lay, m, 1)
                    pv = psm[:].rearrange("p (b t) -> p b t", b=B)
                    if lay % DEPTH == 0:
                        dst = y_mid[:, :, bass.ds(m * P + 1, P)]
                        dve.scalar_tensor_tensor(out=dst, in0=pv, scalar=cols_s[:, 8:9], in1=y_att[:, :, bass.ds(m * P + 1, P)],
                                                 op0=ALU.add, op1=ALU.add).then_inc(yo_done.sem, 2)
                        need(dve, yo_done, lay, m, 2)
                    else:
                        hv = hc[:].rearrange("p (b t) -> p b t", b=B)
                        dve.scalar_tensor_tensor(out=hv, in0=pv, scalar=cols_s[:, 8:9], in1=y_att[:, :, bass.ds(m * P + 1, P)],
                                                 op0=ALU.add, op1=ALU.add).then_inc(yo_done.sem, 1)
                        need(dve, yo_done, lay, m, 1)
                        xv = xT[:, :, bass.ds(m * P, P)]
                        dve.scalar_tensor_tensor(out=xv, in0=hv, scalar=0.5, in1=xv, op0=ALU.mult,
                                                 op1=ALU.add).then_inc(yo_done.sem, 1)
                        need(dve, yo_done, lay, m, 2)

            xf = xT[:, :, :].rearrange("p b t -> p (b t)")
            dve.wait_ge(xt_sb, NT + 2)
            norm(0, xf, y_in, 1, S + 1)
            steps(dve, step, 0)
            norm(1, xf, y_in, 1, S + 1)

            def stage_z(b, u):
                dve.wait_ge(n_out, 1 + 2 * BLOCKS)
                dve.tensor_copy(zs[u].unsqueeze(1), y_in[:, bass.ds(b, 1), 1 + u * CW:1 + (u + 1) * CW]).then_inc(gz_done, 1)

            dve.memset(acc, 0.0).then_inc(zero_done, 1)

            dve.wait_ge(gw_in, 48)
            with dve.Fori(0, B) as b:
                for u in range(2):
                    dve.wait_ge(gv_ps, 2 * b + u + 1)
                    stage_z(b, u)
                for u in range(2):
                    dve.wait_ge(gqk_ps, 2 * b + u + 1)
                    both = lambda t: t[:, u * CW:(u + 1) * CW].unsqueeze(1).broadcast_to([P, 2, CW])
                    v3 = lambda t: t[:, u, :].rearrange("p (a t) -> p a t", a=2)
                    dve.wait_ge(gsum, 2 * b + 1)
                    dve.tensor_tensor(v3(t1), ps_qk[:], both(gcos), ALU.mult).then_inc(grot, 1)
                    dve.tensor_tensor(v3(t2), ps_s[:], both(gsin), ALU.mult).then_inc(grot, 1)
                    dve.wait_ge(grot, 2 * (2 * b + u) + 3)
                    dve.wait_ge(gparts_out[u], 96 * b + 96)
                    dve.tensor_tensor(t1[:, u, :], t1[:, u, :], t2[:, u, :], ALU.add).then_inc(gsum, 1)
                    dve.wait_ge(gv_ps, 2 * b + u + 3)
                    dve.tensor_scalar(
                        v_all[:, bass.ds(b * S, S)].rearrange("p (h t d) -> p t h d", h=GH, t=NT)[:, 4 * u:4 * u + 4, :, :],
                        psr[:, u, :].rearrange("p (t h d) -> p t h d", t=4, d=GD), 1.0, None, ALU.mult).then_inc(gv_sb, 1)
                    dve.wait_ge(gp1, 2 * b + u + 1)
                    dve.tensor_tensor(v3(t2), v3(t1), parts[u][:, :, 0, :], ALU.subtract).then_inc(gr1, 1)
                    dve.wait_ge(gp2, 2 * b + u + 1)
                    dve.tensor_tensor(parts[u][:, :, 2, :], v3(t2), parts[u][:, :, 1, :], ALU.subtract).then_inc(gp3, 1)
            dve.wait_ge(gv_sb, 2 * B + 2)
            dve.wait_ge(gp3, 2 * B)

            def head_step(i, u):
                if live(i, 2):
                    need(dve, pv_ps, 0, i - 4, 2) if live(i, 4) else None
                    need(dve, vh_done, 0, i - 3, 1) if live(i, 3) else None
                    dve.tensor_scalar(vh[:, u % 2, :, 0:GD], v_all[:, bass.ds((i - 2) * (NT * GD), NT * GD)].rearrange("p (t d) -> p t d", d=GD),
                                      1.0, None, ALU.mult).then_inc(vh_done.sem, 1)
                jobs1 = ring1(i, u)
                for n, (kind, head, c, bank) in enumerate(jobs1):
                    if kind == "max":
                        t, half = CHUNKS[c]
                        cols_n = min((t + 1) * P, (half + 1) * 512) - half * 512
                        need(dve, p1_ps, 0, head, c + 1)
                        if c == 0 and live(i, 2):
                            need(dve, r1_done, 0, head - 2, 1)
                        dve.tensor_reduce(nm[:, u % 2, half, t:t + 1], psr[:, bank, 0:cols_n], axis=AX, op=ALU.max,
                                          negate=True).then_inc(p1_max.sem, 1)
                    else:
                        need(dve, nT_ps, 0, head, 1)
                        dve.wait_ge(nT_in[(u - 3) % TURN], turn_at(i - 3, (u - 3) % TURN, 16, 16)) if live(i, 3) else None
                        dve.tensor_copy(nT[:, (u - 1) % 2, :], psr[0:3 * NT, bank, 0:P // 2].bitcast(BF16)).then_inc(nT_sb.sem, 1)
                    if n == 2 and live(i, 3):
                        k = (u - 3) % 2
                        bank2 = ring2(i, u)[0][3]
                        need(dve, fin_ps, 0, i - 3, 1)
                        finish(i - 3, k, bank2)
                if live(i, 3) and len(jobs1) < 3:
                    need(dve, fin_ps, 0, i - 3, 1)
                    finish(i - 3, (u - 3) % 2, ring2(i, u)[0][3])
                if live(i, 0):
                    k = u % 2
                    need(dve, p1_max, 0, i, len(CHUNKS))
                    dve.tensor_tensor(nm[:, k, 0, 4:NT], nm[:, k, 0, 4:NT], nm[:, k, 1, 4:NT], ALU.min).then_inc(nm_done.sem, 1)
                    need(dve, nm_done, 0, i, 1)
                    need(dve, nT_ps, 0, i - 1, 0) if live(i, 2) else None
                    dve.tensor_copy(nparts[:, k, 0, :], nm[:, k, 0, :]).then_inc(n1_done.sem, 1)
                    need(dve, n1_done, 0, i, 1)
                    dve.tensor_tensor(nres[:, k, :], nm[:, k, 0, :], nparts[:, k, 0, :], ALU.subtract).then_inc(r1_done.sem, 1)
                    need(dve, r1_done, 0, i, 1)
                    dve.tensor_copy(nparts[:, k, 1, :], nres[:, k, :]).then_inc(n2_done.sem, 1)
                    need(dve, n2_done, 0, i, 1)
                    dve.tensor_tensor(nparts[:, k, 2, :], nres[:, k, :], nparts[:, k, 1, :], ALU.subtract).then_inc(n3_done.sem, 1)

            def finish(head, k, bank):
                where = (ps_qk, ps_s)[bank]
                need(dve, o_done, 0, head, 0)
                dve.tensor_reduce(osum[:, k, :, :],
                                  where[:].rearrange("p a (t c w) -> p (a t) w c", c=4, w=32)[:, :, 0:VW, :], axis=AX,
                                  op=ALU.add).then_inc(osum_done.sem, 1)
                need(dve, osum_done, 0, head, 1)
                dve.reciprocal(orec[:, k, :], osum[:, k, :, GD]).then_inc(orec_done.sem, 1)
                need(dve, orec_done, 0, head, 1)
                dve.tensor_tensor(o_all[:, bass.ds(head * (NT * GD), NT * GD)].rearrange("p (t d) -> p t d", d=GD),
                                  osum[:, k, :, 0:GD], orec[:, k, :].unsqueeze(2).broadcast_to([P, NT, GD]),
                                  ALU.mult).then_inc(o_done.sem, 1)
            head_steps(dve, head_step)

            with dve.Fori(0, NT // 2) as i:
                for u in range(2):
                    dve.wait_ge(w_tps, 2 * i + u + 1)
                    dve.wait_ge(o_done.sem, o_done.at(0, HEADS, 0))
                    dve.tensor_scalar(t1[:, u, 0:CW].rearrange("p (b h d) -> p b h d", b=B, d=GD),
                                      o_all.rearrange("p (b h t d) -> p b h t d", b=B, h=GH, d=GD)[:, :, :, bass.ds(2 * i + u, 1), :].rearrange("p b h o d -> p b h (o d)"),
                                      1.0, None, ALU.mult).then_inc(w_stage, 1)
                for u in range(2):
                    dve.wait_ge(w_ps, 2 * i + u + 1)
                    xv = xT[:, :, bass.ds((2 * i + u) * P, P)]
                    dve.tensor_tensor(xv, xv, ps_s[:, u, :].rearrange("p (b t) -> p b t", b=B), ALU.add).then_inc(w_done, 1)
            dve.wait_ge(w_done, NT + 2)
            for y in (y_att, y_mid):
                dve.memset(y[:, :, 0:1], 0.0).then_inc(zero_done, 1)
            dve.wait_ge(zero_done, 3)
            norm(2, xf, y_in, 1, S + 1)
            steps(dve, step, DEPTH)
            with dve.Fori(0, NT // 2) as i:
                for u in range(2):
                    dve.wait_ge(o_ps, 2 * i + u + 1)
                    dve.tensor_scalar(prT[:, u, 0:B, :], xT[:, :, bass.ds((2 * i + u) * P, P)], 1.0, None, ALU.mult).then_inc(o_stage, 1)

        @block.scalar
        def _(act):
            for c in credits["scalar"]:
                act.sem_inc(c.sem, 1)
            act.sem_inc(xt_sb, 2)
            act.sem_inc(o_sb, 2)
            act.wait_ge(memsets, N_MEMSET)
            with act.Fori(0, NT // 2) as i:
                for u in range(2):
                    act.wait_ge(xt_ps, 2 * i + u + 3)
                    act.activation(xT[:, :, bass.ds((2 * i + u) * P, P)], ps_qk[:, u, :].rearrange("p (b t) -> p b t", b=B),
                                   ACT.Copy).then_inc(xt_sb, 1)

            def norm(k):
                base = 1 + k * BLOCKS
                with act.Fori(0, BLOCKS // 2) as i:
                    for u in range(2):
                        act.wait_ge(n_cen, base + 2 * i + u + 1)
                        act.activation(t1[:, u, 0:CW], qkn[:, u, 0:CW], ACT.Square).then_inc(n_sq, 1)
                    for u in range(2):
                        act.wait_ge(n_var, k * BLOCKS + 2 * i + u + 1)
                        act.wait_ge(n_out, base + 2 * i)
                        act.activation(sqk[:, u * CW:(u + 1) * CW], ps_s[:, u, :], ACT.Ln, bias=consts[:, 0:1]).then_inc(n_log, 1)
                        act.wait_ge(n_log, k * BLOCKS + 2 * i + u + 1)
                        act.activation(t2[:, u, 0:CW], sqk[:, u * CW:(u + 1) * CW], ACT.Exp, scale=-0.5).then_inc(n_rstd, 1)

            def step(att, mlp):
                for s in range(B + 2):
                    if att is not None and s < B:
                        lay, n = att
                        u = s % 2
                        need(act, qk_ps, lay, n, s + 1)
                        need(act, ss_red, lay, n, s)
                        act.activation(sqk[:], ps_qk[:].rearrange("p a c -> p (a c)"), ACT.Square).then_inc(sq_done.sem, 1)
                    if mlp is not None and s == 3:
                        lay, m = mlp
                        need(act, var_ps, lay, m, 1)
                        act.activation(hq[:], psm[:], ACT.Ln, bias=consts[:, 0:1]).then_inc(lnv_done.sem, 1)
                        need(act, lnv_done, lay, m, 1)
                        act.activation(rstd[:], hq[:], ACT.Exp, scale=-0.5).then_inc(rstd_done.sem, 1)
                    if att is not None and s < B:
                        lay, n = att
                        need(act, v_ps, lay, n, s + 1)
                        need(act, v_lo[s], lay, n, 1)
                        need(act, ring_ps, lay, n, ring_at["pv1", s] + 1 - 24)
                        act.activation(vown[:, s, :], psm[:], ACT.Copy).then_inc(v_sb.sem, 1)
                        need(act, ss_lift, lay, n, 2 * s + 2)
                        act.activation(ss[:, u, 3, :], ss[:, u, 1, :], ACT.Ln).then_inc(rn_log.sem, 1)
                        need(act, rn_log, lay, n, s + 1)
                        act.activation(ss[:, u, 2, :], ss[:, u, 3, :], ACT.Exp, scale=-0.5, bias=consts[:, 1:2]).then_inc(rn_guess.sem, 1)
                    if mlp is not None and s == 2:
                        lay, m = mlp
                        need(act, hc_done, lay, m, 1)
                        act.activation(hq[:], hc[:], ACT.Square).then_inc(hq_done.sem, 1)
                    if att is not None and 1 <= s <= B:
                        lay, n = att
                        b = s - 1
                        u = b % 2
                        r = ring_at["q", b]
                        need(act, ring_ps, lay, n, r + 1)
                        need(act, s_ps, lay, n, b - 1)
                        for h in range(2):
                            last = act.activation(
                                qbd[h * 64:(h + 1) * 64, u, :, :, h * 64:(h + 1) * 64].rearrange("p j w q -> p (j w) q"),
                                psr[h * 64:(h + 1) * 64, r % 3, :].rearrange("p (j q) -> p j q", q=64), ACT.Copy)
                        last.then_inc(ring_free.sem, 1)
                        r = ring_at["k", b]
                        need(act, ring_ps, lay, n, r + 1)
                        need(act, k_carry, lay, n, b + 1)
                        act.activation(kT[:, b, :, WIN:WIN + P], psr[:, r % 3, :].rearrange("p (j t) -> p j t", j=PAIRS),
                                       ACT.Copy).then_inc(ring_free.sem, 1)
                        need(act, max_done, lay, n, s)
                        need(act, ring_ps, lay, n, ring_at["pt1", b - 2] + 1 if b >= 2 else ring_at["pt1", b + 2] + 1 - 24)
                        need(act, rsum_done, lay, n, b - 1)
                        for j in range(UNITS):
                            last = act.activation(pr[:, u, j, :], ps_s[:, j // 4, (j % 4) * P:(j % 4 + 1) * P], ACT.Exp,
                                                  bias=nmax[:, u, j:j + 1], accum_out=psum_e[:, u, 0, j:j + 1])
                        last.then_inc(exp_done.sem, 1)
                    if mlp is not None and s == 4:
                        lay, m = mlp
                        for j in range(CH):
                            need(act, g_ps, lay, m, j + 1)
                            act.activation(gel[0:CHN[j], j, :], psm[0:CHN[j], :], ACT.Gelu,
                                           bias=cols_s[0:CHN[j], 3 + j:4 + j]).then_inc(gelu_done.sem, 1)
                    if att is not None and s >= 2:
                        lay, n = att
                        b = s - 2
                        u = b % 2
                        for h in range(2):
                            r = ring_at[f"pt{h}", b]
                            need(act, ring_ps, lay, n, r + 1)
                            if h == 0:
                                need(act, ring_ps, lay, n, ring_at["pv1", b - 2] + 1 if b >= 2 else ring_at["pv1", b + 2] + 1 - 24)
                            act.activation(prT[:, u, 4 * h:4 * h + 4, :].rearrange("p u q -> p (u q)"), psr[:, r % 3, :],
                                           ACT.Copy).then_inc(ring_free.sem, 1)
                        need(act, wo_ps, lay, n, 0)
                        for h in range(2):
                            r = ring_at[f"pv{h}", b]
                            need(act, ring_ps, lay, n, r + 1)
                            for i in range(2):
                                last = act.activation(
                                    oT[i * 64:(i + 1) * 64, 2 * h:2 * h + 2, b, :].rearrange("p j (w q) -> p j w q", w=2),
                                    psr[i * 64:(i + 1) * 64, r % 3, :].rearrange("p (j w q) -> p j w q", j=2, w=2)[:, :, :, i * 64:(i + 1) * 64],
                                    ACT.Copy)
                            last.then_inc(ring_free.sem, 1)

            norm(0)
            steps(act, step, 0)
            norm(1)
            with act.Fori(0, B) as b:
                for u in range(2):
                    v3 = lambda t: t[:, u, :].rearrange("p (a t) -> p a t", a=2)
                    act.wait_ge(gsum, 2 * b + u + 2)
                    act.activation(parts[u][:, :, 0, :], v3(t1), ACT.Copy).then_inc(gp1, 1)
                    act.wait_ge(gr1, 2 * b + u + 1)
                    act.activation(parts[u][:, :, 1, :], v3(t2), ACT.Copy).then_inc(gp2, 1)
            act.wait_ge(gp3, 2 * B)

            def head_step(i, u):
                for kind, head, c, bank in ring2(i, u):
                    if kind == "fin":
                        continue
                    n = S - c * P
                    need(act, p2_ps, 0, head, c + 1)
                    if live(head, 1):
                        need(act, pv_ps, 0, head - 1, 1 + c // 4)
                    act.activation(pT[c], (ps_qk, ps_s)[bank][:].rearrange("p a q -> p (a q)")[:, 0:n], ACT.Exp,
                                   scale=float(GD) ** -0.5).then_inc(p2_exp.sem, 1)
                if live(i, 2):
                    need(act, pv_ps, 0, i - 2, 2)
                    need(act, fin_ps, 0, i - 2, 0)
                    act.activation(acc_sb[:].rearrange("p (a q) -> p a q", a=2), acc, ACT.Copy).then_inc(acc_done.sem, 1)
            head_steps(act, head_step)

            with act.Fori(0, NT // 2) as i:
                for u in range(2):
                    act.wait_ge(w_tps, 2 * i + u + 3)
                    act.activation(t2[:, u, 0:CW], ps_qk[:, u, :], ACT.Copy).then_inc(w_tsb, 1)
            act.wait_ge(w_done, NT + 2)
            norm(2)
            steps(act, step, DEPTH)
            with act.Fori(0, NT // 2) as i:
                for u in range(2):
                    act.wait_ge(o_ps, 2 * i + u + 3)
                    act.wait_ge(o_out[u], 16 * i + 16)
                    act.activation(pr[:, u, 0:B, :].rearrange("p b t -> p (b t)"), ps_qk[:, u, :], ACT.Copy).then_inc(o_sb, 1)

        @block.gpsimd
        def _(pool):
            for c in credits["gpsimd"]:
                pool.sem_inc(c.sem, 1)
            pool.sem_inc(xt_ps, 2)
            pool.sem_inc(o_ps, 2)
            for c in (gv_ps, gv_sb, w_tps, w_tsb, w_done):
                pool.sem_inc(c, 2)
            for c in (grot, gsum):
                pool.sem_inc(c, 1)
            for u in range(2):
                pool.sem_inc(gparts_out[u], 96)
            for u in range(2):
                pool.sem_inc(o_out[u], 16)

            def step(att, mlp):
                if att is None:
                    return
                lay, n = att
                for s in range(B + 1):
                    if s < B:
                        u = s % 2
                        need(pool, qkn_done, lay, n, s + 1)
                        need(pool, rot_done, lay, n, s - 1)
                        need(pool, tab_scaled, lay, n, 2)
                        for a in range(2):
                            src = qkn[:, u, :].rearrange("p (a h d) -> p a h d", a=2, d=FD)[:, :, :, (1 - a) * 32:(2 - a) * 32]
                            dst = t2[:, u, :].rearrange("p (a h d) -> p a h d", a=2, d=FD)[:, :, :, a * 32:(a + 1) * 32]
                            tab = rope_n[:, 1, :, a * 32:(a + 1) * 32].unsqueeze(2).broadcast_to([P, 2, FH, 32])
                            pool.tensor_tensor(dst, src, tab, ALU.mult).then_inc(t2_done.sem, 1)
                    if s >= 1:
                        u = (s - 1) % 2
                        need(pool, rsum_done, lay, n, s)
                        pool.tensor_tensor(pr[:, u, :, :], pr[:, u, :, :],
                                           psum_e[:, u, 1, :].unsqueeze(2).broadcast_to([P, UNITS, P]),
                                           ALU.mult).then_inc(p_norm.sem, 1)
            steps(pool, step, 0)
            steps(pool, step, DEPTH)


def rope_tables():
    half = np.arange(0, FD, 2, dtype=np.float32)
    inv = (1.0 / 10000.0 ** (half / FD)).astype(np.float32)
    t = np.arange(S, dtype=np.float32)
    freqs = (t[:, None] * inv[None, :]).astype(np.float32)
    base = ((half + 0.4 * FD) / (1.4 * FD)).astype(np.float32)
    power = ((t - S // 2) / float(WIN // 2)).astype(np.float32)
    scale = (base[None, :] ** power[:, None]).astype(np.float32)
    cos, sin = np.cos(freqs), np.sin(freqs)
    both = lambda a, b: np.stack([np.concatenate([a * scale * 8.0, b * scale * 8.0], 1),
                                  np.concatenate([a / scale, b / scale], 1)], 1)
    lay = lambda a: np.ascontiguousarray(a.astype(np.float32).reshape(NT, P, 2, FD).transpose(1, 0, 2, 3))
    return lay(both(cos, cos)), lay(both(-sin, sin))


def global_rope():
    half = GD // 2
    inv = (1.0 / 10000.0 ** (np.arange(half, dtype=np.float32) / half)).astype(np.float32)
    ang = (np.arange(S, dtype=np.float32)[:, None] * inv[None, :]).astype(np.float32)
    cos, sin = np.cos(ang).T, np.sin(ang).T
    tile = lambda a: np.ascontiguousarray(np.tile(a, (GH, 1)).astype(np.float32))
    return tile(np.concatenate([cos, cos])), tile(np.concatenate([-sin, sin]))


def band_mask():
    q = np.arange(P)[:, None, None] % WIN
    w = np.arange(2 * NT)[None, :, None]
    c = np.arange(P)[None, None, :]
    seen = (c >= q) & (c <= q + WIN) & ((w > 0) | (c >= WIN))
    return np.where(seen, 0.0, -1e30).astype(np.float32)


def kernel(L0_attn_x, L0_attn_Wq, L0_attn_Wk, L0_attn_Wv, L0_attn_Wo, L0_ffn_wqkv, L0_ffn_q_scale, L0_ffn_k_scale,
           L0_ffn_wo, L0_ffn_ln_g, L0_ffn_ln_b, L0_ffn_w1, L0_ffn_b1, L0_ffn_w2, L0_ffn_b2):
    import ml_dtypes
    import concourse.bacc as bacc
    from concourse.bass_utils import run_bass_kernel_spmd

    f = lambda a: np.ascontiguousarray(np.asarray(a))
    cols = np.zeros((DEPTH, P, 9), np.float32)
    for j in range(CH):
        cols[:, :CHN[j], j] = f(L0_ffn_b1)[:, j * P:j * P + CHN[j]]
        cols[:, :CHN[j], 3 + j] = f(L0_ffn_b1)[:, HID + j * P:HID + j * P + CHN[j]]
    cols[:, :, 6], cols[:, :, 7], cols[:, :, 8] = f(L0_ffn_ln_g), f(L0_ffn_ln_b), f(L0_ffn_b2)
    qk = np.stack([f(L0_ffn_q_scale), f(L0_ffn_k_scale)], 1)
    swapped = np.concatenate([qk[:, :, FD // 2:], qk[:, :, :FD // 2]], 2)
    qkscale = f(np.broadcast_to(np.stack([qk, swapped], 1)[:, None], (DEPTH, P, 2, 2, FD)))
    rope_cos, rope_sin = rope_tables()
    arrays = {
        "x": f(L0_attn_x), "wqkv": f(L0_ffn_wqkv), "qkscale": qkscale, "wo": f(L0_ffn_wo), "w1": f(L0_ffn_w1),
        "w2": f(L0_ffn_w2), "cols": cols, "rope_cos": rope_cos, "rope_sin": rope_sin,
        "bandmask": band_mask().astype(ml_dtypes.bfloat16), "identb_d": np.eye(P).astype(ml_dtypes.bfloat16),
        "identf_d": np.eye(P, dtype=np.float32),
    }
    Wq, Wk = f(L0_attn_Wq), f(L0_attn_Wk)
    swap = np.arange(P).reshape(GH, 2, GD // 2)[:, ::-1].reshape(-1)
    arrays["gw"] = np.stack([f(w.T) for w in (Wq, Wk, Wq[swap], Wk[swap], f(L0_attn_Wv), f(L0_attn_Wo))])
    arrays["g_cos"], arrays["g_sin"] = global_rope()
    q, k = np.arange(P)[:, None], np.arange(P)[None, :]
    arrays["causal"] = np.where(np.stack([k > q, q > k], 1), -1e30, 0.0).astype(ml_dtypes.bfloat16)
    tail = np.zeros((2, STACK - 9 * GD, S), ml_dtypes.bfloat16)
    tail[0, 0:3] = 1
    arrays["stack_tail"] = tail
    nc = bacc.Bacc("TRN2", target_bir_lowering=False, num_devices=1)
    args = {k: nc.dram_tensor(k, a.shape, mybir.dt.from_np(a.dtype), kind="ExternalInput").ap() for k, a in arrays.items()}
    args["out"] = nc.dram_tensor("out", (B, S, P), F32, kind="ExternalOutput").ap()
    program(nc, **args)
    r = run_bass_kernel_spmd(nc, [arrays], core_ids=[0])
    return r.results[0]["out"]
```

```python
from contextlib import ExitStack

import numpy as np

import concourse.bass as bass
from concourse import mybir

F32 = mybir.dt.float32
BF16 = mybir.dt.bfloat16
I32 = mybir.dt.int32
ALU = mybir.AluOpType
ACT = mybir.ActivationFunctionType
AX = mybir.AxisListType.X

P = 128
B, S = 4, 1024
NT = S // P
TOK = B * S
FH, FD = 8, 64
INNER = FH * FD
PAIRS = FH // 2
WIN = 64
UNITS = 2 * PAIRS
DEPTH = 2
HID = 341
CH = 3
CHN = [min(P, HID - P * j) for j in range(CH)]
GH, GD = 16, 8
STACK = 96
LN_EPS = 1e-5
ROOT_BITS = 0x5f3759df
BLOCKS = 8
CW = TOK // BLOCKS
HEADS = B * GH
TURN = 4
CHUNKS = [(i, c) for i in range(NT) for c in range(1 + i // 4)]
VW = GD + 1


class Count:

    def __init__(self, sem, per, by=1, first=1):
        self.sem, self.per, self.by, self.first = sem, per, by, first

    def at(self, layer, n, c):
        return (layer * NT + n) * (self.per * self.by) + (self.first + c * self.by)


def need(eng, count, layer, n, c):
    v = count.at(layer, n, c)
    if not isinstance(v, int) or v > count.first:
        eng.wait_ge(count.sem, v)


def program(nc, x, wqkv, qkscale, wo, w1, w2, cols, rope_cos, rope_sin, bandmask, identb_d, identf_d,
            gw, g_cos, g_sin, causal, stack_tail, out):
    ctx = ExitStack()
    with ctx:
        def sb(name, shape, dt=F32):
            return ctx.enter_context(nc.sbuf_tensor(name, shape, dt))

        def sem(name):
            return ctx.enter_context(nc.semaphore(name))

        xT = sb("xT", [P, B, S])
        y_in = sb("y_in", [P, B, S + 1])
        y_att = sb("y_att", [P, B, S + 1])
        y_mid = sb("y_mid", [P, B, S + 1])
        identf = sb("identf", [P, P])
        identb = sb("identb", [P, P], BF16)
        ones = sb("ones", [P, P])
        mask = sb("mask", [P, 2 * NT, P], BF16)
        ropec = sb("ropec", [P, NT, 2, FD])
        ropes = sb("ropes", [P, NT, 2, FD])
        eps = sb("eps", [P, 1])
        wqkv_s = sb("wqkv_s", [P, 3 * INNER])
        wo_s = sb("wo_s", [P, PAIRS, P])
        w1_s = sb("w1_s", [P, 2 * HID])
        w2_s = sb("w2_s", [P, CH, P])
        cols_s = sb("cols_s", [P, 9])
        rope_n = sb("rope_n", [P, 2, 2, FD])
        scl = sb("scl", [P, 2, 2, FD])
        hs = sb("hs", [P, B, P])
        sqk = sb("sqk", [P, 2 * INNER])
        ss = sb("ss", [P, 2 * FH])
        ssc = sb("ssc", [P, 2 * FH])
        rn = sb("rn", [P, 4, 2 * FH])
        nw = sb("nw", [P, 2, 2 * FH])
        qkn = sb("qkn", [P, 2, 2 * INNER])
        t1 = sb("t1", [P, 2, 2 * INNER])
        t2 = sb("t2", [P, 2, 2 * INNER])
        qbd = sb("qbd", [P, 2, PAIRS, 2, P])
        kT = sb("kT", [P, B, PAIRS, WIN + P])
        vown = sb("vown", [P, B, INNER])
        vprev = sb("vprev", [P, B, INNER])
        nmax = sb("nmax", [P, 2, UNITS])
        psum_e = sb("psum_e", [P, 2, 2, UNITS])
        pr = sb("pr", [P, 2, UNITS, P])
        prT = sb("prT", [P, 2, UNITS, P])
        oT = sb("oT", [P, PAIRS, B, P])
        h1 = sb("h1", [P, CW])
        hc = sb("hc", [P, CW])
        hq = sb("hq", [P, CW])
        rstd = sb("rstd", [P, CW])
        hn = sb("hn", [P, CW])
        gel = sb("gel", [P, CH, CW])
        act_t = sb("act_t", [P, CH, CW])
        ps = [ctx.enter_context(nc.psum_tensor(f"ps{i}", [P, 2, 512], F32)) for i in range(2)]
        psr = ctx.enter_context(nc.psum_tensor("psr", [P, 4, 512], F32))
        psm = psr[:, 3, :]
        ps_qk, ps_s = ps

        gw_s = wqkv_s[:, 0:6 * P].rearrange("p (w n) -> p w n", w=6)
        gcos = gel[:].rearrange("p a b -> p (a b)")[:, 0:S]
        gsin = act_t[:].rearrange("p a b -> p (a b)")[:, 0:S]
        zs = [hs[:].rearrange("p b t -> p (b t)"), h1[:]]
        parts = [t[:].rearrange("p a u k -> p (a u k)").bitcast(BF16)[:, 0:6 * CW].rearrange("p (a j t) -> p a j t", a=2, j=3)
                 for t in (pr, prT)]
        kst, qst = [t[:].rearrange("p a u k -> p (a u k)").bitcast(BF16).rearrange("p (u t) -> p u t", u=TURN)
                    for t in (pr, prT)]
        v_all = y_att[:].rearrange("p b t -> p (b t)")[:, 4:4 + TOK]
        o_all = y_mid[:].rearrange("p b t -> p (b t)")[:, 4:4 + TOK]
        pT = [t1[:, 0, :], t1[:, 1, 0:896], t2[:, 0, 0:768], t2[:, 1, 0:640],
              qkn[:, 0, 0:512], qkn[:, 0, 512:896], qkn[:, 1, 0:256], qkn[:, 1, 256:384]]
        acc = psr[:, 2:4, :]
        acc_sb = sqk
        causal_s = sb("causal_s", [P, 2, P], BF16)
        vh = sb("vh", [P, 2, NT, VW])
        nm = sb("nm", [P, 2, 2, NT])
        nres = sb("nres", [P, 2, NT])
        nparts = sb("nparts", [P, 2, 3, NT], BF16)
        nT = sb("nT", [3 * NT, 2, P], BF16)
        osum = sb("osum", [P, 2, NT, VW])
        orec = sb("orec", [P, 2, NT])
        scratch = nc.dram_tensor("scratch", (2, HEADS, 3, GD, S), BF16, kind="Internal").ap()

        one = lambda name, per: Count(sem(name), per)
        hs_ready = one("hs_ready", 2)
        tab_scaled = one("tab_scaled", 2)
        qk_ps = one("qk_ps", 4)
        v_ps = one("v_ps", 4)
        sq_done = one("sq_done", 4)
        ss_red = one("ss_red", 4)
        ss_clamp = one("ss_clamp", 4)
        rn_guess = one("rn_guess", 4)
        rn_step = one("rn_step", 9 * B)
        qkn_done = one("qkn_done", 4)
        t1_done = one("t1_done", 4)
        t2_done = one("t2_done", 8)
        rot_done = one("rot_done", 4)
        qkt_ps = one("qkt_ps", 2 * B)
        qkt_sb = one("qkt_sb", 2 * B)
        pt_ps = one("pt_ps", 2 * B)
        pt_sb = one("pt_sb", 2 * B)
        o2_ps = one("o2_ps", 2 * B)
        o2_sb = one("o2_sb", 2 * B)
        k_carry = one("k_carry", 4)
        v_sb = one("v_sb", 4)
        s_ps = one("s_ps", 4)
        max_done = one("max_done", 4)
        exp_done = one("exp_done", 4)
        rsum_done = one("rsum_done", 4)
        p_norm = one("p_norm", 4)
        wo_ps = one("wo_ps", 1)
        y1_done = one("y1_done", 1)
        h1_done = one("h1_done", 2)
        mean_ps = one("mean_ps", 1)
        hc_done = one("hc_done", 1)
        hq_done = one("hq_done", 1)
        var_ps = one("var_ps", 1)
        lnv_done = one("lnv_done", 1)
        rstd_done = one("rstd_done", 1)
        hn_done = one("hn_done", 2)
        g_ps = one("g_ps", CH)
        gelu_done = one("gelu_done", CH)
        a_ps = one("a_ps", CH)
        glu_done = one("glu_done", CH)
        w2_ps = one("w2_ps", 1)
        yo_done = one("yo_done", 2)
        v_lo = [Count(sem(f"v_lo{b}"), 1, 16, 0) for b in range(B)]
        v_hi = [Count(sem(f"v_hi{b}"), 1, 16, 0) for b in range(B)]
        scl_in = sem("scl_in")
        wqkv_in = sem("wqkv_in")
        wo_in = sem("wo_in")
        w1_in = sem("w1_in")
        w2_in = sem("w2_in")
        const_in = sem("const_in")
        memsets = sem("memsets")
        x_in = [sem(f"x_in{i}") for i in range(2)]
        xt_ps = sem("xt_ps")
        xt_sb = sem("xt_sb")
        n_mean = sem("n_mean")
        n_cen = sem("n_cen")
        n_sq = sem("n_sq")
        n_var = sem("n_var")
        n_log = sem("n_log")
        n_rstd = sem("n_rstd")
        n_out = sem("n_out")
        o_stage = sem("o_stage")
        o_ps = sem("o_ps")
        o_sb = sem("o_sb")
        o_out = [sem(f"o_out{i}") for i in range(2)]
        N_MEMSET = 12
        gw_in = sem("gw_in")
        gz_done = sem("gz_done")
        gqk_ps = sem("gqk_ps")
        gv_ps = sem("gv_ps")
        gv_sb = sem("gv_sb")
        grot = sem("grot")
        gsum = sem("gsum")
        gp1 = sem("gp1")
        gr1 = sem("gr1")
        gp2 = sem("gp2")
        gp3 = sem("gp3")
        gparts_out = [sem(f"gparts_out{u}") for u in range(2)]
        st_in = [sem(f"st_in{u}") for u in range(TURN)]
        tail_in = sem("tail_in")
        p1_ps = one("p1_ps", len(CHUNKS))
        p1_max = one("p1_max", len(CHUNKS))
        nm_done = one("nm_done", 1)
        n1_done = one("n1_done", 1)
        r1_done = one("r1_done", 1)
        n2_done = one("n2_done", 1)
        n3_done = one("n3_done", 1)
        nT_ps = one("nT_ps", 1)
        nT_sb = one("nT_sb", 1)
        nT_in = [sem(f"nT_in{u}") for u in range(TURN)]
        p2_ps = one("p2_ps", NT)
        p2_exp = one("p2_exp", NT)
        vh_done = one("vh_done", 1)
        pv_ps = one("pv_ps", 2)
        acc_done = one("acc_done", 1)
        fin_ps = one("fin_ps", 1)
        osum_done = one("osum_done", 1)
        orec_done = one("orec_done", 1)
        o_done = one("o_done", 1)
        w_stage = sem("w_stage")
        w_tps = sem("w_tps")
        w_tsb = sem("w_tsb")
        w_ps = sem("w_ps")
        w_done = sem("w_done")
        zero_done = sem("zero_done")

        credits = {
            "vector": [hs_ready, tab_scaled, ss_red, ss_clamp, rn_guess, rn_step, qkn_done, t1_done, rot_done, k_carry, max_done,
                       rsum_done, y1_done, h1_done, hc_done, hn_done, glu_done, yo_done, p1_max, nm_done, n1_done,
                       r1_done, n2_done, n3_done, nT_sb, vh_done, osum_done, orec_done, o_done],
            "scalar": [sq_done, qkt_sb, pt_sb, o2_sb, v_sb, exp_done, hq_done, lnv_done, rstd_done,
                       gelu_done, p2_exp, acc_done],
            "tensor": [qk_ps, v_ps, qkt_ps, pt_ps, o2_ps, s_ps, wo_ps, mean_ps, var_ps, g_ps, a_ps, w2_ps,
                       p1_ps, nT_ps, p2_ps, pv_ps, fin_ps],
            "gpsimd": [t2_done, p_norm],
        }

        def steps(eng, step, layer0):
            for lay in range(layer0, layer0 + DEPTH):
                for n in range(2):
                    step((layer0, lay, n))
                with eng.Fori(2, NT) as n:
                    step((layer0, lay, n))
            for n in range(2):
                step((layer0, layer0 + DEPTH, n))

        def back(cur, d):
            layer0, lay, n = cur
            if not isinstance(n, int):
                return lay, n - d
            t = (lay - layer0) * NT + n - d
            return (layer0 + t // NT, t % NT) if 0 <= t < DEPTH * NT else None

        def item(cur, s, lag):
            return (back(cur, 0), s - lag) if s >= lag else (back(cur, 1), s - lag + B)

        def head_steps(eng, step):
            for i in range(TURN):
                step(i, i)
            with eng.Fori(1, HEADS // TURN) as g:
                for u in range(TURN):
                    step(g * TURN + u, u)
            for u in range(3):
                step(HEADS + u, u)

        def live(i, back):
            return not isinstance(i, int) or back <= i < HEADS + back

        def ring1(i, u):
            jobs = [("max", i, c) for c in range(len(CHUNKS))] if live(i, 0) else []
            if live(i, 1):
                jobs.insert(2, ("nT", i - 1, 0))
            first = (u + 1) % 2 if not isinstance(i, int) or i else 0
            return [(*job, (first + n) % 2) for n, job in enumerate(jobs)]

        def ring1_free(eng, i, jobs, n):
            if n < 2:
                kind, head, c = "max", i - 1, len(CHUNKS) - 2 + n
                if isinstance(head, int) and head < 0:
                    return
            else:
                kind, head, c, _ = jobs[n - 2]
            need(eng, p1_max if kind == "max" else nT_sb, 0, head, c + 1)

        def ring2(i, u):
            jobs = [("fin", i - 3, 0)] if live(i, 3) else []
            if live(i, 2):
                jobs += [("exp", i - 2, kt) for kt in range(NT)]
            first = (u + 1) % 2 if not isinstance(i, int) or i > 2 else 0
            return [(*job, (first + n) % 2) for n, job in enumerate(jobs)]

        def ring2_free(eng, i, jobs, n):
            if n < 2:
                kind, head, c = "exp", i - 3, NT - 2 + n
                if isinstance(head, int) and head < 0:
                    return
            else:
                kind, head, c, _ = jobs[n - 2]
            need(eng, p2_exp if kind == "exp" else osum_done, 0, head, c + 1)

        RING = [(s, kind, i) for s in range(B) for kind, i in (("qkt", 0), ("qkt", 1), ("pt", 0), ("pt", 1), ("o2", 0), ("o2", 1))]
        RING_LAG = {"qkt": 1, "pt": 2, "o2": 2}
        RING_FREE = {"qkt": qkt_sb, "pt": pt_sb, "o2": o2_sb}

        def bank_of(s, kind, i):
            return RING.index((s, kind, i)) % 3

        def ring_free(eng, cur, s, kind, i):
            at = RING.index((s, kind, i))
            for places in range(3, 3 * len(RING), 3):
                gone, j = divmod(len(RING) - 1 - at + places, len(RING))
                slot, kind_j, i_j = RING[len(RING) - 1 - j]
                lag = RING_LAG[kind_j]
                tile = back(cur, gone + (slot < lag))
                if tile is not None:
                    need(eng, RING_FREE[kind_j], *tile, 2 * ((slot - lag) % B) + i_j + 1)
                    return

        SHARED = [("g", 0, 2, gelu_done), ("v", 0, 0, v_sb), ("g", 1, 2, gelu_done), ("g", 2, 2, gelu_done),
                  ("v", 1, 0, v_sb), ("a", 0, 2, glu_done), ("a", 1, 2, glu_done), ("a", 2, 2, glu_done),
                  ("w2", 0, 2, yo_done),
                  ("v", 2, 0, v_sb), ("wo", 0, 1, y1_done), ("mean", 0, 1, hc_done),
                  ("v", 3, 0, v_sb), ("var", 0, 1, lnv_done)]

        def shared_free(eng, cur, name, number=0):
            at = [job[:2] for job in SHARED].index((name, number))
            for places in range(1, 3 * len(SHARED)):
                gone, j = divmod(len(SHARED) - 1 - at + places, len(SHARED))
                _, number_j, d, frees = SHARED[len(SHARED) - 1 - j]
                tile = back(cur, gone + d)
                if tile is not None:
                    need(eng, frees, *tile, number_j + 1)
                    return

        block = ctx.enter_context(nc.Block())

        def turn_at(i, u, per, first):
            if isinstance(i, int):
                return (i // TURN) * per + first
            return (i - u) * (per // TURN) + first

        @block.sync
        def _(sp):
            sp.dma_start(identf[:], identf_d).then_inc(const_in, 16)
            sp.dma_start(identb[:], identb_d).then_inc(const_in, 16)
            sp.dma_start(mask[:], bandmask).then_inc(const_in, 16)
            sp.dma_start(ropec[:], rope_cos).then_inc(const_in, 16)
            sp.dma_start(ropes[:], rope_sin).then_inc(const_in, 16)
            sp.dma_start(causal_s[:], causal).then_inc(const_in, 16)
            with sp.Fori(0, NT // 2) as i:
                for u in range(2):
                    sp.wait_ge(xt_ps, 2 * i + u + 1)
                    sp.dma_start(prT[:, u, 0:B, :], x[:, bass.ds((2 * i + u) * P, P), :].rearrange("b p d -> p b d")).then_inc(x_in[u], 16)

            def load_attention(lay):
                l = lay % DEPTH
                if lay == DEPTH:
                    sp.wait_ge(w_ps, NT)
                need(sp, v_ps, lay, 0, 0)
                need(sp, qk_ps, lay, 0, 0)
                sp.dma_start(wqkv_s[:], wqkv[l]).then_inc(wqkv_in, 16)
                need(sp, tab_scaled, lay, 0, 0)
                sp.dma_start(scl[:], qkscale[l]).then_inc(scl_in, 16)

            def load_wo(lay):
                need(sp, wo_ps, lay, 0, 0)
                sp.dma_start(wo_s[:], wo[lay % DEPTH].rearrange("(j p) n -> p j n", p=P)).then_inc(wo_in, 16)

            def load_mlp(lay):
                l = lay % DEPTH
                need(sp, a_ps, lay, 0, 0)
                sp.dma_start(w1_s[:], w1[l]).then_inc(w1_in, 16)
                need(sp, w2_ps, lay, 0, 0)
                sp.dma_start(w2_s[:, 0:2, :], w2[l, 0:2 * P, :].rearrange("(j p) n -> p j n", p=P)).then_inc(w2_in, 16)
                sp.dma_start(w2_s[0:CHN[2], 2, :], w2[l, 2 * P:HID, :]).then_inc(w2_in, 16)
                need(sp, yo_done, lay, 0, 0)
                sp.dma_start(cols_s[:], cols[l]).then_inc(w2_in, 16)

            def step(cur):
                layer0, lay, n = cur
                if lay > layer0 and lay < layer0 + DEPTH and isinstance(n, int) and n == 0:
                    load_attention(lay)
                for s in range(B):
                    if back(cur, 0) is not None:
                        tile = back(cur, 0)
                        need(sp, v_sb, *tile, s + 1)
                        sp.dma_start(vprev[WIN:P, s, :], vown[0:WIN, s, :]).then_inc(v_hi[s].sem, 16)
                    tile, b = item(cur, s, 2)
                    if tile is not None:
                        need(sp, o2_ps, *tile, 2 * b + 2)
                        sp.dma_start(vprev[0:WIN, b, :], vown[WIN:P, b, :]).then_inc(v_lo[b].sem, 16)
                if lay > layer0 and lay < layer0 + DEPTH and isinstance(n, int):
                    (load_wo, load_mlp)[n](lay)

            sp.wait_ge(memsets, N_MEMSET)
            for b in range(B):
                sp.dma_start(vprev[0:WIN, b, :], vown[WIN:P, b, :]).then_inc(v_lo[b].sem, 16)
            load_attention(0)
            load_wo(0)
            load_mlp(0)
            steps(sp, step, 0)

            need(sp, v_ps, DEPTH, 0, 0)
            need(sp, yo_done, DEPTH, 0, 0)
            sp.dma_start(gw_s, gw.rearrange("w p n -> p w n")).then_inc(gw_in, 16)
            sp.dma_start(gcos, g_cos).then_inc(gw_in, 16)
            sp.dma_start(gsin, g_sin).then_inc(gw_in, 16)
            with sp.Fori(0, B) as b:
                for u in range(2):
                    sp.wait_ge(gp1, 2 * b + u + 1)
                    sp.wait_ge(gp2, 2 * b + u + 1)
                    sp.wait_ge(gp3, 2 * b + u + 1)
                    for a in range(2):
                        for j in range(3):
                            sp.dma_start(scratch[a, bass.ds(b * GH, GH), j, :, u * CW:(u + 1) * CW],
                                         parts[u][:, a, j, :]).then_inc(gparts_out[u], 16)
            for u in range(2):
                sp.wait_ge(gparts_out[u], 96 * (B + 1))
            for u in range(TURN):
                sp.dma_start(kst[3 * 3 * GD:STACK, u, :], stack_tail[0]).then_inc(tail_in, 16)

            def load_stacks(i, u):
                need(sp, pv_ps, 0, i - TURN + 1, 0) if live(i, TURN) else None
                src = scratch[0, bass.ds(i, 1), :, :, :].rearrange("o j d t -> (o j d) t").unsqueeze(0)
                sp.dma_start(qst[0:9 * GD, u, :], src.broadcast_to([3, 3 * GD, S])).then_inc(st_in[u], 16)
                sp.dma_start(qst[9 * GD:STACK, u, :], stack_tail[1]).then_inc(st_in[u], 16)
                for j in range(3):
                    sp.dma_start(kst[3 * GD * j:3 * GD * (j + 1), u, :],
                                 scratch[1, bass.ds(i, 1), j, :, :].broadcast_to([3, GD, S])).then_inc(st_in[u], 16)

            def store_max(i, u):
                need(sp, nT_sb, 0, i, 1)
                sp.dma_start(qst[9 * GD:9 * GD + 3, u, :], nT[:, u % 2, :]).then_inc(nT_in[u], 16)

            def head_step(i, u):
                if live(i, 0):
                    load_stacks(i, u)
                if live(i, 2):
                    store_max(i - 2, (u - 2) % TURN)
            for i in range(TURN):
                head_step(i, i)
            with sp.Fori(1, HEADS // TURN) as g:
                for u in range(TURN):
                    head_step(g * TURN + u, u)
            for i in range(HEADS, HEADS + 2):
                head_step(i, i % TURN)

            load_attention(DEPTH)
            load_wo(DEPTH)
            load_mlp(DEPTH)
            steps(sp, step, DEPTH)
            with sp.Fori(0, NT // 2) as i:
                for u in range(2):
                    sp.wait_ge(o_sb, 2 * i + u + 3)
                    sp.dma_start(out[:, bass.ds((2 * i + u) * P, P), :].rearrange("b p d -> p b d"), pr[:, u, 0:B, :]).then_inc(o_out[u], 16)
            for u in range(2):
                sp.wait_ge(o_out[u], 16 * (NT // 2 + 1))

        @block.tensor
        def _(pe):
            for c in credits["tensor"]:
                pe.sem_inc(c.sem, 1)
            pe.wait_ge(const_in, 96)
            pe.wait_ge(memsets, N_MEMSET)
            with pe.Fori(0, NT // 2) as i:
                for u in range(2):
                    pe.wait_ge(x_in[u], 16 * i + 16)
                    pe.wait_ge(xt_sb, 2 * i + u + 1)
                    for b in range(B):
                        last = pe.transpose(ps_qk[:, u, b * P:(b + 1) * P], prT[:, u, b, :], identf[:])
                    last.then_inc(xt_ps, 1)

            def norm(k, src):
                base = 1 + k * BLOCKS
                with pe.Fori(0, BLOCKS // 2) as i:
                    for u in range(2):
                        pe.wait_ge(n_cen, base + 2 * i)
                        pe.matmul(ps_qk[:, u, :], ones[:], src[:, bass.ds((2 * i + u) * CW, CW)],
                                  start=True, stop=True).then_inc(n_mean, 1)
                    for u in range(2):
                        pe.wait_ge(n_sq, k * BLOCKS + 2 * i + u + 1)
                        pe.matmul(ps_s[:, u, :], ones[:], t1[:, u, 0:CW], start=True, stop=True).then_inc(n_var, 1)

            xf = xT[:, :, :].rearrange("p b t -> p (b t)")

            def step(cur):
                tile0, tile1, tile2 = (back(cur, d) for d in range(3))

                def project_v(s):
                    if s == 0:
                        if isinstance(tile0[1], int) and tile0[1] == 0:
                            pe.wait_ge(wqkv_in, 16 * (tile0[0] + 1))
                        need(pe, hs_ready, *tile0, 2)
                    shared_free(pe, cur, "v", s)
                    pe.matmul(psm[:], hs[:, s, :], wqkv_s[:, 2 * INNER:], start=True, stop=True).then_inc(v_ps.sem, 1)

                def project_qk(s):
                    need(pe, qkn_done, *tile0, s)
                    for j in range(2):
                        last = pe.matmul(ps_qk[:, j, :], hs[:, s, :], wqkv_s[:, j * INNER:(j + 1) * INNER],
                                         start=True, stop=True)
                    last.then_inc(qk_ps.sem, 1)

                def turn_qk(s):
                    tile, b = item(cur, s, 1)
                    if tile is None:
                        return
                    need(pe, rot_done, *tile, b + 1)
                    for j in range(2):
                        ring_free(pe, cur, s, "qkt", j)
                        for i in range(PAIRS):
                            last = pe.transpose(psr[:, bank_of(s, "qkt", j), i * P:(i + 1) * P],
                                                t1[:, b % 2, j * INNER + i * P:j * INNER + (i + 1) * P], identf[:])
                        last.then_inc(qkt_ps.sem, 1)

                def scores(s):
                    tile, b = item(cur, s, 1)
                    if tile is None:
                        return
                    need(pe, exp_done, *tile, b)
                    for j in range(PAIRS):
                        pe.matmul(ps_s[:, j // 2, (j % 2) * 2 * P:(j % 2 + 1) * 2 * P], identb[:],
                                  mask[:, bass.ds(2 * tile[1], 2), :], start=(j % 2 == 0), stop=False, skip_group_check=True)
                    need(pe, qkt_sb, *tile, 2 * b + 2)
                    for j in range(PAIRS):
                        for w in range(2):
                            last = pe.matmul(ps_s[:, j // 2, ((j % 2) * 2 + w) * P:((j % 2) * 2 + w + 1) * P],
                                             qbd[:, b % 2, j, w, :], kT[:, b, j, w * WIN:w * WIN + P],
                                             start=False, stop=(j % 2 == 1 and w == 1), skip_group_check=True)
                    last.then_inc(s_ps.sem, 1)

                def turn_probs(s):
                    tile, b = item(cur, s, 2)
                    if tile is None:
                        return
                    need(pe, p_norm, *tile, b + 1)
                    for h in range(2):
                        ring_free(pe, cur, s, "pt", h)
                        for i in range(4):
                            last = pe.transpose(psr[:, bank_of(s, "pt", h), i * P:(i + 1) * P], pr[:, b % 2, 4 * h + i, :],
                                                identf[:])
                        last.then_inc(pt_ps.sem, 1)

                def weigh_values(s):
                    tile, b = item(cur, s, 2)
                    if tile is None:
                        return
                    need(pe, v_lo[b], *tile, 1)
                    need(pe, v_hi[b], *tile, 1)
                    for h in range(2):
                        ring_free(pe, cur, s, "o2", h)
                        need(pe, pt_sb, *tile, 2 * b + h + 1)
                        for i in range(4):
                            u = 4 * h + i
                            v = (vprev, vown)[u % 2]
                            last = pe.matmul(psr[:, bank_of(s, "o2", h), i * P:(i + 1) * P], v[:, b, (u // 2) * P:(u // 2 + 1) * P],
                                             prT[:, b % 2, u, :], start=True, stop=True)
                        last.then_inc(o2_ps.sem, 1)

                def gate(j):
                    if tile2 is None:
                        return
                    if j == 0:
                        pe.wait_ge(w1_in, 16 * (tile2[0] + 1))
                        need(pe, hn_done, *tile2, 2)
                    shared_free(pe, cur, "g", j)
                    pe.matmul(psm[0:CHN[j], :], w1_s[:, HID + j * P:HID + j * P + CHN[j]], hn[:],
                              start=True, stop=True).then_inc(g_ps.sem, 1)

                def linear(j):
                    if tile2 is None:
                        return
                    shared_free(pe, cur, "a", j)
                    pe.matmul(psm[0:CHN[j], :], w1_s[:, j * P:j * P + CHN[j]], hn[:],
                              start=True, stop=True).then_inc(a_ps.sem, 1)

                def out_mlp():
                    if tile2 is None:
                        return
                    pe.wait_ge(w2_in, 48 * (tile2[0] + 1))
                    shared_free(pe, cur, "w2")
                    for j in range(CH):
                        last = pe.matmul(psm[:], w2_s[0:CHN[j], j, :], act_t[0:CHN[j], j, :], start=(j == 0), stop=(j == CH - 1))
                    last.then_inc(w2_ps.sem, 1)

                def out_attention():
                    if tile1 is None:
                        return
                    pe.wait_ge(wo_in, 16 * (tile1[0] + 1))
                    need(pe, o2_sb, *tile1, 2 * B)
                    shared_free(pe, cur, "wo")
                    for j in range(PAIRS):
                        last = pe.matmul(psm[:], wo_s[:, j, :], oT[:, j, :, :], start=(j == 0), stop=(j == PAIRS - 1))
                    last.then_inc(wo_ps.sem, 1)

                def mean():
                    if tile1 is None:
                        return
                    need(pe, h1_done, *tile1, 2)
                    shared_free(pe, cur, "mean")
                    pe.matmul(psm[:], ones[:], h1[:], start=True, stop=True).then_inc(mean_ps.sem, 1)

                def variance():
                    if tile1 is None:
                        return
                    need(pe, hq_done, *tile1, 1)
                    shared_free(pe, cur, "var")
                    pe.matmul(psm[:], ones[:], hq[:], start=True, stop=True).then_inc(var_ps.sem, 1)

                gate(0)
                turn_qk(0)
                if tile0 is not None:
                    project_v(0)
                    project_qk(0)
                gate(1)
                turn_probs(0)
                gate(2)
                scores(0)
                weigh_values(0)
                for s in range(1, B):
                    if tile0 is not None:
                        project_v(s)
                        project_qk(s)
                    if s == 1:
                        linear(0)
                    turn_qk(s)
                    if s == 1:
                        linear(1)
                    if s == 2:
                        out_attention()
                    if s == 3:
                        variance()
                    turn_probs(s)
                    if s == 1:
                        linear(2)
                    scores(s)
                    if s == 1:
                        out_mlp()
                    if s == 2:
                        mean()
                    weigh_values(s)

            pe.wait_ge(xt_sb, NT + 2)
            norm(0, xf)
            steps(pe, step, 0)
            need(pe, yo_done, DEPTH, 0, 0)
            norm(1, xf)

            pe.wait_ge(gw_in, 48)
            with pe.Fori(0, B) as b:
                for u in range(2):
                    pe.wait_ge(gz_done, 2 * b + u + 1)
                    pe.wait_ge(grot, 2 * (2 * b + u) + 1)
                    for j in range(2):
                        pe.matmul(ps_qk[:, j, :], gw_s[:, j, :], zs[u], start=True, stop=True)
                    for j in range(2):
                        last = pe.matmul(ps_s[:, j, :], gw_s[:, 2 + j, :], zs[u], start=True, stop=True)
                    last.then_inc(gqk_ps, 1)
                    pe.wait_ge(gv_sb, 2 * b + u + 1)
                    for i in range(4):
                        last = pe.matmul(psr[:, u, i * P:(i + 1) * P], zs[u][:, i * P:(i + 1) * P], gw_s[:, 4, :],
                                         start=True, stop=True)
                    last.then_inc(gv_ps, 1)

            pe.wait_ge(tail_in, 16 * TURN)
            pe.wait_ge(gv_sb, 2 * B + 2)
            pe.wait_ge(grot, 4 * B + 1)

            def max_job(i, u, c, bank):
                t, half = CHUNKS[c]
                lo, hi = half * 512, min((t + 1) * P, (half + 1) * 512)
                diag = hi == (t + 1) * P
                last = pe.matmul(psr[:, bank, 0:hi - lo], qst[0:STACK, u, t * P:(t + 1) * P], kst[0:STACK, u, lo:hi],
                                 start=True, stop=not diag)
                if diag:
                    last = pe.matmul(psr[:, bank, hi - lo - P:hi - lo], identb[:], causal_s[:, 0, :], start=False, stop=True)
                last.then_inc(p1_ps.sem, 1)

            def exp_job(i, u, kt, bank):
                if kt == 0:
                    pe.wait_ge(nT_in[u], turn_at(i, u, 16, 16))
                where = (ps_qk, ps_s)[bank]
                n = S - kt * P
                for lo in range(0, n, 512):
                    hi = min(n, lo + 512)
                    last = pe.matmul(where[:, lo // 512, 0:hi - lo], kst[0:STACK, u, kt * P:(kt + 1) * P],
                                     qst[0:STACK, u, kt * P + lo:kt * P + hi], start=True, stop=lo > 0)
                    if lo == 0:
                        last = pe.matmul(where[:, 0, 0:P], identb[:], causal_s[:, 1, :], start=False, stop=True)
                last.then_inc(p2_ps.sem, 1)

            def products(i, u, part):
                need(pe, p2_exp, 0, i, 4 * part + 4)
                if part == 0:
                    need(pe, vh_done, 0, i, 1)
                    pe.wait_ge(zero_done, 1)
                    need(pe, acc_done, 0, i, 0)
                for half in range(part, 2):
                    for kt in range(4 * part, 4 * part + 4):
                        lo = max(kt * P, half * 512)
                        c = kt % 4
                        last = pe.matmul(acc[32 * c:32 * c + VW, half, lo - half * 512:512], vh[:, u % 2, kt, :],
                                         pT[kt][:, lo - kt * P:(half + 1) * 512 - kt * P],
                                         start=(part == 0), stop=(part == 1 or half == 0), skip_group_check=True)
                last.then_inc(pv_ps.sem, 1)

            def head_step(i, u):
                jobs1, jobs2 = ring1(i, u), ring2(i, u)
                order = []
                for n in range(max(len(jobs1), len(jobs2) * 3 // 2 + 2)):
                    if n < len(jobs1):
                        order.append((1, n))
                    while len([o for o in order if o[0] == 2]) < min(len(jobs2), (n + 1) * 9 // 13 + (0 if n < len(jobs1) - 1 else len(jobs2))):
                        order.append((2, len([o for o in order if o[0] == 2])))
                if live(i, 0):
                    pe.wait_ge(st_in[u], turn_at(i, u, 80, 80))
                for ring, n in order:
                    if ring == 1:
                        kind, head, c, bank = jobs1[n]
                        ring1_free(pe, i, jobs1, n)
                        if kind == "max":
                            max_job(head, u, c, bank)
                        else:
                            need(pe, n3_done, 0, head, 1)
                            pe.transpose(psr[0:3 * NT, bank, 0:P // 2].bitcast(BF16),
                                         nparts[:, (u - 1) % 2, :, :].rearrange("p j t -> p (j t)"),
                                         identb[:]).then_inc(nT_ps.sem, 1)
                    else:
                        kind, head, c, bank = jobs2[n]
                        ring2_free(pe, i, jobs2, n)
                        if kind == "fin":
                            need(pe, acc_done, 0, head, 1)
                            where = (ps_qk, ps_s)[bank]
                            for t in range(NT):
                                last = pe.transpose(where[:, t // 4, (t % 4) * P:(t % 4 + 1) * P],
                                                    acc_sb[:, t * P:(t + 1) * P], identf[:])
                            last.then_inc(fin_ps.sem, 1)
                        else:
                            exp_job(head, (u - 2) % TURN, c, bank)
                            if c == 5:
                                products(head, (u - 2) % TURN, 0)
                if live(i, 2):
                    products(i - 2, (u - 2) % TURN, 1)
            head_steps(pe, head_step)

            with pe.Fori(0, NT // 2) as i:
                for u in range(2):
                    pe.wait_ge(w_stage, 2 * i + u + 1)
                    pe.wait_ge(w_tsb, 2 * i + u + 1)
                    for b in range(B):
                        last = pe.transpose(ps_qk[:, u, b * P:(b + 1) * P], t1[:, u, b * P:(b + 1) * P], identf[:])
                    last.then_inc(w_tps, 1)
                    pe.wait_ge(w_tsb, 2 * i + u + 3)
                    pe.wait_ge(w_done, 2 * i + u + 1)
                    pe.matmul(ps_s[:, u, :], gw_s[:, 5, :], t2[:, u, 0:CW], start=True, stop=True).then_inc(w_ps, 1)

            pe.wait_ge(w_done, NT + 2)
            norm(2, xf)
            steps(pe, step, DEPTH)
            with pe.Fori(0, NT // 2) as i:
                for u in range(2):
                    pe.wait_ge(o_stage, 2 * i + u + 1)
                    pe.wait_ge(o_sb, 2 * i + u + 1)
                    for b in range(B):
                        last = pe.transpose(ps_qk[:, u, b * P:(b + 1) * P], prT[:, u, b, :], identf[:])
                    last.then_inc(o_ps, 1)

        @block.vector
        def _(dve):
            for c in credits["vector"]:
                dve.sem_inc(c.sem, 1)
            dve.sem_inc(n_cen, 1)
            dve.sem_inc(n_out, 1)
            for buf in (qbd[:], kT[:], vown[:], vprev[:]):
                dve.memset(buf, 0.0).then_inc(memsets, 1)
            dve.memset(ones[:], 1.0 / P).then_inc(memsets, 1)
            dve.memset(eps[:], LN_EPS).then_inc(memsets, 1)
            for y in (y_in, y_att, y_mid):
                dve.memset(y[:, :, 0:1], 0.0).then_inc(memsets, 1)
            dve.memset(w2_s[:, 2, :], 0.0).then_inc(memsets, 1)
            dve.memset(hs[:], 0.0).then_inc(memsets, 1)
            dve.memset(vh[:, :, :, GD:VW], 1.0).then_inc(memsets, 1)
            dve.wait_ge(memsets, N_MEMSET)
            dve.wait_ge(const_in, 96)

            def norm(k, src, dst, dst_off, dst_row):
                base = 1 + k * BLOCKS
                with dve.Fori(0, BLOCKS // 2) as i:
                    for u in range(2):
                        dve.wait_ge(n_mean, k * BLOCKS + 2 * i + u + 1)
                        dve.wait_ge(n_out, base + 2 * i)
                        dve.tensor_tensor(qkn[:, u, 0:CW], src[:, bass.ds((2 * i + u) * CW, CW)], ps_qk[:, u, :],
                                          ALU.subtract).then_inc(n_cen, 1)
                    for u in range(2):
                        dve.wait_ge(n_rstd, k * BLOCKS + 2 * i + u + 1)
                        dve.wait_ge(n_cen, base + 2 * i + u + 1)
                        dve.tensor_tensor(dst[:, bass.ds(i, 1), 1 + u * CW:1 + (u + 1) * CW].rearrange("p a t -> p (a t)"),
                                          qkn[:, u, 0:CW], t2[:, u, 0:CW], ALU.mult).then_inc(n_out, 1)

            def stage(lay, n):
                y = (y_in, y_mid)[lay % DEPTH]
                dve.wait_ge(v_ps.sem, v_ps.at(lay, n, 0))
                need(dve, qk_ps, lay, n, 0)
                if isinstance(n, int):
                    if lay % DEPTH:
                        need(dve, yo_done, lay - 1, n, 2)
                    else:
                        dve.wait_ge(n_out, 1 + BLOCKS * (2 * (lay // DEPTH) + 1))
                dve.tensor_copy(hs[0:64, :, :], y[0:64, :, bass.ds(n * P + 1, P)]).then_inc(hs_ready.sem, 1)
                dve.tensor_copy(hs[64:P, :, :], y[64:P, :, bass.ds(n * P, P)]).then_inc(hs_ready.sem, 1)

            def scale_tables(lay, n):
                dve.wait_ge(scl_in, 16 * (lay + 1))
                need(dve, t1_done, lay, n, 0)
                need(dve, t2_done, lay, n, 0)
                for i, tab in enumerate((ropec, ropes)):
                    dve.tensor_tensor(rope_n[:, i, :, :], tab[:, bass.ds(n, 1), :, :].rearrange("p o a d -> p (o a) d"),
                                      scl[:, i, :, :], ALU.mult).then_inc(tab_scaled.sem, 1)

            def step(cur):
                tile0, tile1, tile2 = (back(cur, d) for d in range(3))

                def sum_reciprocals(s):
                    tile, b = item(cur, s, 2)
                    if tile is None:
                        return
                    need(dve, exp_done, *tile, b + 1)
                    need(dve, p_norm, *tile, b - 1)
                    dve.reciprocal(psum_e[:, b % 2, 1, :], psum_e[:, b % 2, 0, :]).then_inc(rsum_done.sem, 1)

                def carry_keys(s):
                    tile, b = item(cur, s, 1)
                    if tile is None:
                        return
                    need(dve, s_ps, *tile, b - 3)
                    need(dve, qkt_sb, *tile, 2 * (b - B) + 2)
                    dve.tensor_copy(kT[:, b, :, 0:WIN], kT[:, b, :, P:P + WIN]).then_inc(k_carry.sem, 1)

                def squares(s):
                    need(dve, sq_done, *tile0, s + 1)
                    dve.tensor_reduce(ss[:], sqk[:].rearrange("p (h d) -> p h d", d=FD), axis=AX,
                                      op=ALU.add).then_inc(ss_red.sem, 1)
                    need(dve, ss_red, *tile0, s + 1)
                    dve.tensor_scalar(ssc[:], ss[:], 1e-24, None, ALU.max).then_inc(ss_clamp.sem, 1)
                    need(dve, ss_clamp, *tile0, s + 1)
                    dve.tensor_scalar(rn[:, 0, :].bitcast(I32), ssc[:].bitcast(I32), -0.5, float(ROOT_BITS), ALU.mult,
                                      ALU.add).then_inc(rn_guess.sem, 1)

                def newton(s, k):
                    if k == 0:
                        need(dve, rn_guess, *tile0, s + 1)
                    else:
                        need(dve, rn_step, *tile0, 9 * s + 3 * k)
                    dve.tensor_tensor(nw[:, 0, :], rn[:, k, :], rn[:, k, :], ALU.mult).then_inc(rn_step.sem, 1)
                    need(dve, rn_step, *tile0, 9 * s + 3 * k + 1)
                    dve.scalar_tensor_tensor(out=nw[:, 1, :], in0=nw[:, 0, :], scalar=-0.5, in1=ssc[:],
                                             op0=ALU.mult, op1=ALU.mult).then_inc(rn_step.sem, 1)
                    need(dve, rn_step, *tile0, 9 * s + 3 * k + 2)
                    dve.scalar_tensor_tensor(out=rn[:, k + 1, :], in0=nw[:, 1, :], scalar=1.5, in1=rn[:, k, :],
                                             op0=ALU.add, op1=ALU.mult).then_inc(rn_step.sem, 1)

                def normalise(s):
                    u = s % 2
                    need(dve, rn_step, *tile0, 9 * s + 9)
                    need(dve, t2_done, *tile0, 2 * s - 2)
                    need(dve, t1_done, *tile0, s - 1)
                    dve.tensor_tensor(qkn[:, u, :].rearrange("p (h d) -> p h d", d=FD),
                                      ps_qk[:].rearrange("p a (h d) -> p (a h) d", d=FD),
                                      rn[:, 3, :].unsqueeze(2).broadcast_to([P, 2 * FH, FD]),
                                      ALU.mult).then_inc(qkn_done.sem, 1)

                def rope_cosines(s):
                    u = s % 2
                    need(dve, qkn_done, *tile0, s + 1)
                    need(dve, tab_scaled, *tile0, 2)
                    need(dve, qkt_ps, *tile0, 2 * (s - 2) + 2)
                    dve.tensor_tensor(t1[:, u, :].rearrange("p (a h d) -> p a h d", a=2, d=FD),
                                      qkn[:, u, :].rearrange("p (a h d) -> p a h d", a=2, d=FD),
                                      rope_n[:, 0, :, :].unsqueeze(2).broadcast_to([P, 2, FH, FD]),
                                      ALU.mult).then_inc(t1_done.sem, 1)

                def rope_sum(s):
                    u = s % 2
                    need(dve, t2_done, *tile0, 2 * s + 2)
                    need(dve, t1_done, *tile0, s + 1)
                    dve.tensor_tensor(t1[:, u, :], t1[:, u, :], t2[:, u, :], ALU.add).then_inc(rot_done.sem, 1)

                def maxima(s):
                    tile, b = item(cur, s, 1)
                    if tile is None:
                        return
                    need(dve, s_ps, *tile, b + 1)
                    need(dve, exp_done, *tile, b - 1)
                    dve.tensor_reduce(nmax[:, b % 2, :], ps_s[:].rearrange("p a (u k) -> p (a u) k", k=P), axis=AX,
                                      op=ALU.max, negate=True).then_inc(max_done.sem, 1)

                def gated(j):
                    if tile2 is None:
                        return
                    need(dve, a_ps, *tile2, j + 1)
                    need(dve, gelu_done, *tile2, j + 1)
                    dve.scalar_tensor_tensor(out=act_t[0:CHN[j], j, :], in0=psm[0:CHN[j], :],
                                             scalar=cols_s[0:CHN[j], j:j + 1], in1=gel[0:CHN[j], j, :],
                                             op0=ALU.add, op1=ALU.mult).then_inc(glu_done.sem, 1)

                def layer_out():
                    if tile2 is None:
                        return
                    lay, m = tile2
                    need(dve, w2_ps, lay, m, 1)
                    pv = psm[:].rearrange("p (b t) -> p b t", b=B)
                    mid = y_att[:, :, bass.ds(m * P + 1, P)]
                    if lay % DEPTH == 0:
                        dve.scalar_tensor_tensor(out=y_mid[:, :, bass.ds(m * P + 1, P)], in0=pv, scalar=cols_s[:, 8:9],
                                                 in1=mid, op0=ALU.add, op1=ALU.add).then_inc(yo_done.sem, 2)
                        return
                    hv = hc[:].rearrange("p (b t) -> p b t", b=B)
                    dve.scalar_tensor_tensor(out=hv, in0=pv, scalar=cols_s[:, 8:9], in1=mid,
                                             op0=ALU.add, op1=ALU.add).then_inc(yo_done.sem, 1)
                    need(dve, yo_done, lay, m, 1)
                    xv = xT[:, :, bass.ds(m * P, P)]
                    dve.scalar_tensor_tensor(out=xv, in0=hv, scalar=0.5, in1=xv, op0=ALU.mult,
                                             op1=ALU.add).then_inc(yo_done.sem, 1)

                def attention_out():
                    if tile1 is None:
                        return
                    lay, m = tile1
                    y = (y_in, y_mid)[lay % DEPTH]
                    need(dve, wo_ps, lay, m, 1)
                    dve.tensor_tensor(y_att[:, :, bass.ds(m * P + 1, P)], psm[:].rearrange("p (b t) -> p b t", b=B),
                                      y[:, :, bass.ds(m * P + 1, P)], ALU.add).then_inc(y1_done.sem, 1)
                    need(dve, y1_done, lay, m, 1)
                    h1v = h1[:].rearrange("p (b t) -> p b t", b=B)
                    dve.tensor_scalar(h1v[0:64, :, :], y_att[0:64, :, bass.ds(m * P + 1, P)], 1.0, None, ALU.mult).then_inc(h1_done.sem, 1)
                    dve.tensor_copy(h1v[64:P, :, :], y_att[64:P, :, bass.ds(m * P, P)]).then_inc(h1_done.sem, 1)

                def centre():
                    if tile1 is None:
                        return
                    need(dve, mean_ps, *tile1, 1)
                    need(dve, h1_done, *tile1, 2)
                    dve.tensor_tensor(hc[:], h1[:], psm[:], ALU.subtract).then_inc(hc_done.sem, 1)

                def layer_norm():
                    if tile1 is None:
                        return
                    need(dve, rstd_done, *tile1, 1)
                    need(dve, hc_done, *tile1, 1)
                    dve.tensor_tensor(hc[:], hc[:], rstd[:], ALU.mult).then_inc(hn_done.sem, 1)
                    need(dve, hn_done, *tile1, 1)
                    dve.wait_ge(w2_in, 48 * (tile1[0] + 1))
                    dve.tensor_scalar(hn[:], hc[:], cols_s[:, 6:7], cols_s[:, 7:8], ALU.mult,
                                      ALU.add).then_inc(hn_done.sem, 1)

                for s in range(B):
                    if s == 0 and tile0 is not None:
                        stage(*tile0)
                    sum_reciprocals(s)
                    carry_keys(s)
                    if s == 1:
                        gated(0)
                    if tile0 is not None:
                        squares(s)
                        newton(s, 0)
                    if s == 1:
                        gated(1)
                    if s == 0 and tile0 is not None:
                        scale_tables(*tile0)
                    if tile0 is not None:
                        newton(s, 1)
                        newton(s, 2)
                        normalise(s)
                    if s == 1:
                        gated(2)
                    if s == 2:
                        attention_out()
                    if tile0 is not None:
                        rope_cosines(s)
                    maxima(s)
                    if s == 1:
                        layer_out()
                    if s == 2:
                        centre()
                    if tile0 is not None:
                        rope_sum(s)
                    if s == 3:
                        layer_norm()

            xf = xT[:, :, :].rearrange("p b t -> p (b t)")
            dve.wait_ge(xt_sb, NT + 2)
            norm(0, xf, y_in, 1, S + 1)
            steps(dve, step, 0)
            norm(1, xf, y_in, 1, S + 1)

            def stage_z(b, u):
                dve.wait_ge(n_out, 1 + 2 * BLOCKS)
                dve.tensor_copy(zs[u].unsqueeze(1), y_in[:, bass.ds(b, 1), 1 + u * CW:1 + (u + 1) * CW]).then_inc(gz_done, 1)

            dve.memset(acc, 0.0).then_inc(zero_done, 1)

            dve.wait_ge(gw_in, 48)
            with dve.Fori(0, B) as b:
                for u in range(2):
                    dve.wait_ge(gv_ps, 2 * b + u + 1)
                    stage_z(b, u)
                for u in range(2):
                    dve.wait_ge(gqk_ps, 2 * b + u + 1)
                    both = lambda t: t[:, u * CW:(u + 1) * CW].unsqueeze(1).broadcast_to([P, 2, CW])
                    v3 = lambda t: t[:, u, :].rearrange("p (a t) -> p a t", a=2)
                    dve.wait_ge(gsum, 2 * b + 1)
                    dve.tensor_tensor(v3(t1), ps_qk[:], both(gcos), ALU.mult).then_inc(grot, 1)
                    dve.tensor_tensor(v3(t2), ps_s[:], both(gsin), ALU.mult).then_inc(grot, 1)
                    dve.wait_ge(grot, 2 * (2 * b + u) + 3)
                    dve.wait_ge(gparts_out[u], 96 * b + 96)
                    dve.tensor_tensor(t1[:, u, :], t1[:, u, :], t2[:, u, :], ALU.add).then_inc(gsum, 1)
                    dve.wait_ge(gv_ps, 2 * b + u + 3)
                    dve.tensor_scalar(
                        v_all[:, bass.ds(b * S, S)].rearrange("p (h t d) -> p t h d", h=GH, t=NT)[:, 4 * u:4 * u + 4, :, :],
                        psr[:, u, :].rearrange("p (t h d) -> p t h d", t=4, d=GD), 1.0, None, ALU.mult).then_inc(gv_sb, 1)
                    dve.wait_ge(gp1, 2 * b + u + 1)
                    dve.tensor_tensor(v3(t2), v3(t1), parts[u][:, :, 0, :], ALU.subtract).then_inc(gr1, 1)
                    dve.wait_ge(gp2, 2 * b + u + 1)
                    dve.tensor_tensor(parts[u][:, :, 2, :], v3(t2), parts[u][:, :, 1, :], ALU.subtract).then_inc(gp3, 1)
            dve.wait_ge(gv_sb, 2 * B + 2)
            dve.wait_ge(gp3, 2 * B)

            def head_step(i, u):
                if live(i, 2):
                    need(dve, pv_ps, 0, i - 4, 2) if live(i, 4) else None
                    need(dve, vh_done, 0, i - 3, 1) if live(i, 3) else None
                    dve.tensor_scalar(vh[:, u % 2, :, 0:GD], v_all[:, bass.ds((i - 2) * (NT * GD), NT * GD)].rearrange("p (t d) -> p t d", d=GD),
                                      1.0, None, ALU.mult).then_inc(vh_done.sem, 1)
                jobs1 = ring1(i, u)
                for n, (kind, head, c, bank) in enumerate(jobs1):
                    if kind == "max":
                        t, half = CHUNKS[c]
                        cols_n = min((t + 1) * P, (half + 1) * 512) - half * 512
                        need(dve, p1_ps, 0, head, c + 1)
                        if c == 0 and live(i, 2):
                            need(dve, r1_done, 0, head - 2, 1)
                        dve.tensor_reduce(nm[:, u % 2, half, t:t + 1], psr[:, bank, 0:cols_n], axis=AX, op=ALU.max,
                                          negate=True).then_inc(p1_max.sem, 1)
                    else:
                        need(dve, nT_ps, 0, head, 1)
                        dve.wait_ge(nT_in[(u - 3) % TURN], turn_at(i - 3, (u - 3) % TURN, 16, 16)) if live(i, 3) else None
                        dve.tensor_copy(nT[:, (u - 1) % 2, :], psr[0:3 * NT, bank, 0:P // 2].bitcast(BF16)).then_inc(nT_sb.sem, 1)
                    if n == 2 and live(i, 3):
                        k = (u - 3) % 2
                        bank2 = ring2(i, u)[0][3]
                        need(dve, fin_ps, 0, i - 3, 1)
                        finish(i - 3, k, bank2)
                if live(i, 3) and len(jobs1) < 3:
                    need(dve, fin_ps, 0, i - 3, 1)
                    finish(i - 3, (u - 3) % 2, ring2(i, u)[0][3])
                if live(i, 0):
                    k = u % 2
                    need(dve, p1_max, 0, i, len(CHUNKS))
                    dve.tensor_tensor(nm[:, k, 0, 4:NT], nm[:, k, 0, 4:NT], nm[:, k, 1, 4:NT], ALU.min).then_inc(nm_done.sem, 1)
                    need(dve, nm_done, 0, i, 1)
                    need(dve, nT_ps, 0, i - 1, 0) if live(i, 2) else None
                    dve.tensor_copy(nparts[:, k, 0, :], nm[:, k, 0, :]).then_inc(n1_done.sem, 1)
                    need(dve, n1_done, 0, i, 1)
                    dve.tensor_tensor(nres[:, k, :], nm[:, k, 0, :], nparts[:, k, 0, :], ALU.subtract).then_inc(r1_done.sem, 1)
                    need(dve, r1_done, 0, i, 1)
                    dve.tensor_copy(nparts[:, k, 1, :], nres[:, k, :]).then_inc(n2_done.sem, 1)
                    need(dve, n2_done, 0, i, 1)
                    dve.tensor_tensor(nparts[:, k, 2, :], nres[:, k, :], nparts[:, k, 1, :], ALU.subtract).then_inc(n3_done.sem, 1)

            def finish(head, k, bank):
                where = (ps_qk, ps_s)[bank]
                need(dve, o_done, 0, head, 0)
                dve.tensor_reduce(osum[:, k, :, :],
                                  where[:].rearrange("p a (t c w) -> p (a t) w c", c=4, w=32)[:, :, 0:VW, :], axis=AX,
                                  op=ALU.add).then_inc(osum_done.sem, 1)
                need(dve, osum_done, 0, head, 1)
                dve.reciprocal(orec[:, k, :], osum[:, k, :, GD]).then_inc(orec_done.sem, 1)
                need(dve, orec_done, 0, head, 1)
                dve.tensor_tensor(o_all[:, bass.ds(head * (NT * GD), NT * GD)].rearrange("p (t d) -> p t d", d=GD),
                                  osum[:, k, :, 0:GD], orec[:, k, :].unsqueeze(2).broadcast_to([P, NT, GD]),
                                  ALU.mult).then_inc(o_done.sem, 1)
            head_steps(dve, head_step)

            with dve.Fori(0, NT // 2) as i:
                for u in range(2):
                    dve.wait_ge(w_tps, 2 * i + u + 1)
                    dve.wait_ge(o_done.sem, o_done.at(0, HEADS, 0))
                    dve.tensor_scalar(t1[:, u, 0:CW].rearrange("p (b h d) -> p b h d", b=B, d=GD),
                                      o_all.rearrange("p (b h t d) -> p b h t d", b=B, h=GH, d=GD)[:, :, :, bass.ds(2 * i + u, 1), :].rearrange("p b h o d -> p b h (o d)"),
                                      1.0, None, ALU.mult).then_inc(w_stage, 1)
                for u in range(2):
                    dve.wait_ge(w_ps, 2 * i + u + 1)
                    xv = xT[:, :, bass.ds((2 * i + u) * P, P)]
                    dve.tensor_tensor(xv, xv, ps_s[:, u, :].rearrange("p (b t) -> p b t", b=B), ALU.add).then_inc(w_done, 1)
            dve.wait_ge(w_done, NT + 2)
            for y in (y_att, y_mid):
                dve.memset(y[:, :, 0:1], 0.0).then_inc(zero_done, 1)
            dve.wait_ge(zero_done, 3)
            norm(2, xf, y_in, 1, S + 1)
            steps(dve, step, DEPTH)
            with dve.Fori(0, NT // 2) as i:
                for u in range(2):
                    dve.wait_ge(o_ps, 2 * i + u + 1)
                    dve.tensor_scalar(prT[:, u, 0:B, :], xT[:, :, bass.ds((2 * i + u) * P, P)], 1.0, None, ALU.mult).then_inc(o_stage, 1)

        @block.scalar
        def _(act):
            for c in credits["scalar"]:
                act.sem_inc(c.sem, 1)
            act.sem_inc(xt_sb, 2)
            act.sem_inc(o_sb, 2)
            act.wait_ge(memsets, N_MEMSET)
            with act.Fori(0, NT // 2) as i:
                for u in range(2):
                    act.wait_ge(xt_ps, 2 * i + u + 3)
                    act.activation(xT[:, :, bass.ds((2 * i + u) * P, P)], ps_qk[:, u, :].rearrange("p (b t) -> p b t", b=B),
                                   ACT.Copy).then_inc(xt_sb, 1)

            def norm(k):
                base = 1 + k * BLOCKS
                with act.Fori(0, BLOCKS // 2) as i:
                    for u in range(2):
                        act.wait_ge(n_cen, base + 2 * i + u + 1)
                        act.activation(t1[:, u, 0:CW], qkn[:, u, 0:CW], ACT.Square).then_inc(n_sq, 1)
                    for u in range(2):
                        act.wait_ge(n_var, k * BLOCKS + 2 * i + u + 1)
                        act.wait_ge(n_out, base + 2 * i)
                        act.activation(sqk[:, u * CW:(u + 1) * CW], ps_s[:, u, :], ACT.Ln, bias=eps[:]).then_inc(n_log, 1)
                        act.wait_ge(n_log, k * BLOCKS + 2 * i + u + 1)
                        act.activation(t2[:, u, 0:CW], sqk[:, u * CW:(u + 1) * CW], ACT.Exp, scale=-0.5).then_inc(n_rstd, 1)

            def step(cur):
                tile0, tile1, tile2 = (back(cur, d) for d in range(3))

                def keep_values(s):
                    if tile0 is None:
                        return
                    need(act, v_ps, *tile0, s + 1)
                    need(act, v_lo[s], *tile0, 1)
                    act.activation(vown[:, s, :], psm[:], ACT.Copy).then_inc(v_sb.sem, 1)

                def keep_outputs(s):
                    tile, b = item(cur, s, 3)
                    if tile is None:
                        return
                    need(act, wo_ps, *tile, 0)
                    for h in range(2):
                        bank = psr[:, bank_of((b + 2) % B, "o2", h), :]
                        need(act, o2_ps, *tile, 2 * b + h + 1)
                        for i in range(2):
                            last = act.activation(
                                oT[i * 64:(i + 1) * 64, 2 * h:2 * h + 2, b, :].rearrange("p j (w q) -> p j w q", w=2),
                                bank[i * 64:(i + 1) * 64, :].rearrange("p (j w q) -> p j w q", j=2, w=2)[:, :, :, i * 64:(i + 1) * 64],
                                ACT.Copy)
                        last.then_inc(o2_sb.sem, 1)

                def squares(s):
                    if tile0 is None:
                        return
                    need(act, qk_ps, *tile0, s + 1)
                    need(act, ss_red, *tile0, s)
                    act.activation(sqk[:], ps_qk[:].rearrange("p a c -> p (a c)"), ACT.Square).then_inc(sq_done.sem, 1)

                def keep_qk(s):
                    tile, b = item(cur, s, 1)
                    if tile is None:
                        return
                    need(act, qkt_ps, *tile, 2 * b + 1)
                    need(act, s_ps, *tile, b - 1)
                    for h in range(2):
                        last = act.activation(
                            qbd[h * 64:(h + 1) * 64, b % 2, :, :, h * 64:(h + 1) * 64].rearrange("p j w q -> p (j w) q"),
                            psr[h * 64:(h + 1) * 64, bank_of(s, "qkt", 0), :].rearrange("p (j q) -> p j q", q=64), ACT.Copy)
                    last.then_inc(qkt_sb.sem, 1)
                    need(act, qkt_ps, *tile, 2 * b + 2)
                    need(act, k_carry, *tile, b + 1)
                    act.activation(kT[:, b, :, WIN:WIN + P], psr[:, bank_of(s, "qkt", 1), :].rearrange("p (j t) -> p j t", j=PAIRS),
                                   ACT.Copy).then_inc(qkt_sb.sem, 1)

                def keep_probs(s):
                    tile, b = item(cur, s, 2)
                    if tile is None:
                        return
                    need(act, o2_ps, *tile, 2 * (b - 2) + 2)
                    for h in range(2):
                        need(act, pt_ps, *tile, 2 * b + h + 1)
                        act.activation(prT[:, b % 2, 4 * h:4 * h + 4, :].rearrange("p u q -> p (u q)"),
                                       psr[:, bank_of(s, "pt", h), :], ACT.Copy).then_inc(pt_sb.sem, 1)

                def exponentials(s):
                    tile, b = item(cur, s, 1)
                    if tile is None:
                        return
                    u = b % 2
                    need(act, max_done, *tile, b + 1)
                    need(act, pt_ps, *tile, 2 * (b - 2) + 2)
                    need(act, rsum_done, *tile, b - 1)
                    for j in range(UNITS):
                        last = act.activation(pr[:, u, j, :], ps_s[:, j // 4, (j % 4) * P:(j % 4 + 1) * P], ACT.Exp,
                                              bias=nmax[:, u, j:j + 1], accum_out=psum_e[:, u, 0, j:j + 1])
                    last.then_inc(exp_done.sem, 1)

                def gelu(j):
                    if tile2 is None:
                        return
                    need(act, g_ps, *tile2, j + 1)
                    act.activation(gel[0:CHN[j], j, :], psm[0:CHN[j], :], ACT.Gelu,
                                   bias=cols_s[0:CHN[j], 3 + j:4 + j]).then_inc(gelu_done.sem, 1)

                def square_centred():
                    if tile1 is None:
                        return
                    need(act, hc_done, *tile1, 1)
                    act.activation(hq[:], hc[:], ACT.Square).then_inc(hq_done.sem, 1)

                def deviation():
                    if tile1 is None:
                        return
                    need(act, var_ps, *tile1, 1)
                    act.activation(hq[:], psm[:], ACT.Ln, bias=eps[:]).then_inc(lnv_done.sem, 1)
                    need(act, lnv_done, *tile1, 1)
                    act.activation(rstd[:], hq[:], ACT.Exp, scale=-0.5).then_inc(rstd_done.sem, 1)

                keep_outputs(0)
                gelu(0)
                keep_qk(0)
                keep_values(0)
                squares(0)
                gelu(1)
                keep_probs(0)
                gelu(2)
                exponentials(0)
                for s in range(1, B):
                    keep_values(s)
                    keep_outputs(s)
                    squares(s)
                    if s == 3:
                        square_centred()
                    keep_qk(s)
                    if s == 3:
                        deviation()
                    keep_probs(s)
                    exponentials(s)

            norm(0)
            steps(act, step, 0)
            norm(1)
            with act.Fori(0, B) as b:
                for u in range(2):
                    v3 = lambda t: t[:, u, :].rearrange("p (a t) -> p a t", a=2)
                    act.wait_ge(gsum, 2 * b + u + 2)
                    act.activation(parts[u][:, :, 0, :], v3(t1), ACT.Copy).then_inc(gp1, 1)
                    act.wait_ge(gr1, 2 * b + u + 1)
                    act.activation(parts[u][:, :, 1, :], v3(t2), ACT.Copy).then_inc(gp2, 1)
            act.wait_ge(gp3, 2 * B)

            def head_step(i, u):
                for kind, head, c, bank in ring2(i, u):
                    if kind == "fin":
                        continue
                    n = S - c * P
                    need(act, p2_ps, 0, head, c + 1)
                    if live(head, 1):
                        need(act, pv_ps, 0, head - 1, 1 + c // 4)
                    act.activation(pT[c], (ps_qk, ps_s)[bank][:].rearrange("p a q -> p (a q)")[:, 0:n], ACT.Exp,
                                   scale=float(GD) ** -0.5).then_inc(p2_exp.sem, 1)
                if live(i, 2):
                    need(act, pv_ps, 0, i - 2, 2)
                    need(act, fin_ps, 0, i - 2, 0)
                    act.activation(acc_sb[:].rearrange("p (a q) -> p a q", a=2), acc, ACT.Copy).then_inc(acc_done.sem, 1)
            head_steps(act, head_step)

            with act.Fori(0, NT // 2) as i:
                for u in range(2):
                    act.wait_ge(w_tps, 2 * i + u + 3)
                    act.activation(t2[:, u, 0:CW], ps_qk[:, u, :], ACT.Copy).then_inc(w_tsb, 1)
            act.wait_ge(w_done, NT + 2)
            norm(2)
            steps(act, step, DEPTH)
            with act.Fori(0, NT // 2) as i:
                for u in range(2):
                    act.wait_ge(o_ps, 2 * i + u + 3)
                    act.wait_ge(o_out[u], 16 * i + 16)
                    act.activation(pr[:, u, 0:B, :].rearrange("p b t -> p (b t)"), ps_qk[:, u, :], ACT.Copy).then_inc(o_sb, 1)

        @block.gpsimd
        def _(pool):
            for c in credits["gpsimd"]:
                pool.sem_inc(c.sem, 1)
            pool.sem_inc(xt_ps, 2)
            pool.sem_inc(o_ps, 2)
            for c in (gv_ps, gv_sb, w_tps, w_tsb, w_done):
                pool.sem_inc(c, 2)
            for c in (grot, gsum):
                pool.sem_inc(c, 1)
            for u in range(2):
                pool.sem_inc(gparts_out[u], 96)
            for u in range(2):
                pool.sem_inc(o_out[u], 16)

            def step(cur):
                for s in range(B):
                    tile, b = item(cur, s, 2)
                    if tile is not None:
                        need(pool, rsum_done, *tile, b + 1)
                        pool.tensor_tensor(pr[:, b % 2, :, :], pr[:, b % 2, :, :],
                                           psum_e[:, b % 2, 1, :].unsqueeze(2).broadcast_to([P, UNITS, P]),
                                           ALU.mult).then_inc(p_norm.sem, 1)
                    tile = back(cur, 0)
                    if tile is not None:
                        u = s % 2
                        need(pool, qkn_done, *tile, s + 1)
                        need(pool, rot_done, *tile, s - 1)
                        need(pool, tab_scaled, *tile, 2)
                        for a in range(2):
                            src = qkn[:, u, :].rearrange("p (a h d) -> p a h d", a=2, d=FD)[:, :, :, (1 - a) * 32:(2 - a) * 32]
                            dst = t2[:, u, :].rearrange("p (a h d) -> p a h d", a=2, d=FD)[:, :, :, a * 32:(a + 1) * 32]
                            tab = rope_n[:, 1, :, a * 32:(a + 1) * 32].unsqueeze(2).broadcast_to([P, 2, FH, 32])
                            pool.tensor_tensor(dst, src, tab, ALU.mult).then_inc(t2_done.sem, 1)

            steps(pool, step, 0)
            steps(pool, step, DEPTH)


def rope_tables():
    half = np.arange(0, FD, 2, dtype=np.float32)
    inv = (1.0 / 10000.0 ** (half / FD)).astype(np.float32)
    t = np.arange(S, dtype=np.float32)
    freqs = (t[:, None] * inv[None, :]).astype(np.float32)
    base = ((half + 0.4 * FD) / (1.4 * FD)).astype(np.float32)
    power = ((t - S // 2) / float(WIN // 2)).astype(np.float32)
    scale = (base[None, :] ** power[:, None]).astype(np.float32)
    cos, sin = np.cos(freqs), np.sin(freqs)
    both = lambda a, b: np.stack([np.concatenate([a * scale * 8.0, b * scale * 8.0], 1),
                                  np.concatenate([a / scale, b / scale], 1)], 1)
    lay = lambda a: np.ascontiguousarray(a.astype(np.float32).reshape(NT, P, 2, FD).transpose(1, 0, 2, 3))
    return lay(both(cos, cos)), lay(both(-sin, sin))


def global_rope():
    half = GD // 2
    inv = (1.0 / 10000.0 ** (np.arange(half, dtype=np.float32) / half)).astype(np.float32)
    ang = (np.arange(S, dtype=np.float32)[:, None] * inv[None, :]).astype(np.float32)
    cos, sin = np.cos(ang).T, np.sin(ang).T
    tile = lambda a: np.ascontiguousarray(np.tile(a, (GH, 1)).astype(np.float32))
    return tile(np.concatenate([cos, cos])), tile(np.concatenate([-sin, sin]))


def band_mask():
    q = np.arange(P)[:, None, None] % WIN
    w = np.arange(2 * NT)[None, :, None]
    c = np.arange(P)[None, None, :]
    seen = (c >= q) & (c <= q + WIN) & ((w > 0) | (c >= WIN))
    return np.where(seen, 0.0, -1e30).astype(np.float32)


def kernel(L0_attn_x, L0_attn_Wq, L0_attn_Wk, L0_attn_Wv, L0_attn_Wo, L0_ffn_wqkv, L0_ffn_q_scale, L0_ffn_k_scale,
           L0_ffn_wo, L0_ffn_ln_g, L0_ffn_ln_b, L0_ffn_w1, L0_ffn_b1, L0_ffn_w2, L0_ffn_b2):
    import ml_dtypes
    import concourse.bacc as bacc
    from concourse.bass_utils import run_bass_kernel_spmd

    f = lambda a: np.ascontiguousarray(np.asarray(a))
    cols = np.zeros((DEPTH, P, 9), np.float32)
    for j in range(CH):
        cols[:, :CHN[j], j] = f(L0_ffn_b1)[:, j * P:j * P + CHN[j]]
        cols[:, :CHN[j], 3 + j] = f(L0_ffn_b1)[:, HID + j * P:HID + j * P + CHN[j]]
    cols[:, :, 6], cols[:, :, 7], cols[:, :, 8] = f(L0_ffn_ln_g), f(L0_ffn_ln_b), f(L0_ffn_b2)
    qk = np.stack([f(L0_ffn_q_scale), f(L0_ffn_k_scale)], 1)
    swapped = np.concatenate([qk[:, :, FD // 2:], qk[:, :, :FD // 2]], 2)
    qkscale = f(np.broadcast_to(np.stack([qk, swapped], 1)[:, None], (DEPTH, P, 2, 2, FD)))
    rope_cos, rope_sin = rope_tables()
    arrays = {
        "x": f(L0_attn_x), "wqkv": f(L0_ffn_wqkv), "qkscale": qkscale, "wo": f(L0_ffn_wo), "w1": f(L0_ffn_w1),
        "w2": f(L0_ffn_w2), "cols": cols, "rope_cos": rope_cos, "rope_sin": rope_sin,
        "bandmask": band_mask().astype(ml_dtypes.bfloat16), "identb_d": np.eye(P).astype(ml_dtypes.bfloat16),
        "identf_d": np.eye(P, dtype=np.float32),
    }
    Wq, Wk = f(L0_attn_Wq), f(L0_attn_Wk)
    swap = np.arange(P).reshape(GH, 2, GD // 2)[:, ::-1].reshape(-1)
    arrays["gw"] = np.stack([f(w.T) for w in (Wq, Wk, Wq[swap], Wk[swap], f(L0_attn_Wv), f(L0_attn_Wo))])
    arrays["g_cos"], arrays["g_sin"] = global_rope()
    q, k = np.arange(P)[:, None], np.arange(P)[None, :]
    arrays["causal"] = np.where(np.stack([k > q, q > k], 1), -1e30, 0.0).astype(ml_dtypes.bfloat16)
    tail = np.zeros((2, STACK - 9 * GD, S), ml_dtypes.bfloat16)
    tail[0, 0:3] = 1
    arrays["stack_tail"] = tail
    nc = bacc.Bacc("TRN2", target_bir_lowering=False, num_devices=1)
    args = {k: nc.dram_tensor(k, a.shape, mybir.dt.from_np(a.dtype), kind="ExternalInput").ap() for k, a in arrays.items()}
    args["out"] = nc.dram_tensor("out", (B, S, P), F32, kind="ExternalOutput").ap()
    program(nc, **args)
    r = run_bass_kernel_spmd(nc, [arrays], core_ids=[0])
    return r.results[0]["out"]
```

```python
from contextlib import ExitStack

import numpy as np

import concourse.bass as bass
from concourse import mybir

F32 = mybir.dt.float32
BF16 = mybir.dt.bfloat16
I32 = mybir.dt.int32
ALU = mybir.AluOpType
ACT = mybir.ActivationFunctionType
AX = mybir.AxisListType.X

P = 128
B, S = 4, 1024
NT = S // P
TOK = B * S
FH, FD = 8, 64
INNER = FH * FD
PAIRS = FH // 2
WIN = 64
UNITS = 2 * PAIRS
DEPTH = 2
HID = 341
CH = 3
CHN = [min(P, HID - P * j) for j in range(CH)]
GH, GD = 16, 8
STACK = 96
LN_EPS = 1e-5
ROOT_BITS = 0x5f3759df
BLOCKS = 8
CW = TOK // BLOCKS
HEADS = B * GH
TURN = 4
CHUNKS = [(i, c) for i in range(NT) for c in range(1 + i // 4)]
VW = GD + 1


class Count:

    def __init__(self, sem, per, by=1, first=1):
        self.sem, self.per, self.by, self.first = sem, per, by, first

    def at(self, layer, n, c):
        return (layer * NT + n) * (self.per * self.by) + (self.first + c * self.by)


def need(eng, count, layer, n, c):
    v = count.at(layer, n, c)
    if not isinstance(v, int) or v > count.first:
        eng.wait_ge(count.sem, v)


def program(nc, x, wqkv, qkscale, wo, w1, w2, cols, rope_cos, rope_sin, bandmask, identb_d, identf_d,
            gw, g_cos, g_sin, causal, stack_tail, out):
    ctx = ExitStack()
    with ctx:
        def sb(name, shape, dt=F32):
            return ctx.enter_context(nc.sbuf_tensor(name, shape, dt))

        def sem(name):
            return ctx.enter_context(nc.semaphore(name))

        xT = sb("xT", [P, B, S])
        y_in = sb("y_in", [P, B, S + 1])
        y_att = sb("y_att", [P, B, S + 1])
        y_mid = sb("y_mid", [P, B, S + 1])
        identf = sb("identf", [P, P])
        identb = sb("identb", [P, P], BF16)
        ones = sb("ones", [P, P])
        mask = sb("mask", [P, 2 * NT, P], BF16)
        ropec = sb("ropec", [P, NT, 2, FD])
        ropes = sb("ropes", [P, NT, 2, FD])
        eps = sb("eps", [P, 1])
        wqkv_s = sb("wqkv_s", [P, 3 * INNER])
        wo_s = sb("wo_s", [P, PAIRS, P])
        w1_s = sb("w1_s", [P, 2 * HID])
        w2_s = sb("w2_s", [P, CH, P])
        cols_s = sb("cols_s", [P, 9])
        rope_n = sb("rope_n", [P, 2, 2, FD])
        scl = sb("scl", [P, 2, 2, FD])
        hs = sb("hs", [P, B, P])
        sqk = sb("sqk", [P, 2 * INNER])
        ss = sb("ss", [P, 2 * FH])
        ssc = sb("ssc", [P, 2 * FH])
        rn = sb("rn", [P, 4, 2 * FH])
        nw = sb("nw", [P, 2, 2 * FH])
        qkn = sb("qkn", [P, 2, 2 * INNER])
        t1 = sb("t1", [P, 2, 2 * INNER])
        t2 = sb("t2", [P, 2, 2 * INNER])
        qbd = sb("qbd", [P, 2, PAIRS, 2, P])
        kT = sb("kT", [P, B, PAIRS, WIN + P])
        vown = sb("vown", [P, B, INNER])
        vprev = sb("vprev", [P, B, INNER])
        nmax = sb("nmax", [P, 2, UNITS])
        psum_e = sb("psum_e", [P, 2, 2, UNITS])
        pr = sb("pr", [P, 2, UNITS, P])
        prT = sb("prT", [P, 2, UNITS, P])
        oT = sb("oT", [P, PAIRS, B, P])
        h1 = sb("h1", [P, CW])
        hc = sb("hc", [P, CW])
        hq = sb("hq", [P, CW])
        rstd = sb("rstd", [P, CW])
        hn = sb("hn", [P, CW])
        gel = sb("gel", [P, CH, CW])
        act_t = sb("act_t", [P, CH, CW])
        ps = [ctx.enter_context(nc.psum_tensor(f"ps{i}", [P, 2, 512], F32)) for i in range(2)]
        psr = ctx.enter_context(nc.psum_tensor("psr", [P, 4, 512], F32))
        psm = psr[:, 3, :]
        ps_qk, ps_s = ps

        gw_s = wqkv_s[:, 0:6 * P].rearrange("p (w n) -> p w n", w=6)
        gcos = gel[:].rearrange("p a b -> p (a b)")[:, 0:S]
        gsin = act_t[:].rearrange("p a b -> p (a b)")[:, 0:S]
        zs = [hs[:].rearrange("p b t -> p (b t)"), h1[:]]
        parts = [t.bitcast(BF16)[:, 0:6 * CW].rearrange("p (a j t) -> p a j t", a=2, j=3)
                 for t in (qbd[:].rearrange("p u j w q -> p (u j w q)"), oT[:].rearrange("p j b q -> p (j b q)"))]
        kst, qst = [t[:].rearrange("p a u k -> p (a u k)").bitcast(BF16).rearrange("p (u t) -> p u t", u=TURN)
                    for t in (pr, prT)]
        v_all = y_att[:].rearrange("p b t -> p (b t)")[:, 4:4 + TOK]
        o_all = y_mid[:].rearrange("p b t -> p (b t)")[:, 4:4 + TOK]
        pT = [t1[:, 0, :], t1[:, 1, 0:896], t2[:, 0, 0:768], t2[:, 1, 0:640],
              qkn[:, 0, 0:512], qkn[:, 0, 512:896], qkn[:, 1, 0:256], qkn[:, 1, 256:384]]
        acc = psr[:, 2:4, :]
        acc_sb = sqk
        causal_s = sb("causal_s", [P, 2, P], BF16)
        vh = sb("vh", [P, 2, NT, VW])
        nm = sb("nm", [P, 2, 2, NT])
        nres = sb("nres", [P, 2, NT])
        nparts = sb("nparts", [P, 2, 3, NT], BF16)
        nT = sb("nT", [3 * NT, 2, P], BF16)
        osum = sb("osum", [P, 2, NT, VW])
        orec = sb("orec", [P, 2, NT])
        scratch = nc.dram_tensor("scratch", (2, HEADS, 3, GD, S), BF16, kind="Internal").ap()

        one = lambda name, per: Count(sem(name), per)
        hs_ready = one("hs_ready", 2)
        tab_scaled = one("tab_scaled", 2)
        qk_ps = one("qk_ps", 4)
        v_ps = one("v_ps", 4)
        sq_done = one("sq_done", 4)
        ss_red = one("ss_red", 4)
        ss_clamp = one("ss_clamp", 4)
        rn_guess = one("rn_guess", 4)
        rn_step = one("rn_step", 9 * B)
        qkn_done = one("qkn_done", 4)
        t1_done = one("t1_done", 4)
        t2_done = one("t2_done", 8)
        rot_done = one("rot_done", 4)
        rotk_done = one("rotk_done", 4)
        qkt_ps = one("qkt_ps", 2 * B)
        qkt_sb = one("qkt_sb", 2 * B)
        pt_ps = one("pt_ps", 2 * B)
        pt_sb = one("pt_sb", 2 * B)
        o2_ps = one("o2_ps", 2 * B)
        o2_sb = one("o2_sb", 2 * B)
        k_carry = one("k_carry", 4)
        v_sb = one("v_sb", 4)
        s_ps = one("s_ps", 4)
        max_done = one("max_done", 4)
        exp_done = one("exp_done", 4)
        esum_done = one("esum_done", 4)
        rsum_done = one("rsum_done", 4)
        p_norm = one("p_norm", 8)
        wo_ps = one("wo_ps", 1)
        y1_done = one("y1_done", 1)
        h1_done = one("h1_done", 2)
        mean_ps = one("mean_ps", 1)
        hc_done = one("hc_done", 1)
        hq_done = one("hq_done", 1)
        var_ps = one("var_ps", 1)
        lnv_done = one("lnv_done", 1)
        rstd_done = one("rstd_done", 1)
        hn_done = one("hn_done", 2)
        g_ps = one("g_ps", CH)
        gelu_done = one("gelu_done", CH)
        a_ps = one("a_ps", CH)
        glu_done = one("glu_done", CH)
        w2_ps = one("w2_ps", 1)
        yo_done = one("yo_done", 2)
        v_lo = [Count(sem(f"v_lo{b}"), 1, 16, 0) for b in range(B)]
        v_hi = [Count(sem(f"v_hi{b}"), 1, 16, 0) for b in range(B)]
        scl_in = sem("scl_in")
        wqkv_in = sem("wqkv_in")
        wo_in = sem("wo_in")
        w1_in = sem("w1_in")
        w2_in = sem("w2_in")
        const_in = sem("const_in")
        memsets = sem("memsets")
        x_in = [sem(f"x_in{i}") for i in range(2)]
        xt_ps = sem("xt_ps")
        xt_sb = sem("xt_sb")
        n_mean = sem("n_mean")
        n_cen = sem("n_cen")
        n_sq = sem("n_sq")
        n_var = sem("n_var")
        n_log = sem("n_log")
        n_rstd = sem("n_rstd")
        n_out = sem("n_out")
        o_stage = sem("o_stage")
        o_ps = sem("o_ps")
        o_sb = sem("o_sb")
        o_out = [sem(f"o_out{i}") for i in range(2)]
        N_MEMSET = 12
        gw_in = sem("gw_in")
        gz_done = sem("gz_done")
        gqk_ps = sem("gqk_ps")
        gv_ps = sem("gv_ps")
        gv_sb = sem("gv_sb")
        grot = sem("grot")
        gsum = sem("gsum")
        gp1 = sem("gp1")
        gr1 = sem("gr1")
        gp2 = sem("gp2")
        gp3 = sem("gp3")
        gparts_out = [sem(f"gparts_out{u}") for u in range(2)]
        st_in = [sem(f"st_in{u}") for u in range(TURN)]
        tail_in = sem("tail_in")
        p1_ps = one("p1_ps", len(CHUNKS))
        p1_max = one("p1_max", len(CHUNKS))
        nm_done = one("nm_done", 1)
        n1_done = one("n1_done", 1)
        r1_done = one("r1_done", 1)
        n2_done = one("n2_done", 1)
        n3_done = one("n3_done", 1)
        nT_ps = one("nT_ps", 1)
        nT_sb = one("nT_sb", 1)
        nT_in = [sem(f"nT_in{u}") for u in range(TURN)]
        p2_ps = one("p2_ps", NT)
        p2_exp = one("p2_exp", NT)
        vh_done = one("vh_done", 1)
        pv_ps = one("pv_ps", 2)
        acc_done = one("acc_done", 1)
        fin_ps = one("fin_ps", 1)
        osum_done = one("osum_done", 1)
        orec_done = one("orec_done", 1)
        o_done = one("o_done", 1)
        w_stage = sem("w_stage")
        w_tps = sem("w_tps")
        w_tsb = sem("w_tsb")
        w_ps = sem("w_ps")
        w_done = sem("w_done")
        zero_done = sem("zero_done")
        qbd_zero = sem("qbd_zero")

        credits = {
            "vector": [hs_ready, tab_scaled, ss_red, ss_clamp, rn_guess, rn_step, qkn_done, t1_done, rot_done, k_carry, max_done,
                       esum_done, rsum_done, y1_done, h1_done, hc_done, hn_done, glu_done, yo_done, p1_max, nm_done, n1_done,
                       r1_done, n2_done, n3_done, nT_sb, vh_done, osum_done, orec_done, o_done],
            "scalar": [sq_done, qkt_sb, pt_sb, o2_sb, v_sb, exp_done, hq_done, lnv_done, rstd_done,
                       gelu_done, p2_exp, acc_done],
            "tensor": [qk_ps, v_ps, qkt_ps, pt_ps, o2_ps, s_ps, wo_ps, mean_ps, var_ps, g_ps, a_ps, w2_ps,
                       p1_ps, nT_ps, p2_ps, pv_ps, fin_ps],
            "gpsimd": [t2_done, rotk_done, p_norm],
        }

        def steps(eng, step, layer0):
            for lay in range(layer0, layer0 + DEPTH):
                for n in range(2):
                    step((layer0, lay, n))
                with eng.Fori(2, NT - 1) as n:
                    step((layer0, lay, n))
                step((layer0, lay, NT - 1))
            for n in range(2):
                step((layer0, layer0 + DEPTH, n))

        def back(cur, d):
            layer0, lay, n = cur
            if not isinstance(n, int):
                return lay, n - d
            t = (lay - layer0) * NT + n - d
            return (layer0 + t // NT, t % NT) if 0 <= t < DEPTH * NT else None

        def item(cur, s, lag):
            return (back(cur, 0), s - lag) if s >= lag else (back(cur, 1), s - lag + B)

        def chunks(t):
            return t[:].rearrange("p a (c t) -> p (a c) t", t=CW)

        def head_steps(eng, step):
            for i in range(TURN):
                step(i, i)
            with eng.Fori(1, HEADS // TURN) as g:
                for u in range(TURN):
                    step(g * TURN + u, u)
            for u in range(3):
                step(HEADS + u, u)

        def live(i, back):
            return not isinstance(i, int) or back <= i < HEADS + back

        def ring1(i, u):
            jobs = [("max", i, c) for c in range(len(CHUNKS))] if live(i, 0) else []
            if live(i, 1):
                jobs.insert(8, ("nT", i - 1, 0))
            first = (u + 1) % 2 if not isinstance(i, int) or i else 0
            return [(*job, (first + n) % 2) for n, job in enumerate(jobs)]

        def ring1_free(eng, i, jobs, n):
            if n < 2:
                kind, head, c = "max", i - 1, len(CHUNKS) - 2 + n
                if isinstance(head, int) and head < 0:
                    return
            else:
                kind, head, c, _ = jobs[n - 2]
            need(eng, p1_max if kind == "max" else nT_sb, 0, head, c + 1)

        def ring2(i, u):
            jobs = [("exp", i - 2, kt) for kt in range(NT)] if live(i, 2) else []
            if live(i, 3):
                jobs.insert(4, ("fin", i - 3, 0))
            first = (u + 1) % 2 if not isinstance(i, int) or i > 2 else 0
            return [(*job, (first + n) % 2) for n, job in enumerate(jobs)]

        def ring2_free(eng, i, jobs, n):
            if n < 2:
                kind, head, c = "exp", i - 3, NT - 2 + n
                if isinstance(head, int) and head < 0:
                    return
            else:
                kind, head, c, _ = jobs[n - 2]
            need(eng, p2_exp if kind == "exp" else osum_done, 0, head, c + 1)

        RING = [(s, kind, i) for s in range(B) for kind, i in (("qkt", 0), ("qkt", 1), ("pt", 0), ("pt", 1), ("o2", 0), ("o2", 1))]
        RING_LAG = {"qkt": 1, "pt": 2, "o2": 2}
        RING_FREE = {"qkt": qkt_sb, "pt": pt_sb, "o2": o2_sb}

        def bank_of(s, kind, i):
            return RING.index((s, kind, i)) % 3

        def ring_free(eng, cur, s, kind, i):
            at = RING.index((s, kind, i))
            for places in range(3, 3 * len(RING), 3):
                gone, j = divmod(len(RING) - 1 - at + places, len(RING))
                slot, kind_j, i_j = RING[len(RING) - 1 - j]
                lag = RING_LAG[kind_j]
                tile = back(cur, gone + (slot < lag))
                if tile is not None:
                    need(eng, RING_FREE[kind_j], *tile, 2 * ((slot - lag) % B) + i_j + 1)
                    return

        SHARED = [("v", 0, 0, v_sb), ("g", 0, 2, gelu_done), ("g", 1, 2, gelu_done), ("g", 2, 2, gelu_done),
                  ("v", 1, 0, v_sb), ("a", 0, 2, glu_done), ("a", 1, 2, glu_done), ("a", 2, 2, glu_done),
                  ("w2", 0, 2, yo_done),
                  ("v", 2, 0, v_sb), ("wo", 0, 1, y1_done), ("mean", 0, 1, hc_done),
                  ("v", 3, 0, v_sb), ("var", 0, 1, lnv_done)]

        def shared_free(eng, cur, name, number=0):
            at = [job[:2] for job in SHARED].index((name, number))
            for places in range(1, 3 * len(SHARED)):
                gone, j = divmod(len(SHARED) - 1 - at + places, len(SHARED))
                _, number_j, d, frees = SHARED[len(SHARED) - 1 - j]
                tile = back(cur, gone + d)
                if tile is not None:
                    need(eng, frees, *tile, number_j + 1)
                    return

        block = ctx.enter_context(nc.Block())

        def turn_at(i, u, per, first):
            if isinstance(i, int):
                return (i // TURN) * per + first
            return (i - u) * (per // TURN) + first

        @block.sync
        def _(sp):
            sp.dma_start(identf[:], identf_d).then_inc(const_in, 16)
            sp.dma_start(identb[:], identb_d).then_inc(const_in, 16)
            sp.dma_start(mask[:], bandmask).then_inc(const_in, 16)
            sp.dma_start(ropec[:], rope_cos).then_inc(const_in, 16)
            sp.dma_start(ropes[:], rope_sin).then_inc(const_in, 16)
            sp.dma_start(causal_s[:], causal).then_inc(const_in, 16)
            with sp.Fori(0, NT // 2) as i:
                for u in range(2):
                    sp.wait_ge(xt_ps, 2 * i + u + 1)
                    sp.dma_start(prT[:, u, 0:B, :], x[:, bass.ds((2 * i + u) * P, P), :].rearrange("b p d -> p b d")).then_inc(x_in[u], 16)

            def load_attention(lay):
                l = lay % DEPTH
                if lay == DEPTH:
                    sp.wait_ge(w_ps, NT)
                need(sp, v_ps, lay, 0, 0)
                need(sp, qk_ps, lay, 0, 0)
                sp.dma_start(wqkv_s[:], wqkv[l]).then_inc(wqkv_in, 16)
                need(sp, tab_scaled, lay, 0, 0)
                sp.dma_start(scl[:], qkscale[l]).then_inc(scl_in, 16)

            def load_wo(lay):
                need(sp, wo_ps, lay, 0, 0)
                sp.dma_start(wo_s[:], wo[lay % DEPTH].rearrange("(j p) n -> p j n", p=P)).then_inc(wo_in, 16)

            def load_mlp(lay):
                l = lay % DEPTH
                need(sp, a_ps, lay, 0, 0)
                sp.dma_start(w1_s[:], w1[l]).then_inc(w1_in, 16)
                need(sp, w2_ps, lay, 0, 0)
                sp.dma_start(w2_s[:, 0:2, :], w2[l, 0:2 * P, :].rearrange("(j p) n -> p j n", p=P)).then_inc(w2_in, 16)
                sp.dma_start(w2_s[0:CHN[2], 2, :], w2[l, 2 * P:HID, :]).then_inc(w2_in, 16)
                need(sp, yo_done, lay, 0, 0)
                sp.dma_start(cols_s[:], cols[l]).then_inc(w2_in, 16)

            def step(cur):
                layer0, lay, n = cur
                if lay > layer0 and lay < layer0 + DEPTH and isinstance(n, int) and n == 0:
                    load_attention(lay)
                for s in range(B):
                    if back(cur, 0) is not None:
                        tile = back(cur, 0)
                        need(sp, v_sb, *tile, s + 1)
                        sp.dma_start(vprev[WIN:P, s, :], vown[0:WIN, s, :]).then_inc(v_hi[s].sem, 16)
                    tile, b = item(cur, s, 2)
                    if tile is not None:
                        need(sp, o2_ps, *tile, 2 * b + 2)
                        sp.dma_start(vprev[0:WIN, b, :], vown[WIN:P, b, :]).then_inc(v_lo[b].sem, 16)
                if lay > layer0 and lay < layer0 + DEPTH and isinstance(n, int) and n < 2:
                    (load_wo, load_mlp)[n](lay)

            sp.wait_ge(memsets, N_MEMSET)
            for b in range(B):
                sp.dma_start(vprev[0:WIN, b, :], vown[WIN:P, b, :]).then_inc(v_lo[b].sem, 16)
            load_attention(0)
            load_wo(0)
            load_mlp(0)
            steps(sp, step, 0)

            need(sp, v_ps, DEPTH, 0, 0)
            need(sp, yo_done, DEPTH, 0, 0)
            sp.dma_start(gw_s, gw.rearrange("w p n -> p w n")).then_inc(gw_in, 16)
            sp.dma_start(gcos, g_cos).then_inc(gw_in, 16)
            sp.dma_start(gsin, g_sin).then_inc(gw_in, 16)
            for u in range(TURN):
                sp.dma_start(kst[3 * 3 * GD:STACK, u, :], stack_tail[0]).then_inc(tail_in, 16)

            def store_parts(b):
                for u in range(2):
                    sp.wait_ge(gp1, 2 * b + u + 2)
                    sp.wait_ge(gp2, 2 * b + u + 2)
                    sp.wait_ge(gp3, 2 * b + u + 2)
                    for a in range(2):
                        for j in range(3):
                            sp.dma_start(scratch[a, bass.ds(b * GH, GH), j, :, u * CW:(u + 1) * CW],
                                         parts[u][:, a, j, :]).then_inc(gparts_out[u], 16)

            def load_stacks(i, u):
                if live(i, TURN):
                    need(sp, pv_ps, 0, i - TURN + 1, 0)
                src = scratch[0, bass.ds(i, 1), :, :, :].rearrange("o j d t -> (o j d) t").unsqueeze(0)
                sp.dma_start(qst[0:9 * GD, u, :], src.broadcast_to([3, 3 * GD, S])).then_inc(st_in[u], 16)
                sp.dma_start(qst[9 * GD:STACK, u, :], stack_tail[1]).then_inc(st_in[u], 16)
                for j in range(3):
                    sp.dma_start(kst[3 * GD * j:3 * GD * (j + 1), u, :],
                                 scratch[1, bass.ds(i, 1), j, :, :].broadcast_to([3, GD, S])).then_inc(st_in[u], 16)

            def store_max(i, u):
                need(sp, nT_sb, 0, i, 1)
                sp.dma_start(qst[9 * GD:9 * GD + 3, u, :], nT[:, u % 2, :]).then_inc(nT_in[u], 16)

            def head_step(i, u):
                if live(i, 0):
                    load_stacks(i, u)
                if live(i, 2):
                    store_max(i - 2, (u - 2) % TURN)

            store_parts(0)
            for u in range(2):
                sp.wait_ge(gparts_out[u], 96 * 2)
            for i in range(TURN):
                load_stacks(i, i)
            with sp.Fori(1, B) as b:
                store_parts(b)
            for u in range(2):
                sp.wait_ge(gparts_out[u], 96 * (B + 1))
            for i in range(TURN - 2):
                store_max(i, i)
            with sp.Fori(1, HEADS // TURN) as g:
                for u in range(TURN):
                    head_step(g * TURN + u, u)
            for i in range(HEADS, HEADS + 2):
                head_step(i, i % TURN)

            load_attention(DEPTH)
            load_wo(DEPTH)
            load_mlp(DEPTH)
            steps(sp, step, DEPTH)
            with sp.Fori(0, NT // 2) as i:
                for u in range(2):
                    sp.wait_ge(o_sb, 2 * i + u + 3)
                    sp.dma_start(out[:, bass.ds((2 * i + u) * P, P), :].rearrange("b p d -> p b d"), pr[:, u, 0:B, :]).then_inc(o_out[u], 16)
            for u in range(2):
                sp.wait_ge(o_out[u], 16 * (NT // 2 + 1))

        @block.tensor
        def _(pe):
            for c in credits["tensor"]:
                pe.sem_inc(c.sem, 1)
            pe.wait_ge(const_in, 96)
            pe.wait_ge(memsets, N_MEMSET)
            with pe.Fori(0, NT // 2) as i:
                for u in range(2):
                    pe.wait_ge(x_in[u], 16 * i + 16)
                    pe.wait_ge(xt_sb, 2 * i + u + 1)
                    for b in range(B):
                        last = pe.transpose(ps_qk[:, u, b * P:(b + 1) * P], prT[:, u, b, :], identf[:])
                    last.then_inc(xt_ps, 1)

            def norm(k, src):
                with pe.Fori(0, BLOCKS // 4) as i:
                    for u in range(4):
                        pe.wait_ge(n_cen, 1 + k * BLOCKS + 4 * i)
                        pe.matmul((ps_qk, ps_s)[u // 2][:, u % 2, :], ones[:], src[:, bass.ds((4 * i + u) * CW, CW)],
                                  start=True, stop=True).then_inc(n_mean, 1)
                    for u in range(4):
                        pe.wait_ge(n_sq, k * BLOCKS + 4 * i + u + 1)
                        pe.matmul(psr[:, u, :], ones[:], chunks(t1)[:, u, :], start=True, stop=True).then_inc(n_var, 1)

            xf = xT[:, :, :].rearrange("p b t -> p (b t)")

            def step(cur):
                tile0, tile1, tile2 = (back(cur, d) for d in range(3))

                def project_v(s):
                    shared_free(pe, cur, "v", s)
                    pe.matmul(psm[:], hs[:, s, :], wqkv_s[:, 2 * INNER:], start=True, stop=True).then_inc(v_ps.sem, 1)

                def project_qk(s):
                    if s == 0:
                        if isinstance(tile0[1], int) and tile0[1] == 0:
                            pe.wait_ge(wqkv_in, 16 * (tile0[0] + 1))
                        need(pe, hs_ready, *tile0, 2)
                    need(pe, qkn_done, *tile0, s)
                    for j in range(2):
                        last = pe.matmul(ps_qk[:, j, :], hs[:, s, :], wqkv_s[:, j * INNER:(j + 1) * INNER],
                                         start=True, stop=True)
                    last.then_inc(qk_ps.sem, 1)

                def turn_qk(s):
                    tile, b = item(cur, s, 1)
                    if tile is None:
                        return
                    for j in range(2):
                        need(pe, (rot_done, rotk_done)[j], *tile, b + 1)
                        ring_free(pe, cur, s, "qkt", j)
                        for i in range(PAIRS):
                            last = pe.transpose(psr[:, bank_of(s, "qkt", j), i * P:(i + 1) * P],
                                                t1[:, b % 2, j * INNER + i * P:j * INNER + (i + 1) * P], identf[:])
                        last.then_inc(qkt_ps.sem, 1)

                def scores(s):
                    tile, b = item(cur, s, 1)
                    if tile is None:
                        return
                    need(pe, exp_done, *tile, b)
                    for j in range(PAIRS):
                        pe.matmul(ps_s[:, j // 2, (j % 2) * 2 * P:(j % 2 + 1) * 2 * P], identb[:],
                                  mask[:, bass.ds(2 * tile[1], 2), :], start=(j % 2 == 0), stop=False, skip_group_check=True)
                    need(pe, qkt_sb, *tile, 2 * b + 2)
                    for j in range(PAIRS):
                        for w in range(2):
                            last = pe.matmul(ps_s[:, j // 2, ((j % 2) * 2 + w) * P:((j % 2) * 2 + w + 1) * P],
                                             qbd[:, b % 2, j, w, :], kT[:, b, j, w * WIN:w * WIN + P],
                                             start=False, stop=(j % 2 == 1 and w == 1), skip_group_check=True)
                    last.then_inc(s_ps.sem, 1)

                def turn_probs(s):
                    tile, b = item(cur, s, 2)
                    if tile is None:
                        return
                    for h in range(2):
                        need(pe, p_norm, *tile, 2 * b + h + 1)
                        ring_free(pe, cur, s, "pt", h)
                        for i in range(4):
                            last = pe.transpose(psr[:, bank_of(s, "pt", h), i * P:(i + 1) * P], pr[:, b % 2, 4 * h + i, :],
                                                identf[:])
                        last.then_inc(pt_ps.sem, 1)

                def weigh_values(s):
                    tile, b = item(cur, s, 2)
                    if tile is None:
                        return
                    need(pe, v_lo[b], *tile, 1)
                    need(pe, v_hi[b], *tile, 1)
                    for h in range(2):
                        ring_free(pe, cur, s, "o2", h)
                        need(pe, pt_sb, *tile, 2 * b + h + 1)
                        for i in range(4):
                            u = 4 * h + i
                            v = (vprev, vown)[u % 2]
                            last = pe.matmul(psr[:, bank_of(s, "o2", h), i * P:(i + 1) * P], v[:, b, (u // 2) * P:(u // 2 + 1) * P],
                                             prT[:, b % 2, u, :], start=True, stop=True)
                        last.then_inc(o2_ps.sem, 1)

                def gate(j):
                    if tile2 is None:
                        return
                    if j == 0:
                        pe.wait_ge(w1_in, 16 * (tile2[0] + 1))
                        need(pe, hn_done, *tile2, 2)
                    shared_free(pe, cur, "g", j)
                    pe.matmul(psm[0:CHN[j], :], w1_s[:, HID + j * P:HID + j * P + CHN[j]], hn[:],
                              start=True, stop=True).then_inc(g_ps.sem, 1)

                def linear(j):
                    if tile2 is None:
                        return
                    shared_free(pe, cur, "a", j)
                    pe.matmul(psm[0:CHN[j], :], w1_s[:, j * P:j * P + CHN[j]], hn[:],
                              start=True, stop=True).then_inc(a_ps.sem, 1)

                def out_mlp():
                    if tile2 is None:
                        return
                    pe.wait_ge(w2_in, 48 * (tile2[0] + 1))
                    shared_free(pe, cur, "w2")
                    for j in range(CH):
                        last = pe.matmul(psm[:], w2_s[0:CHN[j], j, :], act_t[0:CHN[j], j, :], start=(j == 0), stop=(j == CH - 1))
                    last.then_inc(w2_ps.sem, 1)

                def out_attention():
                    if tile1 is None:
                        return
                    pe.wait_ge(wo_in, 16 * (tile1[0] + 1))
                    need(pe, o2_sb, *tile1, 2 * B)
                    shared_free(pe, cur, "wo")
                    for j in range(PAIRS):
                        last = pe.matmul(psm[:], wo_s[:, j, :], oT[:, j, :, :], start=(j == 0), stop=(j == PAIRS - 1))
                    last.then_inc(wo_ps.sem, 1)

                def mean():
                    if tile1 is None:
                        return
                    need(pe, h1_done, *tile1, 2)
                    shared_free(pe, cur, "mean")
                    pe.matmul(psm[:], ones[:], h1[:], start=True, stop=True).then_inc(mean_ps.sem, 1)

                def variance():
                    if tile1 is None:
                        return
                    need(pe, hq_done, *tile1, 1)
                    shared_free(pe, cur, "var")
                    pe.matmul(psm[:], ones[:], hq[:], start=True, stop=True).then_inc(var_ps.sem, 1)

                for s in range(B):
                    if tile0 is not None:
                        project_qk(s)
                        project_v(s)
                    turn_qk(s)
                    if s == 0:
                        gate(0)
                    if s == 1:
                        linear(0)
                    if s == 2:
                        out_attention()
                    turn_probs(s)
                    if s == 0:
                        gate(1)
                    if s == 1:
                        linear(1)
                    if s == 3:
                        variance()
                    scores(s)
                    if s == 0:
                        gate(2)
                    if s == 1:
                        linear(2)
                    weigh_values(s)
                    if s == 1:
                        out_mlp()
                    if s == 2:
                        mean()

            pe.wait_ge(xt_sb, NT + 2)
            norm(0, xf)
            steps(pe, step, 0)
            need(pe, yo_done, DEPTH, 0, 0)
            norm(1, xf)

            pe.wait_ge(gw_in, 48)
            with pe.Fori(0, B) as b:
                for u in range(2):
                    z = y_in[:, bass.ds(b, 1), 1 + u * CW:1 + (u + 1) * CW].rearrange("p a t -> p (a t)")
                    pe.wait_ge(n_out, 1 + 2 * BLOCKS)
                    pe.wait_ge(grot, 2 * (2 * b + u) + 1)
                    for j in range(2):
                        last = pe.matmul(ps_qk[:, j, :], gw_s[:, j, :], z, start=True, stop=True)
                    last.then_inc(gqk_ps, 1)
                    pe.wait_ge(grot, 2 * (2 * b + u) + 2)
                    for j in range(2):
                        last = pe.matmul(ps_s[:, j, :], gw_s[:, 2 + j, :], z, start=True, stop=True)
                    last.then_inc(gqk_ps, 1)
                for u in range(2):
                    pe.wait_ge(gz_done, 2 * b + u + 1)
                    pe.wait_ge(gv_sb, 2 * b + u + 1)
                    for i in range(4):
                        last = pe.matmul(psr[:, u, i * P:(i + 1) * P], zs[u][:, i * P:(i + 1) * P], gw_s[:, 4, :],
                                         start=True, stop=True)
                    last.then_inc(gv_ps, 1)

            pe.wait_ge(tail_in, 16 * TURN)
            pe.wait_ge(gv_sb, 2 * B + 2)
            pe.wait_ge(grot, 4 * B + 2)

            def max_job(i, u, c, bank):
                t, half = CHUNKS[c]
                lo, hi = half * 512, min((t + 1) * P, (half + 1) * 512)
                diag = hi == (t + 1) * P
                last = pe.matmul(psr[:, bank, 0:hi - lo], qst[0:STACK, u, t * P:(t + 1) * P], kst[0:STACK, u, lo:hi],
                                 start=True, stop=not diag)
                if diag:
                    last = pe.matmul(psr[:, bank, hi - lo - P:hi - lo], identb[:], causal_s[:, 0, :], start=False, stop=True)
                last.then_inc(p1_ps.sem, 1)

            def exp_job(i, u, kt, bank):
                if kt == 0:
                    pe.wait_ge(nT_in[u], turn_at(i, u, 16, 16))
                where = (ps_qk, ps_s)[bank]
                n = S - kt * P
                for lo in range(0, n, 512):
                    hi = min(n, lo + 512)
                    last = pe.matmul(where[:, lo // 512, 0:hi - lo], kst[0:STACK, u, kt * P:(kt + 1) * P],
                                     qst[0:STACK, u, kt * P + lo:kt * P + hi], start=True, stop=lo > 0)
                    if lo == 0:
                        last = pe.matmul(where[:, 0, 0:P], identb[:], causal_s[:, 1, :], start=False, stop=True)
                last.then_inc(p2_ps.sem, 1)

            def products(i, u, part, half):
                if part == 0 and half == 0:
                    need(pe, vh_done, 0, i, 1)
                    pe.wait_ge(zero_done, 1)
                    need(pe, acc_done, 0, i, 0)
                need(pe, p2_exp, 0, i, 4 * part + 4)
                for kt in range(4 * part, 4 * part + 4):
                    lo = max(kt * P, half * 512)
                    c = kt % 4
                    last = pe.matmul(acc[32 * c:32 * c + VW, half, lo - half * 512:512], vh[:, u % 2, kt, :],
                                     pT[kt][:, lo - kt * P:(half + 1) * 512 - kt * P],
                                     start=(part == 0), stop=(part == 1 or half == 0), skip_group_check=True)
                if half == 1:
                    last.then_inc(pv_ps.sem, 1)

            ORDER = "m0 e0 m1 e1 m2 p11 m3 e2 m4 e3 m5 m6 e4 m7 p00 m8 e5 m9 p01 e6 m10 e7 m11 e8 m12".split()

            LAST_ORDER = ["p11", "e0"]

            def head_step(i, u):
                jobs1, jobs2 = ring1(i, u), ring2(i, u)
                if live(i, 0):
                    pe.wait_ge(st_in[u], turn_at(i, u, 80, 80))
                only_last = live(i, 3) and not live(i, 2)
                for kind_n in LAST_ORDER if only_last else ORDER:
                    n = int(kind_n[1:])
                    if kind_n[0] == "m" and n < len(jobs1):
                        kind, head, c, bank = jobs1[n]
                        ring1_free(pe, i, jobs1, n)
                        if kind == "max":
                            max_job(head, u, c, bank)
                        else:
                            need(pe, n3_done, 0, head, 1)
                            pe.transpose(psr[0:3 * NT, bank, 0:P // 2].bitcast(BF16),
                                         nparts[:, (u - 1) % 2, :, :].rearrange("p j t -> p (j t)"),
                                         identb[:]).then_inc(nT_ps.sem, 1)
                    if kind_n[0] == "e" and n < len(jobs2):
                        kind, head, c, bank = jobs2[n]
                        ring2_free(pe, i, jobs2, n)
                        if kind == "fin":
                            need(pe, acc_done, 0, head, 1)
                            where = (ps_qk, ps_s)[bank]
                            for t in range(NT):
                                last = pe.transpose(where[:, t // 4, (t % 4) * P:(t % 4 + 1) * P],
                                                    acc_sb[:, t * P:(t + 1) * P], identf[:])
                            last.then_inc(fin_ps.sem, 1)
                        else:
                            exp_job(head, (u - 2) % TURN, c, bank)
                    if kind_n == "p11" and live(i, 3):
                        products(i - 3, (u - 3) % TURN, 1, 1)
                    elif kind_n[0] == "p" and n < 10 and live(i, 2):
                        products(i - 2, (u - 2) % TURN, 0, n)
            head_steps(pe, head_step)

            with pe.Fori(0, NT // 2) as i:
                for u in range(2):
                    pe.wait_ge(w_stage, 2 * i + u + 1)
                    pe.wait_ge(w_tsb, 2 * i + u + 1)
                    for b in range(B):
                        last = pe.transpose(ps_qk[:, u, b * P:(b + 1) * P], t1[:, u, b * P:(b + 1) * P], identf[:])
                    last.then_inc(w_tps, 1)
                    pe.wait_ge(w_tsb, 2 * i + u + 3)
                    pe.wait_ge(w_done, 2 * i + u + 1)
                    pe.matmul(ps_s[:, u, :], gw_s[:, 5, :], t2[:, u, 0:CW], start=True, stop=True).then_inc(w_ps, 1)

            pe.wait_ge(w_done, NT + 2)
            norm(2, xf)
            pe.wait_ge(qbd_zero, 1)
            steps(pe, step, DEPTH)
            with pe.Fori(0, NT // 2) as i:
                for u in range(2):
                    pe.wait_ge(o_stage, 2 * i + u + 1)
                    pe.wait_ge(o_sb, 2 * i + u + 1)
                    for b in range(B):
                        last = pe.transpose(ps_qk[:, u, b * P:(b + 1) * P], prT[:, u, b, :], identf[:])
                    last.then_inc(o_ps, 1)

        @block.vector
        def _(dve):
            for c in credits["vector"]:
                dve.sem_inc(c.sem, 1)
            dve.sem_inc(n_cen, 1)
            dve.sem_inc(n_out, 1)
            for buf in (qbd[:], kT[:], vown[:], vprev[:]):
                dve.memset(buf, 0.0).then_inc(memsets, 1)
            dve.memset(ones[:], 1.0 / P).then_inc(memsets, 1)
            dve.memset(eps[:], LN_EPS).then_inc(memsets, 1)
            for y in (y_in, y_att, y_mid):
                dve.memset(y[:, :, 0:1], 0.0).then_inc(memsets, 1)
            dve.memset(w2_s[:, 2, :], 0.0).then_inc(memsets, 1)
            dve.memset(hs[:], 0.0).then_inc(memsets, 1)
            dve.memset(vh[:, :, :, GD:VW], 1.0).then_inc(memsets, 1)
            dve.wait_ge(memsets, N_MEMSET)
            dve.wait_ge(const_in, 96)

            def norm(k, src, dst):
                done = 1 + k * BLOCKS
                with dve.Fori(0, BLOCKS // 4) as i:
                    for u in range(4):
                        dve.wait_ge(n_mean, k * BLOCKS + 4 * i + u + 1)
                        dve.wait_ge(n_out, done + 4 * i)
                        dve.tensor_tensor(chunks(qkn)[:, u, :], src[:, bass.ds((4 * i + u) * CW, CW)],
                                          (ps_qk, ps_s)[u // 2][:, u % 2, :], ALU.subtract).then_inc(n_cen, 1)
                    for u in range(4):
                        dve.wait_ge(n_rstd, k * BLOCKS + 4 * i + u + 1)
                        dve.wait_ge(n_cen, done + 4 * i + u + 1)
                        dve.tensor_tensor(dst[:, bass.ds(2 * i + u // 2, 1), 1 + (u % 2) * CW:1 + (u % 2 + 1) * CW].rearrange("p a t -> p (a t)"),
                                          chunks(qkn)[:, u, :], chunks(t2)[:, u, :], ALU.mult).then_inc(n_out, 1)

            def stage(lay, n):
                y = (y_in, y_mid)[lay % DEPTH]
                dve.wait_ge(v_ps.sem, v_ps.at(lay, n, 0))
                need(dve, qk_ps, lay, n, 0)
                if isinstance(n, int):
                    if lay % DEPTH:
                        need(dve, yo_done, lay - 1, n, 2)
                    else:
                        dve.wait_ge(n_out, 1 + BLOCKS * (2 * (lay // DEPTH) + 1))
                dve.tensor_copy(hs[0:64, :, :], y[0:64, :, bass.ds(n * P + 1, P)]).then_inc(hs_ready.sem, 1)
                dve.tensor_copy(hs[64:P, :, :], y[64:P, :, bass.ds(n * P, P)]).then_inc(hs_ready.sem, 1)

            def scale_tables(lay, n):
                dve.wait_ge(scl_in, 16 * (lay + 1))
                need(dve, t1_done, lay, n, 0)
                need(dve, t2_done, lay, n, 0)
                for i, tab in enumerate((ropec, ropes)):
                    dve.tensor_tensor(rope_n[:, i, :, :], tab[:, bass.ds(n, 1), :, :].rearrange("p o a d -> p (o a) d"),
                                      scl[:, i, :, :], ALU.mult).then_inc(tab_scaled.sem, 1)

            def step(cur):
                ahead, tile0, tile1, tile2 = (back(cur, d) for d in range(-1, 3))

                def sum_reciprocals(s):
                    tile, b = item(cur, s, 2)
                    if tile is None:
                        return
                    need(dve, exp_done, *tile, b + 1)
                    dve.tensor_reduce(psum_e[:, b % 2, 0, :], pr[:, b % 2, :, :], axis=AX, op=ALU.add).then_inc(esum_done.sem, 1)
                    need(dve, esum_done, *tile, b + 1)
                    need(dve, p_norm, *tile, 2 * (b - 1))
                    dve.reciprocal(psum_e[:, b % 2, 1, :], psum_e[:, b % 2, 0, :]).then_inc(rsum_done.sem, 1)

                def carry_keys(s):
                    tile, b = item(cur, s, 1)
                    if tile is None:
                        return
                    need(dve, s_ps, *tile, b - 3)
                    need(dve, qkt_sb, *tile, 2 * (b - B) + 2)
                    dve.tensor_copy(kT[:, b, :, 0:WIN], kT[:, b, :, P:P + WIN]).then_inc(k_carry.sem, 1)

                def squares(s):
                    need(dve, sq_done, *tile0, s + 1)
                    dve.tensor_reduce(ss[:], sqk[:].rearrange("p (h d) -> p h d", d=FD), axis=AX,
                                      op=ALU.add).then_inc(ss_red.sem, 1)
                    need(dve, ss_red, *tile0, s + 1)
                    dve.tensor_scalar(ssc[:], ss[:], 1e-24, None, ALU.max).then_inc(ss_clamp.sem, 1)
                    need(dve, ss_clamp, *tile0, s + 1)
                    dve.tensor_scalar(rn[:, 0, :].bitcast(I32), ssc[:].bitcast(I32), -0.5, float(ROOT_BITS), ALU.mult,
                                      ALU.add).then_inc(rn_guess.sem, 1)

                def newton(s, k):
                    if k == 0:
                        need(dve, rn_guess, *tile0, s + 1)
                    else:
                        need(dve, rn_step, *tile0, 9 * s + 3 * k)
                    dve.tensor_tensor(nw[:, 0, :], rn[:, k, :], rn[:, k, :], ALU.mult).then_inc(rn_step.sem, 1)
                    need(dve, rn_step, *tile0, 9 * s + 3 * k + 1)
                    dve.scalar_tensor_tensor(out=nw[:, 1, :], in0=nw[:, 0, :], scalar=-0.5, in1=ssc[:],
                                             op0=ALU.mult, op1=ALU.mult).then_inc(rn_step.sem, 1)
                    need(dve, rn_step, *tile0, 9 * s + 3 * k + 2)
                    dve.scalar_tensor_tensor(out=rn[:, k + 1, :], in0=nw[:, 1, :], scalar=1.5, in1=rn[:, k, :],
                                             op0=ALU.add, op1=ALU.mult).then_inc(rn_step.sem, 1)

                def normalise(s):
                    u = s % 2
                    need(dve, rn_step, *tile0, 9 * s + 9)
                    need(dve, t2_done, *tile0, 2 * s - 2)
                    need(dve, t1_done, *tile0, s - 1)
                    dve.tensor_tensor(qkn[:, u, :].rearrange("p (h d) -> p h d", d=FD),
                                      ps_qk[:].rearrange("p a (h d) -> p (a h) d", d=FD),
                                      rn[:, 3, :].unsqueeze(2).broadcast_to([P, 2 * FH, FD]),
                                      ALU.mult).then_inc(qkn_done.sem, 1)

                def rope_cosines(s):
                    u = s % 2
                    need(dve, qkn_done, *tile0, s + 1)
                    need(dve, tab_scaled, *tile0, 2)
                    need(dve, qkt_ps, *tile0, 2 * (s - 2) + 2)
                    dve.tensor_tensor(t1[:, u, :].rearrange("p (a h d) -> p a h d", a=2, d=FD),
                                      qkn[:, u, :].rearrange("p (a h d) -> p a h d", a=2, d=FD),
                                      rope_n[:, 0, :, :].unsqueeze(2).broadcast_to([P, 2, FH, FD]),
                                      ALU.mult).then_inc(t1_done.sem, 1)

                def rope_sum(s):
                    u = s % 2
                    need(dve, t2_done, *tile0, 2 * s + 2)
                    need(dve, t1_done, *tile0, s + 1)
                    dve.tensor_tensor(t1[:, u, 0:INNER], t1[:, u, 0:INNER], t2[:, u, 0:INNER], ALU.add).then_inc(rot_done.sem, 1)

                def maxima(s):
                    tile, b = item(cur, s, 1)
                    if tile is None:
                        return
                    need(dve, s_ps, *tile, b + 1)
                    need(dve, exp_done, *tile, b - 1)
                    dve.tensor_reduce(nmax[:, b % 2, :], ps_s[:].rearrange("p a (u k) -> p (a u) k", k=P), axis=AX,
                                      op=ALU.max, negate=True).then_inc(max_done.sem, 1)

                def gated(j):
                    if tile2 is None:
                        return
                    need(dve, a_ps, *tile2, j + 1)
                    need(dve, gelu_done, *tile2, j + 1)
                    dve.scalar_tensor_tensor(out=act_t[0:CHN[j], j, :], in0=psm[0:CHN[j], :],
                                             scalar=cols_s[0:CHN[j], j:j + 1], in1=gel[0:CHN[j], j, :],
                                             op0=ALU.add, op1=ALU.mult).then_inc(glu_done.sem, 1)

                def layer_out():
                    if tile2 is None:
                        return
                    lay, m = tile2
                    need(dve, w2_ps, lay, m, 1)
                    pv = psm[:].rearrange("p (b t) -> p b t", b=B)
                    mid = y_att[:, :, bass.ds(m * P + 1, P)]
                    if lay % DEPTH == 0:
                        dve.scalar_tensor_tensor(out=y_mid[:, :, bass.ds(m * P + 1, P)], in0=pv, scalar=cols_s[:, 8:9],
                                                 in1=mid, op0=ALU.add, op1=ALU.add).then_inc(yo_done.sem, 2)
                        return
                    hv = hc[:].rearrange("p (b t) -> p b t", b=B)
                    dve.scalar_tensor_tensor(out=hv, in0=pv, scalar=cols_s[:, 8:9], in1=mid,
                                             op0=ALU.add, op1=ALU.add).then_inc(yo_done.sem, 1)
                    need(dve, yo_done, lay, m, 1)
                    xv = xT[:, :, bass.ds(m * P, P)]
                    dve.scalar_tensor_tensor(out=xv, in0=hv, scalar=0.5, in1=xv, op0=ALU.mult,
                                             op1=ALU.add).then_inc(yo_done.sem, 1)

                def attention_out():
                    if tile1 is None:
                        return
                    lay, m = tile1
                    y = (y_in, y_mid)[lay % DEPTH]
                    need(dve, wo_ps, lay, m, 1)
                    dve.tensor_tensor(y_att[:, :, bass.ds(m * P + 1, P)], psm[:].rearrange("p (b t) -> p b t", b=B),
                                      y[:, :, bass.ds(m * P + 1, P)], ALU.add).then_inc(y1_done.sem, 1)
                    need(dve, y1_done, lay, m, 1)
                    h1v = h1[:].rearrange("p (b t) -> p b t", b=B)
                    dve.tensor_scalar(h1v[0:64, :, :], y_att[0:64, :, bass.ds(m * P + 1, P)], 1.0, None, ALU.mult).then_inc(h1_done.sem, 1)
                    dve.tensor_copy(h1v[64:P, :, :], y_att[64:P, :, bass.ds(m * P, P)]).then_inc(h1_done.sem, 1)

                def centre():
                    if tile1 is None:
                        return
                    need(dve, mean_ps, *tile1, 1)
                    need(dve, h1_done, *tile1, 2)
                    dve.tensor_tensor(hc[:], h1[:], psm[:], ALU.subtract).then_inc(hc_done.sem, 1)

                def layer_norm():
                    if tile1 is None:
                        return
                    need(dve, rstd_done, *tile1, 1)
                    need(dve, hc_done, *tile1, 1)
                    dve.tensor_tensor(hc[:], hc[:], rstd[:], ALU.mult).then_inc(hn_done.sem, 1)
                    need(dve, hn_done, *tile1, 1)
                    dve.wait_ge(w2_in, 48 * (tile1[0] + 1))
                    dve.tensor_scalar(hn[:], hc[:], cols_s[:, 6:7], cols_s[:, 7:8], ALU.mult,
                                      ALU.add).then_inc(hn_done.sem, 1)

                for s in range(B):
                    sum_reciprocals(s)
                    carry_keys(s)
                    if tile0 is not None:
                        squares(s)
                        newton(s, 0)
                    if s == 0 and tile0 is not None:
                        scale_tables(*tile0)
                    if s == 1:
                        gated(0)
                    if tile0 is not None:
                        newton(s, 1)
                        newton(s, 2)
                        normalise(s)
                    if s == 1:
                        gated(1)
                    if s == 2:
                        attention_out()
                    if s == 3 and ahead is not None:
                        stage(*ahead)
                    maxima(s)
                    if s == 1:
                        gated(2)
                    if tile0 is not None:
                        rope_cosines(s)
                        rope_sum(s)
                    if s == 1:
                        layer_out()
                    if s == 2:
                        centre()
                    if s == 3:
                        layer_norm()

            xf = xT[:, :, :].rearrange("p b t -> p (b t)")
            dve.wait_ge(xt_sb, NT + 2)
            norm(0, xf, y_in)
            stage(0, 0)
            steps(dve, step, 0)
            norm(1, xf, y_in)

            def stage_z(b, u):
                dve.wait_ge(n_out, 1 + 2 * BLOCKS)
                dve.tensor_copy(zs[u].unsqueeze(1), y_in[:, bass.ds(b, 1), 1 + u * CW:1 + (u + 1) * CW]).then_inc(gz_done, 1)

            dve.memset(acc, 0.0).then_inc(zero_done, 1)

            dve.wait_ge(gw_in, 48)
            v3 = lambda t, u: t[:, u, :].rearrange("p (a t) -> p a t", a=2)
            with dve.Fori(0, B) as b:
                for u in range(2):
                    both = lambda t: t[:, u * CW:(u + 1) * CW].unsqueeze(1).broadcast_to([P, 2, CW])
                    dve.wait_ge(gqk_ps, 2 * (2 * b + u) + 1)
                    dve.wait_ge(gp3, 2 * b + 1)
                    dve.tensor_tensor(v3(t1, u), ps_qk[:], both(gcos), ALU.mult).then_inc(grot, 1)
                    dve.wait_ge(gqk_ps, 2 * (2 * b + u) + 2)
                    dve.tensor_tensor(v3(t2, u), ps_s[:], both(gsin), ALU.mult).then_inc(grot, 1)
                    dve.wait_ge(gv_ps, 2 * b + u + 1)
                    stage_z(b, u)
                for u in range(2):
                    dve.wait_ge(gp1, 2 * b + u + 2)
                    dve.tensor_tensor(v3(t2, u), v3(t1, u), parts[u][:, :, 0, :], ALU.subtract).then_inc(gr1, 1)
                for u in range(2):
                    dve.wait_ge(gv_ps, 2 * b + u + 3)
                    dve.tensor_scalar(
                        v_all[:, bass.ds(b * S, S)].rearrange("p (h t d) -> p t h d", h=GH, t=NT)[:, 4 * u:4 * u + 4, :, :],
                        psr[:, u, :].rearrange("p (t h d) -> p t h d", t=4, d=GD), 1.0, None, ALU.mult).then_inc(gv_sb, 1)
                for u in range(2):
                    dve.wait_ge(gp2, 2 * b + u + 2)
                    dve.tensor_tensor(parts[u][:, :, 2, :], v3(t2, u), parts[u][:, :, 1, :], ALU.subtract).then_inc(gp3, 1)
            dve.wait_ge(gv_sb, 2 * B + 2)
            dve.wait_ge(gp3, 2 * B + 1)

            def head_step(i, u):
                if live(i, 2):
                    if live(i, 4):
                        need(dve, pv_ps, 0, i - 4, 2)
                    if live(i, 3):
                        need(dve, vh_done, 0, i - 3, 1)
                    dve.tensor_scalar(vh[:, u % 2, :, 0:GD], v_all[:, bass.ds((i - 2) * (NT * GD), NT * GD)].rearrange("p (t d) -> p t d", d=GD),
                                      1.0, None, ALU.mult).then_inc(vh_done.sem, 1)
                jobs1 = ring1(i, u)
                if len(jobs1) < 6 and live(i, 1):
                    for k in range(5):
                        split_maxima(i - 1, (u - 1) % 2, k)
                for n, (kind, head, c, bank) in enumerate(jobs1):
                    if kind == "max":
                        t, half = CHUNKS[c]
                        cols_n = min((t + 1) * P, (half + 1) * 512) - half * 512
                        need(dve, p1_ps, 0, head, c + 1)
                        if c == 0 and live(i, 2):
                            need(dve, r1_done, 0, head - 2, 1)
                        dve.tensor_reduce(nm[:, u % 2, half, t:t + 1], psr[:, bank, 0:cols_n], axis=AX, op=ALU.max,
                                          negate=True).then_inc(p1_max.sem, 1)
                        if n < 5 and live(i, 1):
                            split_maxima(i - 1, (u - 1) % 2, n)
                    else:
                        need(dve, nT_ps, 0, head, 1)
                        if live(i, 3):
                            dve.wait_ge(nT_in[(u - 3) % TURN], turn_at(i - 3, (u - 3) % TURN, 16, 16))
                        dve.tensor_copy(nT[:, (u - 1) % 2, :], psr[0:3 * NT, bank, 0:P // 2].bitcast(BF16)).then_inc(nT_sb.sem, 1)
                    if n == 7 and live(i, 3):
                        finish(i - 3, (u - 3) % 2, fin_bank(i, u))
                if len(jobs1) < 6 and live(i, 3):
                    finish(i - 3, (u - 3) % 2, fin_bank(i, u))

            def fin_bank(i, u):
                return [bank for kind, _, _, bank in ring2(i, u) if kind == "fin"][0]

            def split_maxima(head, k, op):
                if op == 0:
                    need(dve, p1_max, 0, head, len(CHUNKS))
                    dve.tensor_tensor(nm[:, k, 0, 4:NT], nm[:, k, 0, 4:NT], nm[:, k, 1, 4:NT], ALU.min).then_inc(nm_done.sem, 1)
                elif op == 1:
                    need(dve, nm_done, 0, head, 1)
                    if live(head, 2):
                        need(dve, nT_ps, 0, head - 1, 0)
                    dve.tensor_copy(nparts[:, k, 0, :], nm[:, k, 0, :]).then_inc(n1_done.sem, 1)
                elif op == 2:
                    need(dve, n1_done, 0, head, 1)
                    dve.tensor_tensor(nres[:, k, :], nm[:, k, 0, :], nparts[:, k, 0, :], ALU.subtract).then_inc(r1_done.sem, 1)
                elif op == 3:
                    need(dve, r1_done, 0, head, 1)
                    dve.tensor_copy(nparts[:, k, 1, :], nres[:, k, :]).then_inc(n2_done.sem, 1)
                else:
                    need(dve, n2_done, 0, head, 1)
                    dve.tensor_tensor(nparts[:, k, 2, :], nres[:, k, :], nparts[:, k, 1, :], ALU.subtract).then_inc(n3_done.sem, 1)

            def finish(head, k, bank):
                where = (ps_qk, ps_s)[bank]
                need(dve, fin_ps, 0, head, 1)
                need(dve, o_done, 0, head, 0)
                dve.tensor_reduce(osum[:, k, :, :],
                                  where[:].rearrange("p a (t c w) -> p (a t) w c", c=4, w=32)[:, :, 0:VW, :], axis=AX,
                                  op=ALU.add).then_inc(osum_done.sem, 1)
                need(dve, osum_done, 0, head, 1)
                dve.reciprocal(orec[:, k, :], osum[:, k, :, GD]).then_inc(orec_done.sem, 1)
                need(dve, orec_done, 0, head, 1)
                dve.tensor_tensor(o_all[:, bass.ds(head * (NT * GD), NT * GD)].rearrange("p (t d) -> p t d", d=GD),
                                  osum[:, k, :, 0:GD], orec[:, k, :].unsqueeze(2).broadcast_to([P, NT, GD]),
                                  ALU.mult).then_inc(o_done.sem, 1)
            head_steps(dve, head_step)

            with dve.Fori(0, NT // 2) as i:
                for u in range(2):
                    dve.wait_ge(w_tps, 2 * i + u + 1)
                    dve.wait_ge(o_done.sem, o_done.at(0, HEADS, 0))
                    dve.tensor_scalar(t1[:, u, 0:CW].rearrange("p (b h d) -> p b h d", b=B, d=GD),
                                      o_all.rearrange("p (b h t d) -> p b h t d", b=B, h=GH, d=GD)[:, :, :, bass.ds(2 * i + u, 1), :].rearrange("p b h o d -> p b h (o d)"),
                                      1.0, None, ALU.mult).then_inc(w_stage, 1)
                for u in range(2):
                    dve.wait_ge(w_ps, 2 * i + u + 1)
                    xv = xT[:, :, bass.ds((2 * i + u) * P, P)]
                    dve.tensor_tensor(xv, xv, ps_s[:, u, :].rearrange("p (b t) -> p b t", b=B), ALU.add).then_inc(w_done, 1)
            dve.wait_ge(w_done, NT + 2)
            for y in (y_att, y_mid):
                dve.memset(y[:, :, 0:1], 0.0).then_inc(zero_done, 1)
            dve.wait_ge(zero_done, 3)
            norm(2, xf, y_in)
            stage(DEPTH, 0)
            steps(dve, step, DEPTH)
            with dve.Fori(0, NT // 2) as i:
                for u in range(2):
                    dve.wait_ge(o_ps, 2 * i + u + 1)
                    dve.tensor_scalar(prT[:, u, 0:B, :], xT[:, :, bass.ds((2 * i + u) * P, P)], 1.0, None, ALU.mult).then_inc(o_stage, 1)

        @block.scalar
        def _(act):
            for c in credits["scalar"]:
                act.sem_inc(c.sem, 1)
            act.sem_inc(xt_sb, 2)
            act.sem_inc(o_sb, 2)
            act.wait_ge(memsets, N_MEMSET)
            with act.Fori(0, NT // 2) as i:
                for u in range(2):
                    act.wait_ge(xt_ps, 2 * i + u + 3)
                    act.activation(xT[:, :, bass.ds((2 * i + u) * P, P)], ps_qk[:, u, :].rearrange("p (b t) -> p b t", b=B),
                                   ACT.Copy).then_inc(xt_sb, 1)

            def norm(k):
                done = 1 + k * BLOCKS
                with act.Fori(0, BLOCKS // 4) as i:
                    for u in range(4):
                        act.wait_ge(n_cen, done + 4 * i + u + 1)
                        act.activation(chunks(t1)[:, u, :], chunks(qkn)[:, u, :], ACT.Square).then_inc(n_sq, 1)
                    for u in range(4):
                        act.wait_ge(n_var, k * BLOCKS + 4 * i + u + 1)
                        act.wait_ge(n_out, done + 4 * i)
                        act.activation(chunks(t2)[:, u, :], psr[:, u, :], ACT.Ln, bias=eps[:]).then_inc(n_log, 1)
                    for u in range(4):
                        act.wait_ge(n_log, k * BLOCKS + 4 * i + u + 1)
                        act.activation(chunks(t2)[:, u, :], chunks(t2)[:, u, :], ACT.Exp, scale=-0.5).then_inc(n_rstd, 1)

            def step(cur):
                tile0, tile1, tile2 = (back(cur, d) for d in range(3))

                def keep_values(s):
                    if tile0 is None:
                        return
                    need(act, v_ps, *tile0, s + 1)
                    need(act, v_lo[s], *tile0, 1)
                    act.activation(vown[:, s, :], psm[:], ACT.Copy).then_inc(v_sb.sem, 1)

                def keep_outputs(s):
                    tile, b = item(cur, s, 3)
                    if tile is None:
                        return
                    need(act, wo_ps, *tile, 0)
                    for h in range(2):
                        bank = psr[:, bank_of((b + 2) % B, "o2", h), :]
                        need(act, o2_ps, *tile, 2 * b + h + 1)
                        for i in range(2):
                            last = act.activation(
                                oT[i * 64:(i + 1) * 64, 2 * h:2 * h + 2, b, :].rearrange("p j (w q) -> p j w q", w=2),
                                bank[i * 64:(i + 1) * 64, :].rearrange("p (j w q) -> p j w q", j=2, w=2)[:, :, :, i * 64:(i + 1) * 64],
                                ACT.Copy)
                        last.then_inc(o2_sb.sem, 1)

                def squares(s):
                    if tile0 is None:
                        return
                    need(act, qk_ps, *tile0, s + 1)
                    need(act, ss_red, *tile0, s)
                    act.activation(sqk[:], ps_qk[:].rearrange("p a c -> p (a c)"), ACT.Square).then_inc(sq_done.sem, 1)

                def keep_qk(s):
                    tile, b = item(cur, s, 1)
                    if tile is None:
                        return
                    need(act, qkt_ps, *tile, 2 * b + 1)
                    need(act, s_ps, *tile, b - 1)
                    for h in range(2):
                        last = act.activation(
                            qbd[h * 64:(h + 1) * 64, b % 2, :, :, h * 64:(h + 1) * 64].rearrange("p j w q -> p (j w) q"),
                            psr[h * 64:(h + 1) * 64, bank_of(s, "qkt", 0), :].rearrange("p (j q) -> p j q", q=64), ACT.Copy)
                    last.then_inc(qkt_sb.sem, 1)
                    need(act, qkt_ps, *tile, 2 * b + 2)
                    need(act, k_carry, *tile, b + 1)
                    act.activation(kT[:, b, :, WIN:WIN + P], psr[:, bank_of(s, "qkt", 1), :].rearrange("p (j t) -> p j t", j=PAIRS),
                                   ACT.Copy).then_inc(qkt_sb.sem, 1)

                def keep_probs(s):
                    tile, b = item(cur, s, 2)
                    if tile is None:
                        return
                    need(act, o2_ps, *tile, 2 * (b - 2) + 2)
                    for h in range(2):
                        need(act, pt_ps, *tile, 2 * b + h + 1)
                        act.activation(prT[:, b % 2, 4 * h:4 * h + 4, :].rearrange("p u q -> p (u q)"),
                                       psr[:, bank_of(s, "pt", h), :], ACT.Copy).then_inc(pt_sb.sem, 1)

                def exponentials(s):
                    tile, b = item(cur, s, 1)
                    if tile is None:
                        return
                    u = b % 2
                    need(act, max_done, *tile, b + 1)
                    need(act, pt_ps, *tile, 2 * (b - 2) + 2)
                    for j in range(UNITS):
                        last = act.activation(pr[:, u, j, :], ps_s[:, j // 4, (j % 4) * P:(j % 4 + 1) * P], ACT.Exp,
                                              bias=nmax[:, u, j:j + 1])
                    last.then_inc(exp_done.sem, 1)

                def gelu(j):
                    if tile2 is None:
                        return
                    need(act, g_ps, *tile2, j + 1)
                    act.activation(gel[0:CHN[j], j, :], psm[0:CHN[j], :], ACT.Gelu,
                                   bias=cols_s[0:CHN[j], 3 + j:4 + j]).then_inc(gelu_done.sem, 1)

                def square_centred():
                    if tile1 is None:
                        return
                    need(act, hc_done, *tile1, 1)
                    act.activation(hq[:], hc[:], ACT.Square).then_inc(hq_done.sem, 1)

                def deviation():
                    if tile1 is None:
                        return
                    need(act, var_ps, *tile1, 1)
                    act.activation(hq[:], psm[:], ACT.Ln, bias=eps[:]).then_inc(lnv_done.sem, 1)
                    need(act, lnv_done, *tile1, 1)
                    act.activation(rstd[:], hq[:], ACT.Exp, scale=-0.5).then_inc(rstd_done.sem, 1)

                for s in range(B):
                    keep_outputs(s)
                    squares(s)
                    keep_values(s)
                    if s == 3:
                        square_centred()
                    if s == 0:
                        gelu(0)
                    keep_qk(s)
                    keep_probs(s)
                    if s == 0:
                        gelu(1)
                        gelu(2)
                    if s == 3:
                        deviation()
                    exponentials(s)

            norm(0)
            steps(act, step, 0)
            norm(1)
            v3 = lambda t, u: t[:, u, :].rearrange("p (a t) -> p a t", a=2)
            with act.Fori(0, B) as b:
                for u in range(2):
                    act.wait_ge(gsum, 2 * b + u + 2)
                    act.wait_ge(gparts_out[u], 96 * b + 96)
                    act.activation(parts[u][:, :, 0, :], v3(t1, u), ACT.Copy).then_inc(gp1, 1)
                for u in range(2):
                    act.wait_ge(gr1, 2 * b + u + 1)
                    act.activation(parts[u][:, :, 1, :], v3(t2, u), ACT.Copy).then_inc(gp2, 1)
            act.wait_ge(gp3, 2 * B + 1)

            def head_step(i, u):
                for kind, head, c, bank in ring2(i, u):
                    if kind == "fin":
                        continue
                    n = S - c * P
                    need(act, p2_ps, 0, head, c + 1)
                    if live(head, 1):
                        need(act, pv_ps, 0, head - 1, 1 + c // 4)
                    act.activation(pT[c], (ps_qk, ps_s)[bank][:].rearrange("p a q -> p (a q)")[:, 0:n], ACT.Exp,
                                   scale=float(GD) ** -0.5).then_inc(p2_exp.sem, 1)
                    if c == 1 and live(i, 3):
                        keep_products(i - 3)
                if live(i, 3) and not live(i, 2):
                    keep_products(i - 3)

            def keep_products(head):
                need(act, pv_ps, 0, head, 2)
                need(act, fin_ps, 0, head, 0)
                act.activation(acc_sb[:].rearrange("p (a q) -> p a q", a=2), acc, ACT.Copy).then_inc(acc_done.sem, 1)
            head_steps(act, head_step)

            with act.Fori(0, NT // 2) as i:
                for u in range(2):
                    act.wait_ge(w_tps, 2 * i + u + 3)
                    act.activation(t2[:, u, 0:CW], ps_qk[:, u, :], ACT.Copy).then_inc(w_tsb, 1)
            act.wait_ge(w_done, NT + 2)
            norm(2)
            act.wait_ge(qbd_zero, 1)
            steps(act, step, DEPTH)
            with act.Fori(0, NT // 2) as i:
                for u in range(2):
                    act.wait_ge(o_ps, 2 * i + u + 3)
                    act.wait_ge(o_out[u], 16 * i + 16)
                    act.activation(pr[:, u, 0:B, :].rearrange("p b t -> p (b t)"), ps_qk[:, u, :], ACT.Copy).then_inc(o_sb, 1)

        @block.gpsimd
        def _(pool):
            for c in credits["gpsimd"]:
                pool.sem_inc(c.sem, 1)
            pool.sem_inc(xt_ps, 2)
            pool.sem_inc(o_ps, 2)
            for c in (gv_ps, gv_sb, w_tps, w_tsb, w_done):
                pool.sem_inc(c, 2)
            pool.sem_inc(grot, 2)
            for c in (gsum, gp1, gp2, gp3):
                pool.sem_inc(c, 1)
            for u in range(2):
                pool.sem_inc(gparts_out[u], 96)
            for u in range(2):
                pool.sem_inc(o_out[u], 16)

            def step(cur):
                for s in range(B):
                    tile, b = item(cur, s, 2)
                    if tile is not None:
                        need(pool, rsum_done, *tile, b + 1)
                        for h in range(2):
                            half = pr[:, b % 2, 4 * h:4 * h + 4, :]
                            pool.tensor_tensor(half, half, psum_e[:, b % 2, 1, 4 * h:4 * h + 4].unsqueeze(2).broadcast_to([P, 4, P]),
                                               ALU.mult).then_inc(p_norm.sem, 1)
                    tile = back(cur, 0)
                    if tile is not None:
                        u = s % 2
                        need(pool, qkn_done, *tile, s + 1)
                        need(pool, rot_done, *tile, s - 1)
                        need(pool, tab_scaled, *tile, 2)
                        for a in range(2):
                            src = qkn[:, u, :].rearrange("p (a h d) -> p a h d", a=2, d=FD)[:, :, :, (1 - a) * 32:(2 - a) * 32]
                            dst = t2[:, u, :].rearrange("p (a h d) -> p a h d", a=2, d=FD)[:, :, :, a * 32:(a + 1) * 32]
                            tab = rope_n[:, 1, :, a * 32:(a + 1) * 32].unsqueeze(2).broadcast_to([P, 2, FH, 32])
                            pool.tensor_tensor(dst, src, tab, ALU.mult).then_inc(t2_done.sem, 1)
                        need(pool, t1_done, *tile, s + 1)
                        need(pool, t2_done, *tile, 2 * s + 2)
                        pool.tensor_tensor(t1[:, u, INNER:], t1[:, u, INNER:], t2[:, u, INNER:], ALU.add).then_inc(rotk_done.sem, 1)

            steps(pool, step, 0)
            with pool.Fori(0, B) as b:
                for u in range(2):
                    pool.wait_ge(grot, 2 * (2 * b + u) + 4)
                    pool.tensor_tensor(t1[:, u, :], t1[:, u, :], t2[:, u, :], ALU.add).then_inc(gsum, 1)
            pool.wait_ge(gparts_out[0], 96 * (B + 1))
            pool.memset(qbd[:], 0.0).then_inc(qbd_zero, 1)
            steps(pool, step, DEPTH)


def rope_tables():
    half = np.arange(0, FD, 2, dtype=np.float32)
    inv = (1.0 / 10000.0 ** (half / FD)).astype(np.float32)
    t = np.arange(S, dtype=np.float32)
    freqs = (t[:, None] * inv[None, :]).astype(np.float32)
    base = ((half + 0.4 * FD) / (1.4 * FD)).astype(np.float32)
    power = ((t - S // 2) / float(WIN // 2)).astype(np.float32)
    scale = (base[None, :] ** power[:, None]).astype(np.float32)
    cos, sin = np.cos(freqs), np.sin(freqs)
    both = lambda a, b: np.stack([np.concatenate([a * scale * 8.0, b * scale * 8.0], 1),
                                  np.concatenate([a / scale, b / scale], 1)], 1)
    lay = lambda a: np.ascontiguousarray(a.astype(np.float32).reshape(NT, P, 2, FD).transpose(1, 0, 2, 3))
    return lay(both(cos, cos)), lay(both(-sin, sin))


def global_rope():
    half = GD // 2
    inv = (1.0 / 10000.0 ** (np.arange(half, dtype=np.float32) / half)).astype(np.float32)
    ang = (np.arange(S, dtype=np.float32)[:, None] * inv[None, :]).astype(np.float32)
    cos, sin = np.cos(ang).T, np.sin(ang).T
    tile = lambda a: np.ascontiguousarray(np.tile(a, (GH, 1)).astype(np.float32))
    return tile(np.concatenate([cos, cos])), tile(np.concatenate([-sin, sin]))


def band_mask():
    q = np.arange(P)[:, None, None] % WIN
    w = np.arange(2 * NT)[None, :, None]
    c = np.arange(P)[None, None, :]
    seen = (c >= q) & (c <= q + WIN) & ((w > 0) | (c >= WIN))
    return np.where(seen, 0.0, -1e30).astype(np.float32)


def kernel(L0_attn_x, L0_attn_Wq, L0_attn_Wk, L0_attn_Wv, L0_attn_Wo, L0_ffn_wqkv, L0_ffn_q_scale, L0_ffn_k_scale,
           L0_ffn_wo, L0_ffn_ln_g, L0_ffn_ln_b, L0_ffn_w1, L0_ffn_b1, L0_ffn_w2, L0_ffn_b2):
    import ml_dtypes
    import concourse.bacc as bacc
    from concourse.bass_utils import run_bass_kernel_spmd

    f = lambda a: np.ascontiguousarray(np.asarray(a))
    cols = np.zeros((DEPTH, P, 9), np.float32)
    for j in range(CH):
        cols[:, :CHN[j], j] = f(L0_ffn_b1)[:, j * P:j * P + CHN[j]]
        cols[:, :CHN[j], 3 + j] = f(L0_ffn_b1)[:, HID + j * P:HID + j * P + CHN[j]]
    cols[:, :, 6], cols[:, :, 7], cols[:, :, 8] = f(L0_ffn_ln_g), f(L0_ffn_ln_b), f(L0_ffn_b2)
    qk = np.stack([f(L0_ffn_q_scale), f(L0_ffn_k_scale)], 1)
    swapped = np.concatenate([qk[:, :, FD // 2:], qk[:, :, :FD // 2]], 2)
    qkscale = f(np.broadcast_to(np.stack([qk, swapped], 1)[:, None], (DEPTH, P, 2, 2, FD)))
    rope_cos, rope_sin = rope_tables()
    arrays = {
        "x": f(L0_attn_x), "wqkv": f(L0_ffn_wqkv), "qkscale": qkscale, "wo": f(L0_ffn_wo), "w1": f(L0_ffn_w1),
        "w2": f(L0_ffn_w2), "cols": cols, "rope_cos": rope_cos, "rope_sin": rope_sin,
        "bandmask": band_mask().astype(ml_dtypes.bfloat16), "identb_d": np.eye(P).astype(ml_dtypes.bfloat16),
        "identf_d": np.eye(P, dtype=np.float32),
    }
    Wq, Wk = f(L0_attn_Wq), f(L0_attn_Wk)
    swap = np.arange(P).reshape(GH, 2, GD // 2)[:, ::-1].reshape(-1)
    arrays["gw"] = np.stack([f(w.T) for w in (Wq, Wk, Wq[swap], Wk[swap], f(L0_attn_Wv), f(L0_attn_Wo))])
    arrays["g_cos"], arrays["g_sin"] = global_rope()
    q, k = np.arange(P)[:, None], np.arange(P)[None, :]
    arrays["causal"] = np.where(np.stack([k > q, q > k], 1), -1e30, 0.0).astype(ml_dtypes.bfloat16)
    tail = np.zeros((2, STACK - 9 * GD, S), ml_dtypes.bfloat16)
    tail[0, 0:3] = 1
    arrays["stack_tail"] = tail
    nc = bacc.Bacc("TRN2", target_bir_lowering=False, num_devices=1)
    args = {k: nc.dram_tensor(k, a.shape, mybir.dt.from_np(a.dtype), kind="ExternalInput").ap() for k, a in arrays.items()}
    args["out"] = nc.dram_tensor("out", (B, S, P), F32, kind="ExternalOutput").ap()
    program(nc, **args)
    r = run_bass_kernel_spmd(nc, [arrays], core_ids=[0])
    return r.results[0]["out"]
```
